# Optimizing a Trainium2 kernel written in Bass

```python
import numpy as np
import jax
import jax.numpy as jnp

def _softmax(x, axis=-1):
    return jax.nn.softmax(x, axis=axis)

def _gelu(x):
    return jax.nn.gelu(x, approximate=True)

def _silu(x):
    return jax.nn.silu(x)

def _sigmoid(x):
    return jax.nn.sigmoid(x)

def _layernorm(x, axis=-1, eps=1e-05):
    m = jnp.mean(x, axis=axis, keepdims=True)
    v = jnp.var(x, axis=axis, keepdims=True)
    return (x - m) / jnp.sqrt(v + eps)

def _scatter_add(tgt, idx, src, axis=0):
    return tgt.at[idx].add(src)

def _segment_sum(src, seg, n):
    return jax.ops.segment_sum(src, seg, n)
kernel_name = 'mk_vit_tower_cls_d1_tok_img768_r4_5fd9f2'

def setup_inputs(seed: int=0):
    np.random.seed(seed)
    _w = jnp.asarray

    def _rec_inputs():
        import jax
        import jax.numpy as jnp
        _rk = jax.random.key(seed)
        x = -9.30917e-05 + 1.0002 * jax.random.normal(jax.random.fold_in(_rk, 1), (64, 3, 96, 96), jnp.float32)
        cls_tok = 0.02 * jax.random.normal(jax.random.fold_in(_rk, 5), (1, 1, 192), jnp.float32)
        return (x, cls_tok)
    x, cls_tok = _rec_inputs()

    def _L0_tok_setup():
        import jax, jax.numpy as jnp
        import numpy as np
        PATCH = 16
        EPS = 1e-05

        def _shift(x, pad_spec):
            l, r, t, b = pad_spec
            H, W = (x.shape[2], x.shape[3])
            xp = jnp.pad(x, ((0, 0), (0, 0), (max(t, 0), max(b, 0)), (max(l, 0), max(r, 0))))
            h0 = -t if t < 0 else 0
            w0 = -l if l < 0 else 0
            return xp[:, :, h0:h0 + H, w0:w0 + W]
        key = jax.random.key(seed)
        k1, k2 = jax.random.split(key)
        B, C, H, Wd = (32, 3, 224, 224)
        patch_dim = PATCH * PATCH * 5 * C
        dim = 192
        x = jax.random.normal(k1, (B, C, H, Wd), dtype=jnp.float32)
        ln_gamma = jnp.ones((patch_dim,), dtype=jnp.float32)
        ln_beta = jnp.zeros((patch_dim,), dtype=jnp.float32)
        W = jax.random.normal(k2, (patch_dim, dim), dtype=jnp.float32) * patch_dim ** (-0.5)
        b = jnp.zeros((dim,), dtype=jnp.float32)
        return {'x': x, 'ln_gamma': ln_gamma, 'ln_beta': ln_beta, 'W': W, 'b': b}
    _L0_tok_all = _L0_tok_setup()
    _L0_tok_in = {k: v for k, v in _L0_tok_all.items() if k in ('ln_gamma', 'ln_beta', 'W', 'b')}
    del _L0_tok_all

    def _L0_attn_setup():
        import jax, jax.numpy as jnp
        import numpy as np
        EMBED_DIM = 192
        QKV_DIM = 192
        key = jax.random.key(seed)
        k1, k2 = jax.random.split(key)
        embeddings = jax.random.normal(k1, (8, 512, EMBED_DIM), dtype=jnp.float32)
        W = jax.random.normal(k2, (1, EMBED_DIM, 3 * QKV_DIM), dtype=jnp.float32) * 0.02
        return {'embeddings': embeddings, 'W': W}
    _L0_attn_all = _L0_attn_setup()
    _L0_attn_in = {k: v for k, v in _L0_attn_all.items() if k in ('W',)}
    del _L0_attn_all

    def _L0_ffn_setup():
        import jax, jax.numpy as jnp
        import numpy as np
        B, L, D, H, F = (4, 512, 192, 12, 768)
        ROUTE_FRAC = 0.15
        LN_EPS = 1e-05

        def _ln(x, g, b):
            m = jnp.mean(x, axis=-1, keepdims=True)
            v = jnp.mean((x - m) ** 2, axis=-1, keepdims=True)
            return (x - m) * jax.lax.rsqrt(v + LN_EPS) * g + b
        key = jax.random.key(seed)
        ks = jax.random.split(key, 20)
        s = 0.02
        return {'hidden_states': jax.random.normal(ks[0], (B, L, D), dtype=jnp.float32), 'g1': jnp.ones((D,), jnp.float32), 'b1': jnp.zeros((D,), jnp.float32), 'g2': jnp.ones((D,), jnp.float32), 'b2': jnp.zeros((D,), jnp.float32), 'Wr': jax.random.normal(ks[1], (D,), jnp.float32) * s, 'br': jnp.zeros((), jnp.float32), 'Wq': jax.random.normal(ks[2], (D, D), jnp.float32) * s, 'bq': jnp.zeros((D,), jnp.float32), 'Wk': jax.random.normal(ks[3], (D, D), jnp.float32) * s, 'bk': jnp.zeros((D,), jnp.float32), 'Wv': jax.random.normal(ks[4], (D, D), jnp.float32) * s, 'bv': jnp.zeros((D,), jnp.float32), 'Wo': jax.random.normal(ks[5], (D, D), jnp.float32) * s, 'bo': jnp.zeros((D,), jnp.float32), 'Wm': jax.random.normal(ks[6], (D, D), jnp.float32) * s, 'bm': jnp.zeros((D,), jnp.float32), 'W1': jax.random.normal(ks[7], (D, F), jnp.float32) * s, 'bf1': jnp.zeros((F,), jnp.float32), 'W2': jax.random.normal(ks[8], (F, D), jnp.float32) * s, 'bf2': jnp.zeros((D,), jnp.float32)}
    _L0_ffn_all = _L0_ffn_setup()
    _L0_ffn_in = {k: v for k, v in _L0_ffn_all.items() if k in ('g1', 'b1', 'g2', 'b2', 'Wr', 'br', 'Wq', 'bq', 'Wk', 'bk', 'Wv', 'bv', 'Wo', 'bo', 'Wm', 'bm', 'W1', 'bf1', 'W2', 'bf2')}
    del _L0_ffn_all
    return {'x': x, 'cls_tok': cls_tok, 'L0_tok_ln_gamma': _L0_tok_in['ln_gamma'], 'L0_tok_ln_beta': _L0_tok_in['ln_beta'], 'L0_tok_W': _L0_tok_in['W'], 'L0_tok_b': _L0_tok_in['b'], 'L0_attn_W': _L0_attn_in['W'], 'L0_ffn_g1': _L0_ffn_in['g1'], 'L0_ffn_b1': _L0_ffn_in['b1'], 'L0_ffn_g2': _L0_ffn_in['g2'], 'L0_ffn_b2': _L0_ffn_in['b2'], 'L0_ffn_Wr': _L0_ffn_in['Wr'], 'L0_ffn_br': _L0_ffn_in['br'], 'L0_ffn_Wq': _L0_ffn_in['Wq'], 'L0_ffn_bq': _L0_ffn_in['bq'], 'L0_ffn_Wk': _L0_ffn_in['Wk'], 'L0_ffn_bk': _L0_ffn_in['bk'], 'L0_ffn_Wv': _L0_ffn_in['Wv'], 'L0_ffn_bv': _L0_ffn_in['bv'], 'L0_ffn_Wo': _L0_ffn_in['Wo'], 'L0_ffn_bo': _L0_ffn_in['bo'], 'L0_ffn_Wm': _L0_ffn_in['Wm'], 'L0_ffn_bm': _L0_ffn_in['bm'], 'L0_ffn_W1': _L0_ffn_in['W1'], 'L0_ffn_bf1': _L0_ffn_in['bf1'], 'L0_ffn_W2': _L0_ffn_in['W2'], 'L0_ffn_bf2': _L0_ffn_in['bf2']}

def reference(x, cls_tok, L0_tok_ln_gamma, L0_tok_ln_beta, L0_tok_W, L0_tok_b, L0_attn_W, L0_ffn_g1, L0_ffn_b1, L0_ffn_g2, L0_ffn_b2, L0_ffn_Wr, L0_ffn_br, L0_ffn_Wq, L0_ffn_bq, L0_ffn_Wk, L0_ffn_bk, L0_ffn_Wv, L0_ffn_bv, L0_ffn_Wo, L0_ffn_bo, L0_ffn_Wm, L0_ffn_bm, L0_ffn_W1, L0_ffn_bf1, L0_ffn_W2, L0_ffn_bf2):
    import jax
    import jax.numpy as jnp

    def _L0_tok_ref(x, ln_gamma, ln_beta, W, b):
        import jax, jax.numpy as jnp
        import numpy as np
        PATCH = 16
        EPS = 1e-05

        def _shift(x, pad_spec):
            l, r, t, b = pad_spec
            H, W = (x.shape[2], x.shape[3])
            xp = jnp.pad(x, ((0, 0), (0, 0), (max(t, 0), max(b, 0)), (max(l, 0), max(r, 0))))
            h0 = -t if t < 0 else 0
            w0 = -l if l < 0 else 0
            return xp[:, :, h0:h0 + H, w0:w0 + W]
        shifts = [(1, -1, 0, 0), (-1, 1, 0, 0), (0, 0, 1, -1), (0, 0, -1, 1)]
        xs = jnp.concatenate([x] + [_shift(x, s) for s in shifts], axis=1)
        B, C5, H, Wd = xs.shape
        h, w = (H // PATCH, Wd // PATCH)
        t = xs.reshape(B, C5, h, PATCH, w, PATCH)
        t = t.transpose(0, 2, 4, 3, 5, 1)
        t = t.reshape(B, h * w, PATCH * PATCH * C5)
        mu = jnp.mean(t, axis=-1, keepdims=True)
        var = jnp.var(t, axis=-1, keepdims=True)
        tn = (t - mu) * jax.lax.rsqrt(var + EPS) * ln_gamma + ln_beta
        return jnp.einsum('bnp,pd->bnd', tn, W) + b

    def _L0_attn_ref(embeddings, W):
        import jax, jax.numpy as jnp
        import numpy as np
        EMBED_DIM = 192
        QKV_DIM = 192
        d = QKV_DIM
        qkv = jnp.einsum('bnd,ude->bne', embeddings, W)
        q = qkv[:, :, :d]
        k = qkv[:, :, d:2 * d]
        v = qkv[:, :, 2 * d:]
        scores = jnp.einsum('bqd,bkd->bqk', q, k) / jnp.sqrt(jnp.float32(d))
        attn = jax.nn.softmax(scores, axis=-2)
        return jnp.einsum('bqk,bkd->bqd', attn, v)

    def _L0_ffn_ref(hidden_states, g1, b1, g2, b2, Wr, br, Wq, bq, Wk, bk, Wv, bv, Wo, bo, Wm, bm, W1, bf1, W2, bf2):
        import jax, jax.numpy as jnp
        import numpy as np
        B, L, D, H, F = (4, 512, 192, 12, 768)
        ROUTE_FRAC = 0.15
        LN_EPS = 1e-05

        def _ln(x, g, b):
            m = jnp.mean(x, axis=-1, keepdims=True)
            v = jnp.mean((x - m) ** 2, axis=-1, keepdims=True)
            return (x - m) * jax.lax.rsqrt(v + LN_EPS) * g + b
        b, l, d = hidden_states.shape
        dh = d // H
        normed = _ln(hidden_states, g1, b1)
        scores = jax.nn.sigmoid(jnp.einsum('bld,d->bl', normed, Wr) + br)
        k = max(1, int(round(ROUTE_FRAC * l)))
        _, idx = jax.lax.top_k(-scores, k)
        attn_mask = jnp.zeros((b, l), bool).at[jnp.arange(b)[:, None], idx].set(True)
        q = (normed @ Wq + bq).reshape(b, l, H, dh)
        kk = (normed @ Wk + bk).reshape(b, l, H, dh)
        v = (normed @ Wv + bv).reshape(b, l, H, dh)
        logits = jnp.einsum('blhd,bmhd->bhlm', q, kk) / jnp.sqrt(jnp.float32(dh))
        probs = jax.nn.softmax(logits, axis=-1)
        ctx = jnp.einsum('bhlm,bmhd->blhd', probs, v).reshape(b, l, d)
        attn_out = ctx @ Wo + bo
        w = scores / (jnp.sum(scores, axis=1, keepdims=True) + 1e-06)
        pooled = jnp.einsum('bl,bld->bd', w, normed)
        mix_out = (normed + scores[..., None] * pooled[:, None, :]) @ Wm + bm
        merged = jnp.where(attn_mask[..., None], attn_out, mix_out)
        h = hidden_states + merged
        n2 = _ln(h, g2, b2)
        ffn = jax.nn.gelu(n2 @ W1 + bf1, approximate=False) @ W2 + bf2
        return h + ffn
    h = _L0_tok_ref(x, L0_tok_ln_gamma, L0_tok_ln_beta, L0_tok_W, L0_tok_b)
    h = jnp.concatenate([jnp.broadcast_to(cls_tok, (h.shape[0], 1, h.shape[2])), h], axis=1)
    h = h + _L0_attn_ref(_layernorm(h, axis=-1), L0_attn_W)
    h = h + _L0_ffn_ref(_layernorm(h, axis=-1), L0_ffn_g1, L0_ffn_b1, L0_ffn_g2, L0_ffn_b2, L0_ffn_Wr, L0_ffn_br, L0_ffn_Wq, L0_ffn_bq, L0_ffn_Wk, L0_ffn_bk, L0_ffn_Wv, L0_ffn_bv, L0_ffn_Wo, L0_ffn_bo, L0_ffn_Wm, L0_ffn_bm, L0_ffn_W1, L0_ffn_bf1, L0_ffn_W2, L0_ffn_bf2)
    return h

_drawn_inputs = setup_inputs


def setup_inputs(seed=0):
    import zlib

    import numpy as np

    out = dict(_drawn_inputs(seed))
    spreads = {'L0_tok_ln_gamma': (1.0, 0.2),
     'L0_tok_ln_beta': (0.0, 0.1),
     'L0_tok_b': (0.0, 0.1),
     'L0_ffn_g1': (1.0, 0.2),
     'L0_ffn_b1': (0.0, 0.428),
     'L0_ffn_g2': (1.0, 0.6),
     'L0_ffn_b2': (0.0, 2.0),
     'L0_ffn_bq': (0.0, 0.8),
     'L0_ffn_bk': (0.0, 2.0),
     'L0_ffn_bv': (0.0, 0.8),
     'L0_ffn_bo': (0.0, 0.39),
     'L0_ffn_bm': (0.0, 0.1),
     'L0_ffn_bf1': (0.0, 0.515),
     'L0_ffn_bf2': (0.0, 0.1)}
    factors = {'L0_ffn_Wq': 8.0, 'L0_ffn_Wk': 8.0, 'L0_ffn_Wv': 8.0, 'L0_ffn_Wo': 8.0}
    for name, (base, spread) in spreads.items():
        noise = np.random.default_rng([zlib.crc32(name.encode()), seed]).standard_normal(out[name].shape)
        drawn = base * np.exp(spread * noise) if base else spread * noise
        out[name] = jnp.asarray(drawn.astype(out[name].dtype))
    for name, factor in factors.items():
        out[name] = (out[name] * factor).astype(out[name].dtype)
    return out
```

```python
from contextlib import ExitStack

import concourse.bass as bass
from concourse import mybir

F32 = mybir.dt.float32
BF16 = mybir.dt.bfloat16
ALU = mybir.AluOpType
ACT = mybir.ActivationFunctionType
AX_X = mybir.AxisListType.X

B, C, HW = 64, 3, 96
PS = 16
NP = HW // PS
POS = NP * NP + 1
D = 192
DH2 = D // 2
SH = 5
FEAT = PS * PS * SH * C
HEADS, DH = 12, 16
HH = HEADS // 2
F = 768
FC = F // 128
TOPK = max(1, int(round(0.15 * POS)))
EPS = 1e-5

IB = 16
ITERS = B // IB
UNITS = 2
GI = 3
GROUPS = 3
SLOTS = GI * GROUPS
GT = GI * POS
UT = SLOTS * POS
UR = [min(UT, IB * POS - u * UT) for u in range(UNITS)]
SEL = GI * TOPK
USEL = SEL * GROUPS
HS = HH * SEL
XP = NP * IB

ROWS = PS + 2
MAIN = C * PS * PS
EDGE = 2 * C * PS
WIN = MAIN + 2 * EDGE
KW = MAIN // 128
CH = KW + 2
WCOL = D + 2
CHUNK = [128] * KW + [EDGE, EDGE + 1]

PER = 24
GS = PER // (UNITS * GROUPS)
US = PER // UNITS
TJOBS = 16
TS_ = PER // (TJOBS // 2)

ZC = 2 * D + 2
NEG = -1e30


def vit_tower(nc, A, out):
    x_d, cls_d = A["x"], A["cls_tok"]

    with ExitStack() as ctx:
        def sb(name, shape, dt=F32):
            return ctx.enter_context(nc.sbuf_tensor(name, shape, dt))

        def sem(name):
            return ctx.enter_context(nc.semaphore(name))

        ps = ctx.enter_context(nc.psum_tensor("ps", [128, 8, 512], F32))

        ident = sb("ident", [128, 128])
        ones = sb("ones", [128, 128])
        same = sb("same", [GT, GI, POS])
        before = sb("before", [GT, GI, POS])
        same_sel = sb("same_sel", [GT, GI, TOPK])
        slot_no = sb("slot_no", [GT, GI, TOPK])
        head_mask = sb("head_mask", [DH2, HH, SEL])
        img_of_tok = sb("img_of_tok", [GI, GI, POS], BF16)
        img_of_sel = sb("img_of_sel", [GI, HH, GI, TOPK], BF16)
        other_img = sb("other_img", [GI, GI, POS], BF16)
        cls_rows = sb("cls_rows", [1, 2, GT])
        minus_half = sb("minus_half", [128, 4])
        counts = sb("counts", [XP, WIN])
        px_ok = sb("px_ok", [128, 4])
        px_sel = sb("px_sel", [128, 2, 8])

        late = sb("late", [128, 5868])
        w_raw = late[:, 0:SH * 2 * C * D].rearrange("p (s a c d) -> p s a c d", s=SH, a=2, c=C)
        o_p = FC * sum(UR)
        gelu_t = [late[:, FC * sum(UR[:u]):FC * sum(UR[:u + 1])].rearrange("p (m t) -> p m t", m=FC) for u in range(UNITS)]
        proj = [late[0:GT, o_p + u * GROUPS * ZC:o_p + (u + 1) * GROUPS * ZC].rearrange("p (g n) -> p g n", g=GROUPS)
                for u in range(UNITS)]
        gb_raw = sb("gb_raw", [128, SH, 2, 2, SH * C])
        w_edge = sb("w_edge", [EDGE, 2, D])
        gb_edge = sb("gb_edge", [EDGE, 2, 2])
        w_eff = sb("w_eff", [128, CH, WCOL])
        rows1 = sb("rows1", [1, 2, D])
        colsum = sb("colsum", [GT, D])
        tok_bias = sb("tok_bias", [GT, D])
        w_attn = sb("w_attn", [DH2, 2, 3 * D])
        w_qT = sb("w_qT", [DH2, 2, D])
        w_kT = sb("w_kT", [DH2, 2, D])
        w_qk = sb("w_qk", [DH2, 2, D])
        gcol = sb("gcol", [DH2, 4, 2])
        wz = sb("wz", [DH2 + 1, 2, ZC + 2 * D])
        wz_b = sb("wz_b", [1, ZC + 2 * D])
        wo = sb("wo", [DH2 + 1, 2, D])
        w1 = sb("w1", [DH2 + 1, 2, F])
        w1_b = sb("w1_b", [1, F])
        w2 = sb("w2", [128, FC, D])
        bm_all = sb("bm_all", [GT, D])
        bf2_all = sb("bf2_all", [GT, D])

        strips = sb("strips", [XP, C, ROWS, HW])
        wins = sb("wins", [XP, NP, WIN + 1])
        wcnt = sb("wcnt", [XP, 2, WIN])
        winT = sb("winT", [128, CH, UNITS, UT])

        def per_unit(name, shape):
            return [sb(f"{name}{u}", shape) for u in range(UNITS)]

        mom = per_unit("mom", [GT, 6, GROUPS])
        bn = per_unit("bn", [GT, GROUPS, 6])
        mv = per_unit("mv", [GT, GROUPS, 2])
        sc = per_unit("sc", [GT, 16, GROUPS])
        h = per_unit("h", [GT, GROUPS, D])
        e = per_unit("e", [GT, GROUPS, D])
        hid = per_unit("hid", [GT, GROUPS, D])
        tmp = per_unit("tmp", [GT, GROUPS, D])
        vs = tmp
        eT = per_unit("eT", [DH2 + 1, 2, UT])
        uT = per_unit("uT", [DH2, 2, UT])
        at = per_unit("at", [GT, GROUPS, GT])
        sy = per_unit("sy", [GT, GROUPS, D + 1])
        pick = per_unit("pick", [GT, GROUPS, USEL])
        pickT = per_unit("pickT", [USEL, UT])
        zselT = per_unit("zselT", [DH2 + 1, 2, USEL])
        qblk = per_unit("qblk", [DH2, 2, GROUPS, HS])
        pr = per_unit("pr", [HS, 2 * GROUPS, GT])
        lsc = per_unit("lsc", [HS, 4, 2 * GROUPS])
        prT = per_unit("prT", [GT, 2, GROUPS * HS])
        ctm = [pr[u][0:DH2].rearrange("p x k -> p (x k)")[:, 0:2 * GROUPS * HS] for u in range(UNITS)]
        ctxT = per_unit("ctxT", [DH2 + 1, 2, USEL])
        ao = per_unit("ao", [USEL, D])
        fin = h

        s = {n: sem(n) for n in (
            "d_tok d_gb d_edge d_small d_big x_in out_done "
            "c_pool c_dve c_act c_pe strips_zero raw_zero consts_done w_eff_ready weights_ready "
            "main_copied edge_copied cnt_ready cnt_used sq_ready tr_a tr_d ev_a ev_d tok_mm m_mu m_sq m_var m_veps "
            "rp_ready m_nmr t1_done h_done bn1 bn1_agg v1_ready r1_ready e_done eT_mm eT_a eT_d u_mm u_ev v_mm v_ev s_mm s_max "
            "s_nb at_exp at_sum o_mm h2_done bn2 bn2_agg v2_ready v2b_ready r2_ready z_done hid_done zT_mm zT_a zT_d p_mm p_ev "
            "k_mm k_ev sg_exp sg_add score rank_mm rk1 rk2 rk3 pick_done not_sel sy_done pool_mm al1 al2 al3 mix1 mix2 mix3 "
            "pT_mm pT_ev zs_mm zs_ev q_mm qb_done l_mm l_max l_nb l_exp l_rcp pr_done prT_mm prT_a prT_d c_mm ctm_done "
            "ctx_done ao_mm ao_ev x_mm hh_done bn3 bn3_agg v3_ready r3_ready z2_done z2T_mm z2T_a z2T_d base1 base2 up_mm gelu_done dn_mm fin_done"
        ).split()}

        CREDIT = ("tr_a", "tr_d", "cnt_used", "tok_mm", "fin_done")
        STORED = 16 * UNITS * GROUPS

        class Now:

            def __init__(self, eng, i):
                self.eng, self.b = eng, i * PER

            def wait(self, name, n):
                self.eng.wait_ge(s[name], self.b + (n + PER if name in CREDIT else n))

            def group(self, name, u, g):
                self.wait(name, US * u + GS * (g + 1))

            def unit(self, name, u):
                self.wait(name, US * (u + 1))

            def last(self, name):
                self.wait(name, 0)

        def bank(u, k):
            return ps[:, 4 * u + k, :]

        def win_src(j, half):
            n = (2 * j + half) % 8
            return ps[0:CHUNK[j], n, 0:3 * XP].rearrange("p (w h b) -> p b h w", w=3, h=NP)

        def win_dst(j, half):
            v = winT[0:CHUNK[j], j].rearrange("p u t -> p (u t)")[:, 0:IB * POS].rearrange("p (b q) -> p b q", q=POS)[:, :, 1:]
            return v.rearrange("p b (h w) -> p b h w", w=NP)[:, :, :, 3 * half:3 * half + 3]

        def v_bank(u, g):
            return bank(u, 3)[0:GT, g * D:(g + 1) * D] if g < 2 else bank(u, 0)[0:GT, 0:D]

        def o_bank(u, g):
            return bank(u, 2)[0:GT, g * D:(g + 1) * D] if g < 2 else bank(u, 1)[0:GT, 0:D]

        def pool_bank(u, g, n=D + 1, o=0):
            return bank(u, 1)[0:GT, g * 256 + o:g * 256 + n] if g < 2 else bank(u, 3)[0:GT, o:n]

        def x_bank(u, g):
            return bank(u, 3)[0:GT, g * 256:g * 256 + D] if g < 2 else bank(u, 2)[0:GT, 256:256 + D]

        tok_rows = A["L0_tok_W"].rearrange("(q f) d -> q f d", f=SH * C)
        gb_rows = [A[n].rearrange("(q f) -> q f", f=SH * C) for n in ("L0_tok_ln_gamma", "L0_tok_ln_beta")]
        OFF = [0, 1, -1, PS, -PS]
        edges = [
            (0, 0, 3, 0, 1), (0, 1, 4, PS * (PS - 1), 1), (1, 0, 1, 0, PS), (1, 1, 2, PS - 1, PS)]
        N_TOK, N_EDGE = 2 * SH, len(edges) * C
        attn_w = A["L0_attn_W"].rearrange("u (c p) n -> p (u c) n", c=2)
        out_rows = out.rearrange("b n d -> (b n) d")

        def chunked(name):
            return A[name].rearrange("(c p) n -> p c n", c=2)

        def row(name):
            return A[name].rearrange("(a n) -> a n", a=1)

        ctx.enter_context(nc.allow_non_contiguous_dma(reason="columns of per-feature factors, a few hundred words"))
        block = ctx.enter_context(nc.Block())

        @block.sync
        def _(sp):
            sp.wait_ge(s["raw_zero"], 1)
            for k in range(SH):
                for a in range(2):
                    lo, hi = max(0, 128 * a + OFF[k]), min(PS * PS, 128 * (a + 1) + OFF[k])
                    p0 = lo - 128 * a - OFF[k]
                    sp.dma_start(w_raw[p0:p0 + hi - lo, k, a], tok_rows[lo:hi, C * k:C * (k + 1), :]).then_inc(s["d_tok"], 16)
            sp.wait_ge(s["strips_zero"], 1)

            def load_images(i):
                for y in range(NP):
                    r0, r1 = max(0, PS * y - 1), min(HW, PS * y + PS + 1)
                    o = r0 - (PS * y - 1)
                    sp.dma_start(strips[IB * y:IB * (y + 1), :, o:o + r1 - r0, :],
                                 x_d[bass.ds(i * IB, IB), :, r0:r1, :]).then_inc(s["x_in"], 16)

            load_images(0)
            sp.dma_start(w2[:], A["L0_ffn_W2"].rearrange("(c p) n -> p c n", p=128)).then_inc(s["d_big"], 16)

            def store_tokens(i, now):
                for u in range(UNITS):
                    for g in range(GROUPS):
                        n = min(GT, UR[u] - GT * g)
                        now.group("fin_done", u, g)
                        sp.dma_start(out_rows[bass.ds(i * (IB * POS) + (u * UT + g * GT), n), :],
                                     fin[u][0:n, g, :]).then_inc(s["out_done"], 16)

            with sp.Fori(0, ITERS - 1) as i:
                now = Now(sp, i)
                now.wait("main_copied", PER)
                now.wait("edge_copied", PER)
                load_images(i + 1)
                store_tokens(i, now)
            store_tokens(ITERS - 1, Now(sp, ITERS - 1))
            sp.wait_ge(s["out_done"], (ITERS + 1) * STORED)

        @block.gpsimd
        def _(pool):
            g = nc.gpsimd
            done = [0]

            def step(ins):
                done[0] += 1
                ins.then_inc(s["c_pool"], 1)
                pool.wait_ge(s["c_pool"], done[0])

            for name in CREDIT:
                pool.sem_inc(s[name], PER)
            pool.sem_inc(s["out_done"], STORED)
            step(g.memset(strips[:, :, 0, :], 0.0))
            g.memset(strips[:, :, ROWS - 1, :], 0.0).then_inc(s["strips_zero"], 1)
            step(g.memset(w_raw[:, 1:SH, :], 0.0))
            g.memset(gb_raw[:], 0.0).then_inc(s["raw_zero"], 1)
            step(g.memset(ones[:], 1.0))
            step(g.memset(minus_half[:], -0.5))

            def select(view, src, pattern, base, cm, op, fill=0.0):
                step(g.affine_select(out=view, in_=src, compare_op=op, fill=fill, base=base,
                                     pattern=pattern, channel_multiplier=cm))

            def band(view, step_, width, n, inner, src=None):
                if src is None:
                    step(g.memset(view, 1.0))
                select(view, view, [[-step_, n], *[[0, k] for k in inner]], 0, 1, ALU.is_ge)
                select(view, view, [[step_, n], *[[0, k] for k in inner]], width - 1, -1, ALU.is_ge)

            step(g.memset(px_sel[:], 1.0))
            select(px_sel[:, 0, :], px_sel[:, 0, :], [[-PS, 8]], -(PS - 1), 1, ALU.not_equal)
            select(px_sel[:, 1, :], px_sel[:, 1, :], [[-PS, 8]], 0, 1, ALU.not_equal)
            step(g.memset(px_ok[:, 2:4], 1.0))
            select(px_ok[:, 2:3], px_ok[:, 2:3], [[0, 1]], 128 - PS - 1, -1, ALU.is_ge)
            select(px_ok[:, 3:4], px_ok[:, 3:4], [[0, 1]], -PS, 1, ALU.is_ge)
            step(g.memset(ident[:], 0.0))
            select(ident[:], ident[:], [[-1, 128]], 0, 1, ALU.not_equal, 1.0)
            step(g.memset(counts[:], float(SH)))
            cm = counts[:, 0:MAIN].rearrange("p (c y x) -> p c y x", c=C, y=PS)
            step(g.memset(counts[:, MAIN:], 1.0))
            for q in (0, PS - 1):
                step(g.memset(cm[:, :, q, :], float(SH - 1)))
                step(g.memset(cm[:, :, :, q], float(SH - 1)))
            for q in (0, PS - 1):
                for r in (0, PS - 1):
                    step(g.memset(cm[:, :, q, r], float(SH - 2)))
            step(g.memset(wins[:, 0, MAIN + EDGE:MAIN + EDGE + EDGE // 2], 0.0))
            step(g.memset(wins[:, NP - 1, MAIN + EDGE + EDGE // 2:WIN], 0.0))
            step(g.memset(winT[:], 0.0))
            band(same[:], POS, POS, GI, [POS])
            step(g.tensor_copy(before[:], same[:]))
            select(before[:], before[:], [[-POS, GI], [-1, POS]], 0, 1, ALU.is_gt)
            band(same_sel[:], POS, POS, GI, [TOPK])
            for j in range(TOPK):
                step(g.memset(slot_no[:, :, j:j + 1], float(j)))
            band(head_mask[:], DH, DH, HH, [SEL])
            step(g.memset(img_of_tok[:], 0.0))
            select(img_of_tok[:], img_of_tok[:], [[-1, GI], [0, POS]], 0, 1, ALU.not_equal, 1.0)
            step(g.memset(other_img[:], NEG))
            select(other_img[:], other_img[:], [[-1, GI], [0, POS]], 0, 1, ALU.not_equal, 0.0)
            step(g.memset(img_of_sel[:], 0.0))
            select(img_of_sel[:], img_of_sel[:], [[0, HH], [-1, GI], [0, TOPK]], 0, 1, ALU.not_equal, 1.0)
            cr = cls_rows[:].rearrange("a k (i q) -> a k i q", i=GI)
            step(g.memset(cls_rows[:, 0, :], 0.0))
            step(g.memset(cr[:, 0, :, 0:1], 1.0))
            step(g.memset(cls_rows[:, 1, :], 1.0))
            step(g.memset(cr[:, 1, :, 0:1], 0.0))
            for u in range(UNITS):
                step(g.memset(pick[u][:], 0.0))
                step(g.memset(eT[u][DH2:, 0, :], 1.0))
                step(g.memset(zselT[u][DH2:, 0, :], 1.0))
                step(g.memset(ctxT[u][DH2:, 0, :], 1.0))
            g.memset(w_eff[96:, CH - 1, :], 0.0).then_inc(s["consts_done"], 1)

            with pool.Fori(0, ITERS) as i:
                now = Now(pool, i)
                w5 = wins[:, :, MAIN:WIN].rearrange("p w (k a c x) -> p w k a c x", k=2, a=2, c=C)
                st5 = strips[:].rearrange("p c y (w x) -> p c y w x", x=PS)
                pool.wait_ge(s["x_in"], (i + 1) * (16 * NP))
                now.last("tr_a")
                now.last("tr_d")
                for a in range(2):
                    src = st5[:, :, a * (ROWS - 1), :, :].rearrange("p c w x -> p w c x")
                    g.tensor_copy(w5[:, :, 0, a, :, :], src).then_inc(s["edge_copied"], PER // 4)
                for a in range(2):
                    x0 = PS - 1 if a == 0 else PS
                    src = strips[:, :, 1:PS + 1, x0:x0 + PS * (NP - 2) + 1:PS].rearrange("p c y w -> p w c y")
                    g.tensor_copy(w5[:, 1 - a:NP - a, 1, a, :, :], src).then_inc(s["edge_copied"], PER // 4)
                for w in range(NP):
                    now.wait("edge_copied", PER)
                    now.wait("main_copied", GS * (w + 1))
                    if w >= 2:
                        now.wait("cnt_used", GS * (w - 1))
                    else:
                        now.last("cnt_used")
                    g.tensor_tensor(wcnt[:, w % 2, :], wins[:, w, 0:WIN], counts[:], ALU.mult).then_inc(s["cnt_ready"], GS)

                def rsqrt(u, src, dst, name, ready):
                    now.unit(name, u)
                    g.tensor_tensor(dst, src, minus_half[0:GT, 0:GROUPS], ALU.pow).then_inc(s[ready], US)

                for u in range(UNITS):
                    rsqrt(u, mom[u][:, 3, :], mom[u][:, 4, :], "m_veps", "rp_ready")
                for u in range(UNITS):
                    rsqrt(u, sc[u][:, 0, :], sc[u][:, 1, :], "v1_ready", "r1_ready")
                for u in range(UNITS):
                    now.unit("v2_ready", u)
                    now.unit("v2b_ready", u)
                    g.tensor_tensor(sc[u][:, 4:6, :], sc[u][:, 2:4, :],
                                    minus_half[0:GT, 0:1].broadcast_to((GT, 2 * GROUPS)).rearrange("p (a g) -> p a g", a=2),
                                    ALU.pow).then_inc(s["r2_ready"], US)
                for u in range(UNITS):
                    now.unit("mix1", u)
                    g.tensor_tensor(tmp[u][:], tmp[u][:], proj[u][:, :, D:2 * D], ALU.add).then_inc(s["mix2"], US)
                for u in range(UNITS):
                    now.unit("l_rcp", u)
                    g.tensor_tensor(pr[u][:], pr[u][:], lsc[u][:, 3, :].rearrange("p (x a) -> p x a", a=1)
                                    .broadcast_to((HS, 2 * GROUPS, GT)), ALU.mult).then_inc(s["pr_done"], US)
                for u in range(UNITS):
                    rsqrt(u, sc[u][:, 6, :], sc[u][:, 7, :], "v3_ready", "r3_ready")
                    g.tensor_tensor(h[u][:], h[u][:], hid[u][:], ALU.add).then_inc(s["base1"], US)
                    now.unit("base1", u)
                    g.tensor_tensor(h[u][:], h[u][:], bf2_all[:].rearrange("p (a d) -> p a d", a=1)
                                    .broadcast_to((GT, GROUPS, D)), ALU.add).then_inc(s["base2"], US)

        N_SMALL = 20

        @block.scalar
        def _(act):
            a_ = nc.scalar
            act.wait_ge(s["raw_zero"], 1)
            for k in range(SH):
                for a in range(2):
                    lo, hi = max(0, 128 * a + OFF[k]), min(PS * PS, 128 * (a + 1) + OFF[k])
                    p0 = lo - 128 * a - OFF[k]
                    for j in range(2):
                        act.dma_start(gb_raw[p0:p0 + hi - lo, k, j, a, :], gb_rows[j][lo:hi, :]).then_inc(s["d_gb"], 16)
            for q, side, k, first, stp in edges:
                for c in range(C):
                    p0 = side * (EDGE // 2) + c * PS
                    src = tok_rows[first:first + stp * (PS - 1) + 1:stp, C * k + c, :]
                    act.dma_start(w_edge[p0:p0 + PS, q, :], src).then_inc(s["d_edge"], 16)
                    for j in range(2):
                        act.dma_start(gb_edge[p0:p0 + PS, q, j:j + 1],
                                      gb_rows[j][first:first + stp * (PS - 1) + 1:stp, C * k + c:C * k + c + 1]
                                      ).then_inc(s["d_edge"], 16)
            small = [
                (rows1[:, 0, :], cls_d.rearrange("a b d -> (a b) d")), (rows1[:, 1, :], row("L0_tok_b")),
                (w_attn[:], attn_w),
                (wz[0:DH2, :, 0:D], chunked("L0_ffn_Wv")), (wz[0:DH2, :, D:2 * D], chunked("L0_ffn_Wm")),
                (wz[0:DH2, :, 2 * D + 1:ZC], A["L0_ffn_Wr"].rearrange("(c p n) -> p c n", c=2, n=1)),
                (wz[0:DH2, :, ZC:ZC + D], chunked("L0_ffn_Wk")), (wz[0:DH2, :, ZC + D:], chunked("L0_ffn_Wq")),
                (wo[0:DH2], chunked("L0_ffn_Wo")), (wo[DH2:, 0, :], row("L0_ffn_bo")),
                (w1[0:DH2], chunked("L0_ffn_W1")), (w1_b[:], row("L0_ffn_bf1")),
                (bm_all[:], row("L0_ffn_bm").broadcast_to((GT, D))), (bf2_all[:], row("L0_ffn_bf2").broadcast_to((GT, D))),
            ] + [(gcol[:, k, :], A[n].rearrange("(c p) -> p c", c=2)) for k, n in
                 enumerate(("L0_ffn_g1", "L0_ffn_b1", "L0_ffn_g2", "L0_ffn_b2"))]
            act.wait_ge(s["c_dve"], 1)
            small += [(wz_b[:, 0:D], row("L0_ffn_bv")), (wz_b[:, 2 * D + 1:ZC], A["L0_ffn_br"].rearrange("(a n) -> a n", a=1)
                       if len(A["L0_ffn_br"].shape) else A["L0_ffn_br"]),
                      (wz_b[:, ZC:ZC + D], row("L0_ffn_bk")), (wz_b[:, ZC + D:], row("L0_ffn_bq"))]
            assert len(small) == N_SMALL + 2
            for dst, src in small:
                act.dma_start(dst, src).then_inc(s["d_small"], 16)

            with act.Fori(0, ITERS) as i:
                now = Now(act, i)

                def copy(dst, src, name, n, scale=1.0):
                    a_.activation(dst, src, ACT.Copy, scale=scale).then_inc(s[name], n)

                for j in range(CH):
                    now.wait("tr_a", TS_ * (j + 1))
                    if j == 0:
                        now.last("tok_mm")
                    a_.activation(win_dst(j, 0), win_src(j, 0), ACT.Copy).then_inc(s["ev_a"], TS_)
                for u in range(UNITS):
                    now.wait("eT_mm", US * u + US // 2)
                    copy(eT[u][0:DH2, 0, :], bank(u, 3)[0:DH2, 0:UT], "eT_a", US)
                for u in range(UNITS):
                    for m in range(2):
                        now.wait("u_mm", US * u + US // 2 * (m + 1))
                        copy(uT[u][:, m, :], bank(u, 1 + m)[0:DH2, 0:UT], "u_ev", US // 2)
                for u in range(UNITS):
                    now.unit("s_nb", u)
                    for g in range(GROUPS):
                        a_.activation(at[u][:, g, :], bank(u, 1)[0:GT, g * GT:(g + 1) * GT], ACT.Exp, bias=sc[u][:, 9, g:g + 1],
                                      scale=D ** -0.5, accum_out=sc[u][:, 10, g:g + 1]).then_inc(s["at_exp"], GS)
                    now.unit("at_sum", u)
                    for g in range(GROUPS):
                        now.group("v_mm", u, max(g, 1))
                        copy(vs[u][:, g, :], v_bank(u, g), "v_ev", GS, sc[u][:, 11, g:g + 1])
                for u in range(UNITS):
                    now.wait("zT_mm", US * u + US // 2)
                    copy(eT[u][0:DH2, 0, :], bank(u, 3)[0:DH2, 0:UT], "zT_a", US)
                for u in range(UNITS):
                    for g in range(GROUPS):
                        now.group("p_mm", u, g)
                        copy(proj[u][:, g, :], bank(u, 1 + g)[0:GT, 0:ZC], "p_ev", GS)
                    now.unit("p_ev", u)
                    a_.activation(sc[u][:, 12, :], proj[u][:, :, ZC - 1], ACT.Exp, scale=-1.0).then_inc(s["sg_exp"], US)
                    for m in range(2):
                        now.wait("k_mm", US * u + US // 2 * (m + 1))
                        copy(uT[u][:, m, :], bank(u, m)[0:DH2, 0:UT], "k_ev", US // 2)
                    now.unit("score", u)
                    for g in range(GROUPS):
                        copy(sy[u][:, g, :], proj[u][:, g, D:2 * D + 1], "sy_done", GS, sc[u][:, 13, g:g + 1])
                for u in range(UNITS):
                    now.unit("zs_mm", u)
                    copy(zselT[u][0:DH2], bank(u, 0)[0:DH2, 0:128].rearrange("p (c n) -> p c n", c=2)[:, :, 0:USEL], "zs_ev", US)
                for u in range(UNITS):
                    now.unit("l_nb", u)
                    for k in range(2 * GROUPS):
                        c, g = k // GROUPS, k % GROUPS
                        a_.activation(pr[u][:, k, :], bank(u, 2 + c)[0:HS, g * GT:(g + 1) * GT], ACT.Exp,
                                      bias=lsc[u][:, 1, k:k + 1], scale=DH ** -0.5,
                                      accum_out=lsc[u][:, 2, k:k + 1]).then_inc(s["l_exp"], US // 6)
                for u in range(UNITS):
                    now.wait("prT_mm", US * u + US // 2)
                    copy(prT[u][:, 0, :], bank(u, 2)[0:GT, 0:GROUPS * HS], "prT_a", US)
                for u in range(UNITS):
                    now.unit("ao_mm", u)
                    copy(ao[u][:], bank(u, 2)[0:USEL, 0:D], "ao_ev", US)
                for u in range(UNITS):
                    now.wait("z2T_mm", US * u + US // 2)
                    copy(eT[u][0:DH2, 0, :], bank(u, 0)[0:DH2, 0:UT], "z2T_a", US)
                for u in range(UNITS):
                    for m in range(FC):
                        now.wait("up_mm", US * u + US // 6 * (m + 1))
                        a_.activation(gelu_t[u][:, m, :], bank(u, (2 + m) % 4)[:, 0:UR[u]], ACT.Gelu).then_inc(s["gelu_done"], US // 6)

        @block.vector
        def _(dve):
            v = nc.vector
            done = [0]

            def step(ins):
                done[0] += 1
                ins.then_inc(s["c_dve"], 1)
                dve.wait_ge(s["c_dve"], done[0])

            step(v.memset(wz_b[:], 0.0))
            step(v.memset(wz_b[:, 2 * D:2 * D + 1], 1.0))
            step(v.memset(wz[0:DH2, :, 2 * D:2 * D + 1], 0.0))
            dve.wait_ge(s["consts_done"], 1)
            step(v.tensor_reduce(px_ok[:, 0:1], px_sel[:, 0, :], AX_X, ALU.min))
            step(v.tensor_reduce(px_ok[:, 1:2], px_sel[:, 1, :], AX_X, ALU.min))
            dve.wait_ge(s["d_gb"], 16 * 4 * SH)
            for k in (1, 2):
                view = gb_raw[:, k].rearrange("p j a f -> p (j a f)")
                step(v.tensor_scalar(view, view, px_ok[:, k - 1:k], None, ALU.mult))
            for a in range(2):
                cnt = w_eff[:, a, D:D + 1]
                step(v.tensor_scalar(cnt, px_ok[:, 0:1], px_ok[:, 1:2], 2.0, ALU.add, ALU.add))
                step(v.tensor_scalar(cnt, cnt, px_ok[:, 3 - a:4 - a], None, ALU.add))
                for c in range(1, C):
                    step(v.tensor_copy(w_eff[:, 2 * c + a, D:D + 1], cnt))
            step(v.memset(w_eff[:, 0:KW, D + 1:], 0.0))
            step(v.memset(w_eff[0:EDGE, KW:, D:D + 1], 1.0))
            step(v.memset(w_eff[0:EDGE, KW:, D + 1:], 0.0))
            step(v.memset(w_eff[EDGE:EDGE + 1, CH - 1, D + 1:], 1.0))
            dve.wait_ge(s["d_tok"], 16 * N_TOK)
            dve.wait_ge(s["d_edge"], 16 * 3 * N_EDGE)
            for k in range(SH):
                for c in range(C):
                    for a in range(2):
                        dst, gam = w_eff[:, 2 * c + a, 0:D], gb_raw[:, k, 0, a, C * k + c:C * k + c + 1]
                        if k == 0:
                            ins = v.tensor_scalar(dst, w_raw[:, k, a, c], gam, None, ALU.mult)
                        else:
                            ins = v.scalar_tensor_tensor(out=dst, in0=w_raw[:, k, a, c], scalar=gam, in1=dst,
                                                         op0=ALU.mult, op1=ALU.add)
                        done[0] += 1
                        ins.then_inc(s["c_dve"], 1)
                dve.wait_ge(s["c_dve"], done[0])
            for q in range(2):
                step(v.tensor_scalar(w_eff[0:EDGE, KW + q, 0:D], w_edge[:, q, :], gb_edge[:, q, 0:1], None, ALU.mult))
            v.memset(lsc[0][:, 0, :], 0.0).then_inc(s["w_eff_ready"], 1)
            for k, dst in ((0, w_qT), (1, w_kT)):
                dve.wait_ge(s["c_pe"], 1 + k)
                step(v.tensor_copy(dst[:], ps[0:DH2, 6 + k, 0:2 * D].rearrange("p (c n) -> p c n", c=2)))
            dve.wait_ge(s["c_pe"], 3)
            step(v.tensor_copy(w_qk[:], ps[0:DH2, 5, 0:2 * D].rearrange("p (c n) -> p c n", c=2)))
            dve.wait_ge(s["c_pe"], 4)
            step(v.tensor_tensor(wz[DH2:, 0, 0:ZC], ps[0:1, 0, 0:ZC], wz_b[:, 0:ZC], ALU.add))
            step(v.tensor_tensor(wz[DH2:, 0, ZC:], ps[0:1, 1, 0:2 * D], wz_b[:, ZC:], ALU.add))
            for j in range(2):
                step(v.tensor_tensor(w1[DH2:, 0, j * 384:(j + 1) * 384], ps[0:1, 2 + j, 0:384], w1_b[:, j * 384:(j + 1) * 384], ALU.add))
            for c in range(2):
                step(v.tensor_scalar(wz[0:DH2, c, :], wz[0:DH2, c, :], gcol[:, 0, c:c + 1], None, ALU.mult))
                step(v.tensor_scalar(w1[0:DH2, c, :], w1[0:DH2, c, :], gcol[:, 2, c:c + 1], None, ALU.mult))
            dve.wait_ge(s["c_pe"], 5)
            step(v.tensor_copy(colsum[:], ps[0:GT, 4, 0:D]))
            step(v.tensor_tensor(rows1[:, 1, :], ps[0:1, 4, 256:256 + D], rows1[:, 1, :], ALU.add))
            dve.wait_ge(s["c_pe"], 6)
            v.tensor_copy(tok_bias[:], ps[0:GT, 5, 0:D]).then_inc(s["weights_ready"], 1)
            dve.wait_ge(s["weights_ready"], 1)

            with dve.Fori(0, ITERS) as i:
                now = Now(dve, i)

                def row_stats(u, g, name):
                    v.bn_stats(bn[u][:, g, :], src_of(name)[u][:, g, :]).then_inc(s[name], GS)

                def src_of(name):
                    return {"bn1": h, "bn2": h, "bn3": hid}[name]

                dve.wait_ge(s["x_in"], (i + 1) * (16 * NP))
                now.last("tr_a")
                now.last("tr_d")
                for w in range(NP):
                    v.tensor_copy(wins[:, w, 0:MAIN].rearrange("p (c y x) -> p c y x", c=C, y=PS),
                                  strips[:, :, 1:PS + 1, PS * w:PS * (w + 1)]).then_inc(s["main_copied"], GS)
                for w in range(NP):
                    now.wait("cnt_ready", GS * (w + 1))
                    now.wait("main_copied", PER)
                    if w >= 2:
                        now.wait("cnt_used", GS * (w - 1))
                    v.tensor_tensor_reduce(wcnt[:, w % 2, :], wcnt[:, w % 2, :], wins[:, w, 0:WIN], 1.0, 0.0, ALU.mult, ALU.add,
                                           wins[:, w, WIN:WIN + 1]).then_inc(s["cnt_used"], GS)
                for j in range(CH):
                    now.wait("tr_d", TS_ * (j + 1))
                    if j == 0:
                        now.last("tok_mm")
                    v.tensor_copy(win_dst(j, 1), win_src(j, 1)).then_inc(s["ev_d"], TS_)

                for u in range(UNITS):
                    m = mom[u]
                    sums = ps[0:GT, 4 * u:4 * u + GROUPS, D]
                    squares = ps[0:GT, 4 * u:4 * u + GROUPS, D + 1]
                    now.unit("tok_mm", u)
                    v.tensor_scalar(m[:, 0, :], sums, 1.0 / FEAT, None, ALU.mult).then_inc(s["m_mu"], US)
                    now.unit("m_mu", u)
                    v.tensor_tensor(m[:, 1, :], m[:, 0, :], m[:, 0, :], ALU.mult).then_inc(s["m_sq"], US)
                    now.unit("m_sq", u)
                    v.scalar_tensor_tensor(out=m[:, 2, :], in0=squares, scalar=1.0 / FEAT, in1=m[:, 1, :],
                                           op0=ALU.mult, op1=ALU.subtract).then_inc(s["m_var"], US)
                    now.unit("m_var", u)
                    v.tensor_scalar(m[:, 3, :], m[:, 2, :], 0.0, EPS, ALU.max, ALU.add).then_inc(s["m_veps"], US)
                    now.unit("rp_ready", u)
                    v.scalar_tensor_tensor(out=m[:, 5, :], in0=m[:, 0, :], scalar=-1.0, in1=m[:, 4, :],
                                           op0=ALU.mult, op1=ALU.mult).then_inc(s["m_nmr"], US)
                    now.unit("m_nmr", u)
                    for g in range(GROUPS):
                        v.scalar_tensor_tensor(out=tmp[u][:, g, :], in0=colsum[:], scalar=m[:, 5, g:g + 1], in1=tok_bias[:],
                                               op0=ALU.mult, op1=ALU.add).then_inc(s["t1_done"], GS)
                    dve.wait_ge(s["out_done"], (i + 1) * STORED)
                    for g in range(GROUPS):
                        now.group("t1_done", u, g)
                        v.scalar_tensor_tensor(out=h[u][:, g, :], in0=bank(u, g)[0:GT, 0:D], scalar=m[:, 4, g:g + 1],
                                               in1=tmp[u][:, g, :], op0=ALU.mult, op1=ALU.add).then_inc(s["h_done"], GS)

                def statistics(u, src, written, sem_bn, sem_agg, outs):
                    for g in range(GROUPS):
                        now.group(written, u, g)
                        v.bn_stats(bn[u][:, g, :], src[u][:, g, :]).then_inc(s[sem_bn], GS)
                    now.unit(sem_bn, u)
                    v.tensor_tensor(sc[u][:, 14:16, :].rearrange("p a g -> p g a"), bn[u][:, :, 1:3], bn[u][:, :, 4:6],
                                    ALU.add).then_inc(s[sem_agg], US // 2)
                    v.tensor_tensor(mv[u][:, :, 0], bn[u][:, :, 1], bn[u][:, :, 4], ALU.subtract).then_inc(s[sem_agg], US // 2)

                def stats(u, src, written, name, agg, outs):
                    b6, q = bn[u], sc[u]
                    for g in range(GROUPS):
                        now.group(written, u, g)
                        v.bn_stats(b6[:, g, :], src[u][:, g, :]).then_inc(s[name], GS)
                    for g in range(GROUPS):
                        if g == 0:
                            now.unit(name, u)
                            v.tensor_copy(mom[u][:, 1, :], b6[:, :, 0]).then_inc(s[agg], US // 4)
                        v.bn_aggr(mv[u][:, g, :], b6[:, g, :]).then_inc(s[agg], US // 4)
                    for ready, dst, fac, add in outs:
                        now.unit(agg, u)
                        v.tensor_scalar(q[:, dst, :], mv[u][:, :, 1], fac, add, ALU.mult, ALU.add).then_inc(s[ready], US)

                for u in range(UNITS):
                    stats(u, h, "h_done", "bn1", "bn1_agg", [("v1_ready", 0, 1.0, EPS)])
                for u in range(UNITS):
                    now.unit("r1_ready", u)
                    for g in range(GROUPS):
                        v.tensor_scalar(e[u][:, g, :], h[u][:, g, :], mv[u][:, g, 0:1], sc[u][:, 1, g:g + 1],
                                        ALU.subtract, ALU.mult).then_inc(s["e_done"], GS)
                for u in range(UNITS):
                    now.unit("eT_mm", u)
                    v.tensor_copy(eT[u][0:DH2, 1, :], bank(u, 0)[0:DH2, 0:UT]).then_inc(s["eT_d"], US)
                for u in range(UNITS):
                    now.unit("s_mm", u)
                    v.tensor_reduce(sc[u][:, 8, :], bank(u, 1)[0:GT, 0:UT].rearrange("p (g q) -> p g q", g=GROUPS), AX_X,
                                    ALU.max).then_inc(s["s_max"], US)
                    now.unit("s_max", u)
                    v.tensor_scalar(sc[u][:, 9, :], sc[u][:, 8, :], -(D ** -0.5), None, ALU.mult).then_inc(s["s_nb"], US)
                for u in range(UNITS):
                    now.unit("at_exp", u)
                    v.reciprocal(sc[u][:, 11, :], sc[u][:, 10, :]).then_inc(s["at_sum"], US)
                for u in range(UNITS):
                    for g in range(GROUPS):
                        now.group("o_mm", u, max(g, 1))
                        v.tensor_tensor(h[u][:, g, :], h[u][:, g, :], o_bank(u, g), ALU.add).then_inc(s["h2_done"], GS)
                    stats(u, h, "h2_done", "bn2", "bn2_agg",
                          [("v2_ready", 2, 1.0, EPS), ("v2b_ready", 3, 1.0 + EPS, EPS * EPS)])
                for u in range(UNITS):
                    now.unit("r2_ready", u)
                    for g in range(GROUPS):
                        v.tensor_scalar(e[u][:, g, :], h[u][:, g, :], mv[u][:, g, 0:1], sc[u][:, 5, g:g + 1],
                                        ALU.subtract, ALU.mult).then_inc(s["z_done"], GS)
                    for g in range(GROUPS):
                        v.tensor_scalar(hid[u][:, g, :], h[u][:, g, :], mv[u][:, g, 0:1], sc[u][:, 4, g:g + 1],
                                        ALU.subtract, ALU.mult).then_inc(s["hid_done"], GS)
                for u in range(UNITS):
                    now.unit("zT_mm", u)
                    v.tensor_copy(eT[u][0:DH2, 1, :], bank(u, 0)[0:DH2, 0:UT]).then_inc(s["zT_d"], US)
                for u in range(UNITS):
                    q = sc[u]
                    now.unit("sg_exp", u)
                    v.tensor_scalar(q[:, 14, :], q[:, 12, :], 1.0, None, ALU.add).then_inc(s["sg_add"], US)
                    now.unit("sg_add", u)
                    v.reciprocal(q[:, 13, :], q[:, 14, :]).then_inc(s["score"], US)
                for u in range(UNITS):
                    for g in range(GROUPS):
                        others = bank(u, 2)[0:GT, g * GT:(g + 1) * GT]
                        now.unit("rank_mm", u)
                        v.scalar_tensor_tensor(out=at[u][:, g, :], in0=others, scalar=sc[u][:, 13, g:g + 1],
                                               in1=same[:].rearrange("p i q -> p (i q)"), op0=ALU.is_lt, op1=ALU.mult,
                                               accum_out=mom[u][:, 0, g:g + 1]).then_inc(s["rk1"], GS)
                        now.group("rk1", u, g)
                        v.scalar_tensor_tensor(out=at[u][:, g, :], in0=others, scalar=sc[u][:, 13, g:g + 1],
                                               in1=before[:].rearrange("p i q -> p (i q)"), op0=ALU.is_equal, op1=ALU.mult,
                                               accum_out=mom[u][:, 1, g:g + 1]).then_inc(s["rk2"], GS)
                    now.unit("rk2", u)
                    v.tensor_tensor(mom[u][:, 2, :], mom[u][:, 0, :], mom[u][:, 1, :], ALU.add).then_inc(s["rk3"], US)
                    now.unit("rk3", u)
                    for g in range(GROUPS):
                        v.scalar_tensor_tensor(out=pick[u][:, g, g * SEL:(g + 1) * SEL], in0=slot_no[:].rearrange("p i j -> p (i j)"),
                                               scalar=mom[u][:, 2, g:g + 1], in1=same_sel[:].rearrange("p i j -> p (i j)"),
                                               op0=ALU.is_equal, op1=ALU.mult).then_inc(s["pick_done"], GS)
                    v.tensor_scalar(mom[u][:, 5, :], mom[u][:, 2, :], float(TOPK), None, ALU.is_ge).then_inc(s["not_sel"], US)
                for u in range(UNITS):
                    now.unit("pT_mm", u)
                    v.tensor_copy(pickT[u][:], bank(u, 2)[0:USEL, 0:UT]).then_inc(s["pT_ev"], US)
                for u in range(UNITS):
                    q = sc[u]
                    now.unit("pool_mm", u)
                    v.tensor_scalar(q[:, 14, 0:2], bank(u, 1)[0:GT, D:D + 257:256], 1e-6, None, ALU.add).then_inc(s["al1"], US // 2)
                    v.tensor_scalar(q[:, 14, 2:3], pool_bank(u, 2, D + 1, D), 1e-6, None, ALU.add).then_inc(s["al1"], US // 2)
                    now.unit("al1", u)
                    v.reciprocal(q[:, 15, :], q[:, 14, :]).then_inc(s["al2"], US)
                    now.unit("al2", u)
                    v.tensor_tensor(q[:, 8, :], q[:, 15, :], q[:, 13, :], ALU.mult).then_inc(s["al3"], US)
                    now.unit("al3", u)
                    for g in range(GROUPS):
                        v.scalar_tensor_tensor(out=tmp[u][:, g, :], in0=pool_bank(u, g, D), scalar=q[:, 8, g:g + 1], in1=bm_all[:],
                                               op0=ALU.mult, op1=ALU.add).then_inc(s["mix1"], GS)
                    now.unit("q_mm", u)
                    for c in range(2):
                        src = bank(u, 0)[0:DH2, 128 + 64 * c:128 + 64 * c + USEL].rearrange("p (g a j) -> p g a j", g=GROUPS, a=1)
                        v.tensor_tensor(qblk[u][:, c].rearrange("p g (h j) -> p g h j", h=HH),
                                        src.broadcast_to((DH2, GROUPS, HH, SEL)),
                                        head_mask[:].rearrange("p (a h) j -> p a h j", a=1).broadcast_to((DH2, GROUPS, HH, SEL)),
                                        ALU.mult).then_inc(s["qb_done"], US // 2)
                for u in range(UNITS):
                    now.unit("mix2", u)
                    now.unit("not_sel", u)
                    for g in range(GROUPS):
                        v.scalar_tensor_tensor(out=hid[u][:, g, :], in0=tmp[u][:, g, :], scalar=mom[u][:, 5, g:g + 1],
                                               in1=hid[u][:, g, :], op0=ALU.mult, op1=ALU.add).then_inc(s["mix3"], GS)
                    q = lsc[u]
                    now.unit("l_mm", u)
                    v.tensor_reduce(q[:, 0, :].rearrange("p (c g) -> p c g", c=2),
                                    ps[0:HS, 4 * u + 2:4 * u + 4, 0:UT].rearrange("p c (g k) -> p c g k", g=GROUPS),
                                    AX_X, ALU.max).then_inc(s["l_max"], US)
                    now.unit("l_max", u)
                    v.tensor_scalar(q[:, 1, :], q[:, 0, :], -(DH ** -0.5), None, ALU.mult).then_inc(s["l_nb"], US)
                for u in range(UNITS):
                    now.unit("l_exp", u)
                    v.reciprocal(lsc[u][:, 3, :], lsc[u][:, 2, :]).then_inc(s["l_rcp"], US)
                for u in range(UNITS):
                    now.unit("prT_mm", u)
                    v.tensor_copy(prT[u][:, 1, :], bank(u, 3)[0:GT, 0:GROUPS * HS]).then_inc(s["prT_d"], US)
                for u in range(UNITS):
                    now.unit("c_mm", u)
                    v.tensor_tensor(ctm[u].rearrange("p (c g n) -> p c g n", c=2, g=GROUPS),
                                    ps[0:DH2, 4 * u:4 * u + 2, 0:GROUPS * HS].rearrange("p c (g n) -> p c g n", g=GROUPS),
                                    head_mask[:].rearrange("p (a b h) j -> p a b (h j)", a=1, b=1)
                                    .broadcast_to((DH2, 2, GROUPS, HS)), ALU.mult).then_inc(s["ctm_done"], US)
                    now.unit("ctm_done", u)
                    v.tensor_reduce(ctxT[u][0:DH2].rearrange("p c (g j) -> p (c g) j", g=GROUPS),
                                    ctm[u].rearrange("p (x h j) -> p x j h", h=HH, j=SEL), AX_X, ALU.add).then_inc(s["ctx_done"], US)
                for u in range(UNITS):
                    for g in range(GROUPS):
                        now.group("x_mm", u, max(g, 1))
                        now.group("mix3", u, g)
                        v.tensor_tensor(hid[u][:, g, :], hid[u][:, g, :], x_bank(u, g), ALU.add).then_inc(s["hh_done"], GS)
                    stats(u, hid, "hh_done", "bn3", "bn3_agg", [("v3_ready", 6, 1.0, EPS)])
                for u in range(UNITS):
                    now.unit("r3_ready", u)
                    for g in range(GROUPS):
                        v.tensor_scalar(e[u][:, g, :], hid[u][:, g, :], mv[u][:, g, 0:1], sc[u][:, 7, g:g + 1],
                                        ALU.subtract, ALU.mult).then_inc(s["z2_done"], GS)
                for u in range(UNITS):
                    now.unit("z2T_mm", u)
                    v.tensor_copy(eT[u][0:DH2, 1, :], bank(u, 1)[0:DH2, 0:UT]).then_inc(s["z2T_d"], US)
                for u in range(UNITS):
                    for g in range(GROUPS):
                        n = min(GT, UR[u] - GT * g)
                        now.group("dn_mm", u, g)
                        if g == 0:
                            now.unit("base2", u)
                        v.tensor_tensor(fin[u][0:n, g, :], bank(u, g)[0:n, 0:D], h[u][0:n, g, :], ALU.add).then_inc(s["fin_done"], GS)

        @block.tensor
        def _(pe):
            t = nc.tensor
            pe.wait_ge(s["consts_done"], 1)
            pe.wait_ge(s["d_small"], 16 * (N_SMALL + 2))
            for k in range(2):
                for c in range(2):
                    for m in range(2):
                        last = t.transpose(ps[0:DH2, 6 + k, m * D + c * DH2:m * D + (c + 1) * DH2],
                                           w_attn[:, c, k * D + m * DH2:k * D + (m + 1) * DH2], ident[0:DH2, 0:DH2])
                last.then_inc(s["c_pe"], 1)
            pe.wait_ge(s["c_dve"], SETUP_QK)
            for m in range(2):
                for c in range(2):
                    last = t.matmul(ps[0:DH2, 5, m * D:(m + 1) * D], w_qT[:, c, m * DH2:(m + 1) * DH2], w_kT[:, c, :],
                                    start=(c == 0), stop=(c == 1))
            last.then_inc(s["c_pe"], 1)
            for j, (src, k, lo, hi) in enumerate(((wz, 1, 0, ZC), (wz, 1, ZC, ZC + 2 * D), (w1, 3, 0, 384), (w1, 3, 384, 768))):
                for c in range(2):
                    last = t.matmul(ps[0:1, j, 0:hi - lo], gcol[:, k, c:c + 1], src[0:DH2, c, lo:hi], start=(c == 0), stop=(c == 1))
            last.then_inc(s["c_pe"], 1)
            pe.wait_ge(s["w_eff_ready"], 1)
            for j in range(CH):
                n = min(CHUNK[j], 128) if j < KW else EDGE
                t.matmul(ps[0:GT, 4, 0:D], ones[0:n, 0:GT], w_eff[0:n, j, 0:D], start=(j == 0), stop=(j == CH - 1))
            pieces = [(gb_raw[:, k, 1, a, C * k + c:C * k + c + 1], w_raw[:, k, a, c]) for k in range(SH) for c in range(C)
                      for a in range(2)] + [(gb_edge[:, q, 1:2], w_edge[:, q, :]) for q in range(2)]
            for j, (bet, w) in enumerate(pieces):
                last = t.matmul(ps[0:1, 4, 256:256 + D], bet, w, start=(j == 0), stop=(j == len(pieces) - 1))
            last.then_inc(s["c_pe"], 1)
            pe.wait_ge(s["c_dve"], SETUP_ROWS)
            for j in range(2):
                last = t.matmul(ps[0:GT, 5, 0:D], cls_rows[:, j, :], rows1[:, j, :], start=(j == 0), stop=(j == 1))
            last.then_inc(s["c_pe"], 1)
            pe.wait_ge(s["weights_ready"], 1)
            pe.wait_ge(s["d_big"], 16)

            with pe.Fori(0, ITERS) as i:
                now = Now(pe, i)

                def to_columns(u, src, done, name, banks):
                    for c in range(2):
                        for g in range(GROUPS):
                            now.group(done, u, g)
                            last = t.transpose(bank(u, banks[c])[0:DH2, g * GT:(g + 1) * GT],
                                               src[u][:, g, c * DH2:(c + 1) * DH2], ident[0:GT, 0:GT])
                        last.then_inc(s[name], US // 2)

                now.last("fin_done")
                for j in range(CH):
                    for half in range(2):
                        n = 2 * j + half
                        if j == 0 and half == 0:
                            now.wait("main_copied", PER)
                            now.wait("edge_copied", PER)
                        if j == CH - 1 and half == 0:
                            now.wait("cnt_used", PER)
                        if n >= 8:
                            now.wait("ev_d" if half else "ev_a", TS_ * (j - 3))
                        for w in range(3):
                            last = t.transpose(ps[0:CHUNK[j], n % 8, w * XP:(w + 1) * XP],
                                               wins[:, 3 * half + w, sum(CHUNK[:j]):sum(CHUNK[:j + 1])], ident[0:XP, 0:XP])
                        last.then_inc(s["tr_d" if half else "tr_a"], TS_)
                for u in range(UNITS):
                    for g in range(GROUPS):
                        if g == 0:
                            now.wait("ev_a", PER)
                            now.wait("ev_d", PER)
                        for j in range(CH):
                            last = t.matmul(bank(u, g)[0:GT, 0:WCOL], winT[0:CHUNK[j], j, u, g * GT:(g + 1) * GT],
                                            w_eff[0:CHUNK[j], j, :], start=(j == 0), stop=(j == CH - 1))
                        last.then_inc(s["tok_mm"], GS)
                for u in range(UNITS):
                    to_columns(u, e, "e_done", "eT_mm", (3, 0))
                for u in range(UNITS):
                    now.unit("eT_a", u)
                    now.unit("eT_d", u)
                    for m in range(2):
                        for c in range(2):
                            last = t.matmul(bank(u, 1 + m)[0:DH2, 0:UT], w_qk[:, c, m * DH2:(m + 1) * DH2], eT[u][0:DH2, c, :],
                                            start=(c == 0), stop=(c == 1))
                        last.then_inc(s["u_mm"], US // 2)
                    for g in range(GROUPS):
                        for c in range(2):
                            last = t.matmul(v_bank(u, g), eT[u][0:DH2, c, g * GT:(g + 1) * GT], w_attn[:, c, 2 * D:3 * D],
                                            start=(c == 0), stop=(c == 1))
                        last.then_inc(s["v_mm"], GS)
                for u in range(UNITS):
                    now.unit("u_ev", u)
                    for g in range(GROUPS):
                        o = bank(u, 1)[0:GT, g * GT:(g + 1) * GT]
                        cols = slice(g * GT, (g + 1) * GT)
                        t.matmul(o, img_of_tok[:].rearrange("p i q -> p (i q)"), other_img[:].rearrange("p i q -> p (i q)"),
                                 start=True, stop=False)
                        for c in range(2):
                            last = t.matmul(o, eT[u][0:DH2, c, cols], uT[u][:, c, cols], start=False, stop=(c == 1))
                    last.then_inc(s["s_mm"], US)
                for u in range(UNITS):
                    for g in range(GROUPS):
                        now.group("v_ev", u, g)
                        t.matmul(o_bank(u, g), at[u][:, g, :], vs[u][:, g, :], start=True, stop=True).then_inc(s["o_mm"], GS)
                for u in range(UNITS):
                    to_columns(u, e, "z_done", "zT_mm", (3, 0))
                for u in range(UNITS):
                    now.unit("zT_a", u)
                    now.unit("zT_d", u)
                    for g in range(GROUPS):
                        t.matmul(bank(u, 1 + g)[0:GT, 0:ZC], eT[u][0:DH2 + 1, 0, g * GT:(g + 1) * GT], wz[:, 0, 0:ZC],
                                 start=True, stop=False)
                        t.matmul(bank(u, 1 + g)[0:GT, 0:ZC], eT[u][0:DH2, 1, g * GT:(g + 1) * GT], wz[0:DH2, 1, 0:ZC],
                                 start=False, stop=True).then_inc(s["p_mm"], GS)
                    for m in range(2):
                        o = bank(u, m)[0:DH2, 0:UT]
                        if m == 1:
                            now.group("p_ev", u, 0)
                        cols = slice(ZC + m * DH2, ZC + (m + 1) * DH2)
                        t.matmul(o, wz[:, 0, cols], eT[u][:, 0, :], start=True, stop=False)
                        t.matmul(o, wz[0:DH2, 1, cols], eT[u][0:DH2, 1, :], start=False, stop=True).then_inc(s["k_mm"], US // 2)
                for u in range(UNITS):
                    now.unit("score", u)
                    now.unit("p_ev", u)
                    for g in range(GROUPS):
                        last = t.transpose(bank(u, 2)[0:GT, g * GT:(g + 1) * GT], sc[u][:, 13, g:g + 1].broadcast_to((GT, GT)),
                                           ident[0:GT, 0:GT])
                    last.then_inc(s["rank_mm"], US)
                for u in range(UNITS):
                    now.unit("k_ev", u)
                    for g in range(GROUPS):
                        now.group("sy_done", u, g)
                        last = t.matmul(pool_bank(u, g), same[:].rearrange("p i q -> p (i q)"), sy[u][:, g, :], start=True, stop=True)
                    last.then_inc(s["pool_mm"], US)
                for u in range(UNITS):
                    for c in range(2):
                        for g in range(GROUPS):
                            if c == 0:
                                now.group("pick_done", u, g)
                            last = t.matmul(bank(u, 0)[0:DH2, 64 * c + g * SEL:64 * c + (g + 1) * SEL],
                                            e[u][:, g, c * DH2:(c + 1) * DH2], pick[u][:, g, g * SEL:(g + 1) * SEL],
                                            start=True, stop=True)
                    last.then_inc(s["zs_mm"], US)
                    for g in range(GROUPS):
                        last = t.transpose(bank(u, 2)[0:USEL, g * GT:(g + 1) * GT], pick[u][:, g, :], ident[0:GT, 0:GT])
                    last.then_inc(s["pT_mm"], US)
                for u in range(UNITS):
                    now.unit("zs_ev", u)
                    for m in range(2):
                        o = bank(u, 0)[0:DH2, 128 + 64 * m:128 + 64 * m + USEL]
                        cols = slice(ZC + D + m * DH2, ZC + D + (m + 1) * DH2)
                        t.matmul(o, wz[:, 0, cols], zselT[u][:, 0, :], start=True, stop=False)
                        last = t.matmul(o, wz[0:DH2, 1, cols], zselT[u][0:DH2, 1, :], start=False, stop=True)
                    last.then_inc(s["q_mm"], US)
                for u in range(UNITS):
                    now.unit("qb_done", u)
                    now.unit("pT_ev", u)
                    for c in range(2):
                        for g in range(GROUPS):
                            o = bank(u, 2 + c)[0:HS, g * GT:(g + 1) * GT]
                            t.matmul(o, img_of_sel[:].rearrange("p h i j -> p (h i j)"), other_img[:].rearrange("p i q -> p (i q)"),
                                     start=True, stop=False)
                            last = t.matmul(o, qblk[u][:, c, g, :], uT[u][:, c, g * GT:(g + 1) * GT], start=False, stop=True)
                    last.then_inc(s["l_mm"], US)
                for u in range(UNITS):
                    now.unit("pr_done", u)
                    for c in range(2):
                        for g in range(GROUPS):
                            last = t.transpose(bank(u, 2 + c)[0:GT, g * HS:(g + 1) * HS], pr[u][:, c * GROUPS + g, :],
                                               ident[0:HS, 0:HS])
                        last.then_inc(s["prT_mm"], US // 2)
                for u in range(UNITS):
                    now.unit("prT_a", u)
                    now.unit("prT_d", u)
                    now.unit("mix1", u)
                    for c in range(2):
                        for g in range(GROUPS):
                            last = t.matmul(bank(u, c)[0:DH2, g * HS:(g + 1) * HS], proj[u][:, g, c * DH2:(c + 1) * DH2],
                                            prT[u][:, c, g * HS:(g + 1) * HS], start=True, stop=True)
                    last.then_inc(s["c_mm"], US)
                for u in range(UNITS):
                    now.unit("ctx_done", u)
                    t.matmul(bank(u, 2)[0:USEL, 0:D], ctxT[u][:, 0, :], wo[:, 0, :], start=True, stop=False)
                    t.matmul(bank(u, 2)[0:USEL, 0:D], ctxT[u][0:DH2, 1, :], wo[0:DH2, 1, :], start=False, stop=True)\
                        .then_inc(s["ao_mm"], US)
                for u in range(UNITS):
                    now.unit("ao_ev", u)
                    for g in range(GROUPS):
                        t.matmul(x_bank(u, g), pickT[u][:, g * GT:(g + 1) * GT], ao[u][:], start=True, stop=True)\
                            .then_inc(s["x_mm"], GS)
                for u in range(UNITS):
                    to_columns(u, e, "z2_done", "z2T_mm", (0, 1))
                for u in range(UNITS):
                    now.unit("z2T_a", u)
                    now.unit("z2T_d", u)
                    for m in range(FC):
                        o = bank(u, (2 + m) % 4)[:, 0:UR[u]]
                        if m >= 4:
                            now.wait("gelu_done", US * u + US // 6 * (m - 3))
                        t.matmul(o, w1[:, 0, m * 128:(m + 1) * 128], eT[u][:, 0, 0:UR[u]], start=True, stop=False)
                        t.matmul(o, w1[0:DH2, 1, m * 128:(m + 1) * 128], eT[u][0:DH2, 1, 0:UR[u]], start=False, stop=True)\
                            .then_inc(s["up_mm"], US // 6)
                for u in range(UNITS):
                    now.unit("gelu_done", u)
                    for g in range(GROUPS):
                        n = min(GT, UR[u] - GT * g)
                        for m in range(FC):
                            last = t.matmul(bank(u, g)[0:n, 0:D], gelu_t[u][:, m, g * GT:g * GT + n], w2[:, m, :],
                                            start=(m == 0), stop=(m == FC - 1))
                        last.then_inc(s["dn_mm"], GS)


SETUP_COUNTS = 3 + 2 + 2 + 2 * (2 + (C - 1)) + 4
SETUP_QK = SETUP_COUNTS + SH * C * 2 + 2 + 2
SETUP_ROWS = SETUP_QK + 1 + 4 + 4 + 2

_INS = ['x', 'cls_tok', 'L0_tok_ln_gamma', 'L0_tok_ln_beta', 'L0_tok_W', 'L0_tok_b', 'L0_attn_W', 'L0_ffn_g1', 'L0_ffn_b1',
        'L0_ffn_g2', 'L0_ffn_b2', 'L0_ffn_Wr', 'L0_ffn_br', 'L0_ffn_Wq', 'L0_ffn_bq', 'L0_ffn_Wk', 'L0_ffn_bk', 'L0_ffn_Wv',
        'L0_ffn_bv', 'L0_ffn_Wo', 'L0_ffn_bo', 'L0_ffn_Wm', 'L0_ffn_bm', 'L0_ffn_W1', 'L0_ffn_bf1', 'L0_ffn_W2', 'L0_ffn_bf2']


def kernel(**inputs):
    import numpy as _np
    import concourse.bacc as _bacc
    from concourse import mybir as _mybir
    from concourse.bass_utils import run_bass_kernel_spmd as _run

    nc = _bacc.Bacc("TRN2", target_bir_lowering=False, num_devices=1)
    arrays, args = {}, {}
    for name in _INS:
        a = _np.ascontiguousarray(inputs[name])
        if a.ndim == 0:
            a = a.reshape(1)
        arrays[f"in_{name}_dram"] = a
        args[name] = nc.dram_tensor(f"in_{name}_dram", a.shape, _mybir.dt.from_np(a.dtype), kind="ExternalInput").ap()
    out = nc.dram_tensor("out_0_dram", (B, POS, D), _mybir.dt.float32, kind="ExternalOutput").ap()
    vit_tower(nc, args, out)
    r = _run(nc, [arrays], core_ids=[0])
    return r.results[0]["out_0_dram"]
```

```python
from contextlib import ExitStack

import concourse.bass as bass
from concourse import mybir

F32 = mybir.dt.float32
BF16 = mybir.dt.bfloat16
ALU = mybir.AluOpType
ACT = mybir.ActivationFunctionType
AX_X = mybir.AxisListType.X

B, C, HW = 64, 3, 96
PS = 16
NP = HW // PS
POS = NP * NP + 1
D = 192
DH2 = D // 2
SH = 5
FEAT = PS * PS * SH * C
HEADS, DH = 12, 16
HH = HEADS // 2
F = 768
FC = F // 128
TOPK = max(1, int(round(0.15 * POS)))
EPS = 1e-5

IB = 16
ITERS = B // IB
UNITS = 2
GI = 3
GROUPS = 3
SLOTS = GI * GROUPS
GT = GI * POS
UT = SLOTS * POS
UR = [min(UT, IB * POS - u * UT) for u in range(UNITS)]
SEL = GI * TOPK
USEL = SEL * GROUPS
HS = HH * SEL
XP = NP * IB

ROWS = PS + 2
MAIN = C * PS * PS
EDGE = 2 * C * PS
WIN = MAIN + 2 * EDGE
KW = MAIN // 128
CH = KW + 2
WCOL = D + 2
CHUNK = [128] * KW + [EDGE, EDGE + 1]

PER = 24
GS = PER // (UNITS * GROUPS)
US = PER // UNITS
TJOBS = 16
TS_ = PER // (TJOBS // 2)
UP = US // FC



def plan(before, after):
    order = []

    def stages(names, fill=()):
        fill = [list(f) for f in fill]
        for name in names.split():
            for u in range(UNITS):
                order.append((name, u))
                if fill:
                    order.extend(p for p in fill.pop(0) if (before if p[0] in ("up", "down") else after))

    def pieces(name, *ks):
        return [(name, k) for k in ks]

    up = [pieces("up", 2 * n, 2 * n + 1) for n in range(FC)]
    down = [pieces("down", n) for n in range(UNITS * GROUPS)]
    turn = [pieces("turn", n) for n in range(TJOBS)]
    patch = [pieces("patch", n) for n in range(UNITS * GROUPS)]
    stages("sums token", [pieces("halo", 0) + up[0], up[1], up[2], up[3]])
    stages("norm1")
    stages("flip1", [up[4], up[5]])
    stages("uv score", [[], [], down[0], down[1]])
    stages("weigh attend", [[], [], pieces("copy", 0, 1, 2) + down[2], pieces("copy", 3, 4, 5) + down[3]])
    stages("norm2 flip2", [[], [], down[4] + pieces("squares", 0), down[5] + pieces("squares", 1)])
    stages("project router", [turn[0] + turn[1], turn[2] + turn[3], pieces("squares", 2), pieces("squares", 3)])
    stages("rank pool", [turn[4] + turn[5], turn[6] + turn[7] + pieces("squares", 4), turn[8], turn[9] + pieces("squares", 5)])
    stages("pick query", [turn[10] + turn[11], turn[12] + turn[13], turn[14], turn[15]])
    stages("logits", [patch[0], patch[1]])
    stages("shares flip3", [[], [], patch[2], []])
    stages("context out", [patch[3], [], patch[4], []])
    stages("scatter", [patch[5], []])
    stages("norm3 flip4")
    return order


BEFORE_FIRST = ([("halo", 0)] + [("copy", n) for n in range(NP)] + [("squares", n) for n in range(NP)]
                + [("turn", n) for n in range(TJOBS)] + [("patch", n) for n in range(UNITS * GROUPS)])
AFTER_LAST = [("up", n) for n in range(UNITS * FC)] + [("down", n) for n in range(UNITS * GROUPS)]

ZC = 2 * D + 2
NEG = -1e30


def vit_tower(nc, A, out):
    x_d, cls_d = A["x"], A["cls_tok"]

    with ExitStack() as ctx:
        def sb(name, shape, dt=F32):
            return ctx.enter_context(nc.sbuf_tensor(name, shape, dt))

        def sem(name):
            return ctx.enter_context(nc.semaphore(name))

        ps = ctx.enter_context(nc.psum_tensor("ps", [128, 8, 512], F32))

        ident = sb("ident", [128, 128])
        ones = sb("ones", [128, 128])
        same = sb("same", [GT, GI, POS])
        before = sb("before", [GT, GI, POS])
        same_sel = sb("same_sel", [GT, GI, TOPK])
        slot_no = sb("slot_no", [GT, GI, TOPK])
        head_mask = sb("head_mask", [DH2, HH, SEL])
        img_of_tok = sb("img_of_tok", [GI, GI, POS], BF16)
        img_of_sel = sb("img_of_sel", [GI, HH, GI, TOPK], BF16)
        other_img = sb("other_img", [GI, GI, POS], BF16)
        cls_rows = sb("cls_rows", [1, 2, GT])
        minus_half = sb("minus_half", [128, 4])
        counts = sb("counts", [XP, WIN], BF16)
        px_ok = sb("px_ok", [128, 4])
        px_sel = sb("px_sel", [128, 2, 8])

        late = sb("late", [128, 5868])
        w_raw = late[:, 0:SH * 2 * C * D].rearrange("p (s a c d) -> p s a c d", s=SH, a=2, c=C)
        o_p = FC * sum(UR)
        gelu_t = [late[:, FC * sum(UR[:u]):FC * sum(UR[:u + 1])].rearrange("p (m t) -> p m t", m=FC) for u in range(UNITS)]
        proj = [late[0:GT, o_p + u * GROUPS * ZC:o_p + (u + 1) * GROUPS * ZC].rearrange("p (g n) -> p g n", g=GROUPS)
                for u in range(UNITS)]
        gb_raw = sb("gb_raw", [128, SH, 2, 2, SH * C])
        w_edge = sb("w_edge", [EDGE, 2, D])
        gb_edge = sb("gb_edge", [EDGE, 2, 2])
        w_eff = sb("w_eff", [128, CH, WCOL])
        rows1 = sb("rows1", [1, 2, D])
        colsum = sb("colsum", [GT, D])
        tok_bias = sb("tok_bias", [GT, D])
        w_attn = sb("w_attn", [DH2, 2, 3 * D])
        w_qT = sb("w_qT", [DH2, 2, D])
        w_kT = sb("w_kT", [DH2, 2, D])
        w_qk = sb("w_qk", [DH2, 2, D])
        gcol = sb("gcol", [DH2, 4, 2])
        wz = sb("wz", [DH2 + 1, 2, ZC + 2 * D])
        wz_b = sb("wz_b", [1, ZC + 2 * D])
        wo = sb("wo", [DH2 + 1, 2, D])
        w1 = sb("w1", [DH2 + 1, 2, F])
        w1_b = sb("w1_b", [1, F])
        w2 = sb("w2", [128, FC, D])
        bm_all = sb("bm_all", [GT, D])
        bf2_all = sb("bf2_all", [GT, D])

        strips = sb("strips", [XP, C, ROWS, HW])
        wins = sb("wins", [XP, NP, WIN + 1])
        wcnt = sb("wcnt", [XP, WIN])
        winT = sb("winT", [128, CH, UNITS, UT])

        def per_unit(name, shape):
            return [sb(f"{name}{u}", shape) for u in range(UNITS)]

        mom = per_unit("mom", [GT, 6, GROUPS])
        bn = per_unit("bn", [GT, GROUPS, 6])
        mv = per_unit("mv", [GT, GROUPS, 2])
        sc = per_unit("sc", [GT, 16, GROUPS])
        h = per_unit("h", [GT, GROUPS, D])
        e = per_unit("e", [GT, GROUPS, D])
        hid = per_unit("hid", [GT, GROUPS, D])
        raw = per_unit("raw", [GT, GROUPS, WCOL])
        tmp = per_unit("tmp", [GT, GROUPS, D + 1])
        vs = tmp
        sy = tmp
        eT = per_unit("eT", [DH2 + 1, 2, UT])
        z2T = per_unit("z2T", [DH2 + 1, 2, UT])
        shareT = per_unit("shareT", [GT, 2, UT])
        uT = [shareT[u][0:DH2] for u in range(UNITS)]
        pick = per_unit("pick", [GT, GROUPS, USEL])
        pickT = per_unit("pickT", [USEL, UT])
        zselT = per_unit("zselT", [DH2 + 1, 2, USEL])
        qblk = per_unit("qblk", [DH2, 2, GROUPS, HS])
        probs = per_unit("probs", [GT, 2 * GROUPS, GT])
        pr = [probs[u][0:HS] for u in range(UNITS)]
        at = probs
        lsc = per_unit("lsc", [HS, 4, 2 * GROUPS])
        prT = [shareT[u][:, :, 0:GROUPS * HS] for u in range(UNITS)]
        ctm = [pr[u][0:DH2].rearrange("p x k -> p (x k)")[:, 0:2 * GROUPS * HS] for u in range(UNITS)]
        ctxT = per_unit("ctxT", [DH2 + 1, 2, USEL])
        ao = per_unit("ao", [USEL, D])
        base = per_unit("base", [GT, GROUPS, D])

        s = {n: sem(n) for n in (
            "d_tok d_gb d_edge d_small d_big x_in out_done "
            "c_pool c_dve c_act c_pe strips_zero raw_zero consts_done w_eff_ready weights_ready "
            "main_copied edge_copied cnt_ready cnt_used sq_ready tr_a tr_d ev_a ev_d tok_mm m_mu m_sq m_var m_veps "
            "rp_ready m_nmr t1_done h_done bn1 bn1_agg v1_ready r1_ready raw_ev e_done eT_mm eT_a eT_d u_mm u_ev v_mm v_ev s_mm s_max "
            "s_nb at_exp at_sum o_mm h2_done bn2 bn2_agg v2_ready v2b_ready r2_ready z_done hid_done zT_mm zT_a zT_d p_mm p_ev "
            "k_mm k_ev sg_exp sg_add score rank_mm rk1 rk2 rk3 pick_done not_sel sy_done pool_mm al1 al2 al3 mix1 mix2 mix3 "
            "pT_ev zs_mm zs_ev q_mm qb_done l_mm l_max l_nb l_exp l_rcp pr_done prT_mm prT_a prT_d c_mm ctm_done "
            "ctx_done ao_mm ao_ev x_mm hh_done bn3 bn3_agg v3_ready r3_ready z2_done z2T_mm z2T_a z2T_d base1 base2 up_mm gelu_done dn_mm fin_done"
        ).split()}

        STORED = 16 * UNITS * GROUPS

        class Tile:

            def __init__(self, eng, i):
                self.eng, self.i, self.b = eng, i, i * PER

            def wait(self, name, n):
                self.eng.wait_ge(s[name], self.b + n)

            def group(self, name, u, g):
                self.wait(name, US * u + GS * (g + 1))

            def unit(self, name, u):
                self.wait(name, US * (u + 1))

            def before(self, name, n=0):
                if self.i is not FIRST:
                    self.wait(name, -n)

        FIRST = 0

        def turns(eng, do):
            def run(i, order):
                for name, k in order:
                    if name in ("up", "down"):
                        tile = i - 1
                    elif name in ("halo", "copy", "squares", "turn", "patch"):
                        tile = i + 1
                    else:
                        tile = i
                    if name in do:
                        do[name](Tile(eng, tile), k)

            run(-1, BEFORE_FIRST)
            run(0, plan(False, True))
            with eng.Fori(1, ITERS - 1) as i:
                run(i, plan(True, True))
            run(ITERS - 1, plan(True, False))
            run(ITERS, AFTER_LAST)

        def bank(u, k):
            return ps[:, 3 * u + k, :]

        def spare(n):
            return ps[:, 6 + n % 2, :]

        def win_src(j, half):
            return spare(half)[0:CHUNK[j], 0:3 * XP].rearrange("p (w h b) -> p b h w", w=3, h=NP)

        def win_dst(j, half):
            v = winT[0:CHUNK[j], j].rearrange("p u t -> p (u t)")[:, 0:IB * POS].rearrange("p (b q) -> p b q", q=POS)[:, :, 1:]
            return v.rearrange("p b (h w) -> p b h w", w=NP)[:, :, :, 3 * half:3 * half + 3]

        def v_bank(u, g):
            return bank(u, 1)[0:GT, g * D:(g + 1) * D] if g < 2 else bank(u, 2)[0:GT, 0:D]

        def o_bank(u, g):
            return bank(u, 0)[0:GT, g * D:(g + 1) * D] if g < 2 else bank(u, 1)[0:GT, 0:D]

        def pool_bank(u, g, n=D + 1, o=0):
            return bank(u, 0)[0:GT, g * 256 + o:g * 256 + n] if g < 2 else bank(u, 1)[0:GT, o:n]

        def x_bank(u, g):
            return bank(u, 0)[0:GT, g * 256:g * 256 + D] if g < 2 else bank(u, 1)[0:GT, 0:D]

        def real(u, g):
            return min(GT, UR[u] - GT * g)

        tok_rows = A["L0_tok_W"].rearrange("(q f) d -> q f d", f=SH * C)
        gb_rows = [A[n].rearrange("(q f) -> q f", f=SH * C) for n in ("L0_tok_ln_gamma", "L0_tok_ln_beta")]
        OFF = [0, 1, -1, PS, -PS]
        edges = [
            (0, 0, 3, 0, 1), (0, 1, 4, PS * (PS - 1), 1), (1, 0, 1, 0, PS), (1, 1, 2, PS - 1, PS)]
        N_TOK, N_EDGE = 2 * SH, len(edges) * C
        attn_w = A["L0_attn_W"].rearrange("u (c p) n -> p (u c) n", c=2)
        out_rows = out.rearrange("b n d -> (b n) d")

        def chunked(name):
            return A[name].rearrange("(c p) n -> p c n", c=2)

        def row(name):
            return A[name].rearrange("(a n) -> a n", a=1)

        ctx.enter_context(nc.allow_non_contiguous_dma(reason="columns of per-feature factors, a few hundred words"))
        block = ctx.enter_context(nc.Block())

        @block.sync
        def _(sp):
            sp.wait_ge(s["raw_zero"], 1)
            for k in range(SH):
                for a in range(2):
                    lo, hi = max(0, 128 * a + OFF[k]), min(PS * PS, 128 * (a + 1) + OFF[k])
                    p0 = lo - 128 * a - OFF[k]
                    sp.dma_start(w_raw[p0:p0 + hi - lo, k, a], tok_rows[lo:hi, C * k:C * (k + 1), :]).then_inc(s["d_tok"], 16)
            sp.wait_ge(s["strips_zero"], 1)

            def load_images(i):
                for y in range(NP):
                    r0, r1 = max(0, PS * y - 1), min(HW, PS * y + PS + 1)
                    o = r0 - (PS * y - 1)
                    sp.dma_start(strips[IB * y:IB * (y + 1), :, o:o + r1 - r0, :],
                                 x_d[bass.ds(i * IB, IB), :, r0:r1, :]).then_inc(s["x_in"], 16)

            load_images(0)
            sp.dma_start(w2[:], A["L0_ffn_W2"].rearrange("(c p) n -> p c n", p=128)).then_inc(s["d_big"], 16)

            with sp.Fori(0, ITERS - 1) as i:
                t = Tile(sp, i)
                t.wait("main_copied", PER)
                t.wait("edge_copied", PER)
                load_images(i + 1)
            with sp.Fori(0, ITERS) as i:
                t = Tile(sp, i)
                for u in range(UNITS):
                    for g in range(GROUPS):
                        t.group("fin_done", u, g)
                        sp.dma_start(out_rows[bass.ds(i * (IB * POS) + (u * UT + g * GT), real(u, g)), :],
                                     base[u][0:real(u, g), g, :]).then_inc(s["out_done"], 16)
            sp.wait_ge(s["out_done"], ITERS * STORED)

        @block.gpsimd
        def _(pool):
            g = nc.gpsimd
            done = [0]

            def step(ins):
                done[0] += 1
                ins.then_inc(s["c_pool"], 1)
                pool.wait_ge(s["c_pool"], done[0])

            step(g.memset(strips[:, :, 0, :], 0.0))
            g.memset(strips[:, :, ROWS - 1, :], 0.0).then_inc(s["strips_zero"], 1)
            step(g.memset(w_raw[:, 1:SH, :], 0.0))
            g.memset(gb_raw[:], 0.0).then_inc(s["raw_zero"], 1)
            step(g.memset(ones[:], 1.0))
            step(g.memset(minus_half[:], -0.5))

            def select(view, src, pattern, base, cm, op, fill=0.0):
                step(g.affine_select(out=view, in_=src, compare_op=op, fill=fill, base=base,
                                     pattern=pattern, channel_multiplier=cm))

            def band(view, step_, width, n, inner, src=None):
                if src is None:
                    step(g.memset(view, 1.0))
                select(view, view, [[-step_, n], *[[0, k] for k in inner]], 0, 1, ALU.is_ge)
                select(view, view, [[step_, n], *[[0, k] for k in inner]], width - 1, -1, ALU.is_ge)

            step(g.memset(px_sel[:], 1.0))
            select(px_sel[:, 0, :], px_sel[:, 0, :], [[-PS, 8]], -(PS - 1), 1, ALU.not_equal)
            select(px_sel[:, 1, :], px_sel[:, 1, :], [[-PS, 8]], 0, 1, ALU.not_equal)
            step(g.memset(px_ok[:, 2:4], 1.0))
            select(px_ok[:, 2:3], px_ok[:, 2:3], [[0, 1]], 128 - PS - 1, -1, ALU.is_ge)
            select(px_ok[:, 3:4], px_ok[:, 3:4], [[0, 1]], -PS, 1, ALU.is_ge)
            step(g.memset(ident[:], 0.0))
            select(ident[:], ident[:], [[-1, 128]], 0, 1, ALU.not_equal, 1.0)
            step(g.memset(counts[:], float(SH)))
            cm = counts[:, 0:MAIN].rearrange("p (c y x) -> p c y x", c=C, y=PS)
            step(g.memset(counts[:, MAIN:], 1.0))
            for q in (0, PS - 1):
                step(g.memset(cm[:, :, q, :], float(SH - 1)))
                step(g.memset(cm[:, :, :, q], float(SH - 1)))
            for q in (0, PS - 1):
                for r in (0, PS - 1):
                    step(g.memset(cm[:, :, q, r], float(SH - 2)))
            step(g.memset(wins[:, 0, MAIN + EDGE:MAIN + EDGE + EDGE // 2], 0.0))
            step(g.memset(wins[:, NP - 1, MAIN + EDGE + EDGE // 2:WIN], 0.0))
            step(g.memset(winT[:], 0.0))
            band(same[:], POS, POS, GI, [POS])
            step(g.tensor_copy(before[:], same[:]))
            select(before[:], before[:], [[-POS, GI], [-1, POS]], 0, 1, ALU.is_gt)
            band(same_sel[:], POS, POS, GI, [TOPK])
            for j in range(TOPK):
                step(g.memset(slot_no[:, :, j:j + 1], float(j)))
            band(head_mask[:], DH, DH, HH, [SEL])
            step(g.memset(img_of_tok[:], 0.0))
            select(img_of_tok[:], img_of_tok[:], [[-1, GI], [0, POS]], 0, 1, ALU.not_equal, 1.0)
            step(g.memset(other_img[:], NEG))
            select(other_img[:], other_img[:], [[-1, GI], [0, POS]], 0, 1, ALU.not_equal, 0.0)
            step(g.memset(img_of_sel[:], 0.0))
            select(img_of_sel[:], img_of_sel[:], [[0, HH], [-1, GI], [0, TOPK]], 0, 1, ALU.not_equal, 1.0)
            cr = cls_rows[:].rearrange("a k (i q) -> a k i q", i=GI)
            step(g.memset(cls_rows[:, 0, :], 0.0))
            step(g.memset(cr[:, 0, :, 0:1], 1.0))
            step(g.memset(cls_rows[:, 1, :], 1.0))
            step(g.memset(cr[:, 1, :, 0:1], 0.0))
            for u in range(UNITS):
                step(g.memset(pick[u][:], 0.0))
                step(g.memset(eT[u][DH2:, 0, :], 1.0))
                step(g.memset(z2T[u][DH2:, 0, :], 1.0))
                step(g.memset(zselT[u][DH2:, 0, :], 1.0))
                step(g.memset(ctxT[u][DH2:, 0, :], 1.0))
            g.memset(w_eff[96:, CH - 1, :], 0.0).then_inc(s["consts_done"], 1)

            w5 = wins[:, :, MAIN:WIN].rearrange("p w (k a c x) -> p w k a c x", k=2, a=2, c=C)
            st5 = strips[:].rearrange("p c y (w x) -> p c y w x", x=PS)

            def halo(t, _):
                pool.wait_ge(s["x_in"], (t.i + 1) * (16 * NP))
                t.before("tr_a")
                t.before("tr_d")
                for a in range(2):
                    src = st5[:, :, a * (ROWS - 1), :, :].rearrange("p c w x -> p w c x")
                    g.tensor_copy(w5[:, :, 0, a, :, :], src).then_inc(s["edge_copied"], PER // 4)
                for a in range(2):
                    x0 = PS - 1 if a == 0 else PS
                    src = strips[:, :, 1:PS + 1, x0:x0 + PS * (NP - 2) + 1:PS].rearrange("p c y w -> p w c y")
                    g.tensor_copy(w5[:, 1 - a:NP - a, 1, a, :, :], src).then_inc(s["edge_copied"], PER // 4)

            def squares(t, w):
                t.wait("edge_copied", PER)
                t.wait("main_copied", GS * (w + 1))
                if w > 0:
                    t.wait("cnt_used", GS * w)
                else:
                    t.before("cnt_used")
                g.tensor_tensor(wcnt[:], wins[:, w, 0:WIN], counts[:], ALU.mult).then_inc(s["cnt_ready"], GS)

            def rsqrt(t, u, src, dst, name, ready):
                t.unit(name, u)
                g.tensor_tensor(dst, src, minus_half[0:GT, 0:GROUPS], ALU.pow).then_inc(s[ready], US)

            def sums(t, u):
                rsqrt(t, u, mom[u][:, 3, :], mom[u][:, 4, :], "m_veps", "rp_ready")

            def token(t, u):
                rsqrt(t, u, sc[u][:, 0, :], sc[u][:, 1, :], "v1_ready", "r1_ready")

            def attend(t, u):
                t.unit("v2_ready", u)
                t.unit("v2b_ready", u)
                g.tensor_tensor(sc[u][:, 4:6, :], sc[u][:, 2:4, :],
                                minus_half[0:GT, 0:1].broadcast_to((GT, 2 * GROUPS)).rearrange("p (a g) -> p a g", a=2),
                                ALU.pow).then_inc(s["r2_ready"], US)

            def pool_(t, u):
                t.unit("mix1", u)
                g.tensor_tensor(tmp[u][:, :, 0:D], tmp[u][:, :, 0:D], proj[u][:, :, D:2 * D], ALU.add).then_inc(s["mix2"], US)

            def shares(t, u):
                t.unit("l_rcp", u)
                g.tensor_tensor(pr[u][:], pr[u][:], lsc[u][:, 3, :].rearrange("p (x a) -> p x a", a=1)
                                .broadcast_to((HS, 2 * GROUPS, GT)), ALU.mult).then_inc(s["pr_done"], US)

            def scatter(t, u):
                rsqrt(t, u, sc[u][:, 6, :], sc[u][:, 7, :], "v3_ready", "r3_ready")
                if t.i is not FIRST:
                    pool.wait_ge(s["out_done"], t.i * STORED)
                g.tensor_tensor(base[u][:], h[u][:], hid[u][:], ALU.add).then_inc(s["base1"], US)
                t.unit("base1", u)
                g.tensor_tensor(base[u][:], base[u][:], bf2_all[:].rearrange("p (a d) -> p a d", a=1)
                                .broadcast_to((GT, GROUPS, D)), ALU.add).then_inc(s["base2"], US)

            turns(pool, dict(halo=halo, squares=squares, sums=sums, token=token, attend=attend, pool=pool_,
                             shares=shares, scatter=scatter))

        N_SMALL = 20

        @block.scalar
        def _(act):
            a_ = nc.scalar
            act.wait_ge(s["raw_zero"], 1)
            for k in range(SH):
                for a in range(2):
                    lo, hi = max(0, 128 * a + OFF[k]), min(PS * PS, 128 * (a + 1) + OFF[k])
                    p0 = lo - 128 * a - OFF[k]
                    for j in range(2):
                        act.dma_start(gb_raw[p0:p0 + hi - lo, k, j, a, :], gb_rows[j][lo:hi, :]).then_inc(s["d_gb"], 16)
            for q, side, k, first, stp in edges:
                for c in range(C):
                    p0 = side * (EDGE // 2) + c * PS
                    src = tok_rows[first:first + stp * (PS - 1) + 1:stp, C * k + c, :]
                    act.dma_start(w_edge[p0:p0 + PS, q, :], src).then_inc(s["d_edge"], 16)
                    for j in range(2):
                        act.dma_start(gb_edge[p0:p0 + PS, q, j:j + 1],
                                      gb_rows[j][first:first + stp * (PS - 1) + 1:stp, C * k + c:C * k + c + 1]
                                      ).then_inc(s["d_edge"], 16)
            small = [
                (rows1[:, 0, :], cls_d.rearrange("a b d -> (a b) d")), (rows1[:, 1, :], row("L0_tok_b")),
                (w_attn[:], attn_w),
                (wz[0:DH2, :, 0:D], chunked("L0_ffn_Wv")), (wz[0:DH2, :, D:2 * D], chunked("L0_ffn_Wm")),
                (wz[0:DH2, :, 2 * D + 1:ZC], A["L0_ffn_Wr"].rearrange("(c p n) -> p c n", c=2, n=1)),
                (wz[0:DH2, :, ZC:ZC + D], chunked("L0_ffn_Wk")), (wz[0:DH2, :, ZC + D:], chunked("L0_ffn_Wq")),
                (wo[0:DH2], chunked("L0_ffn_Wo")), (wo[DH2:, 0, :], row("L0_ffn_bo")),
                (w1[0:DH2], chunked("L0_ffn_W1")), (w1_b[:], row("L0_ffn_bf1")),
                (bm_all[:], row("L0_ffn_bm").broadcast_to((GT, D))), (bf2_all[:], row("L0_ffn_bf2").broadcast_to((GT, D))),
            ] + [(gcol[:, k, :], A[n].rearrange("(c p) -> p c", c=2)) for k, n in
                 enumerate(("L0_ffn_g1", "L0_ffn_b1", "L0_ffn_g2", "L0_ffn_b2"))]
            act.wait_ge(s["c_dve"], 1)
            small += [(wz_b[:, 0:D], row("L0_ffn_bv")), (wz_b[:, 2 * D + 1:ZC], A["L0_ffn_br"].rearrange("(a n) -> a n", a=1)
                       if len(A["L0_ffn_br"].shape) else A["L0_ffn_br"]),
                      (wz_b[:, ZC:ZC + D], row("L0_ffn_bk")), (wz_b[:, ZC + D:], row("L0_ffn_bq"))]
            assert len(small) == N_SMALL + 2
            for dst, src in small:
                act.dma_start(dst, src).then_inc(s["d_small"], 16)

            def copy(dst, src, name, n, scale=1.0):
                a_.activation(dst, src, ACT.Copy, scale=scale).then_inc(s[name], n)

            def window(t, w):
                if w == 0:
                    act.wait_ge(s["x_in"], (t.i + 1) * (16 * NP))
                    t.before("tr_a")
                    t.before("tr_d")
                copy(wins[:, w, 0:MAIN].rearrange("p (c y x) -> p c y x", c=C, y=PS),
                     strips[:, :, 1:PS + 1, PS * w:PS * (w + 1)], "main_copied", GS)

            def turn(t, n):
                j, half = n // 2, n % 2
                t.wait("tr_d" if half else "tr_a", TS_ * (j + 1))
                if n == 0:
                    t.before("tok_mm")
                    act.wait_ge(s["consts_done"], 1)
                copy(win_dst(j, half), win_src(j, half), "ev_d" if half else "ev_a", TS_)

            def patch(t, n):
                u, g = divmod(n, GROUPS)
                t.group("tok_mm", u, g)
                if n == 0:
                    t.before("h_done")
                copy(raw[u][:, g, :], spare(n)[0:GT, 0:WCOL], "raw_ev", GS)

            def flip1(t, u):
                t.wait("eT_mm", US * u + US // 2)
                copy(eT[u][0:DH2, 0, :], bank(u, 0)[0:DH2, 0:UT], "eT_a", US)

            def uv(t, u):
                for m in range(2):
                    t.wait("u_mm", US * u + US // 2 * (m + 1))
                    copy(uT[u][:, m, :], bank(u, 2 - 2 * m)[0:DH2, 0:UT], "u_ev", US // 2)

            def score(t, u):
                t.unit("s_nb", u)
                for g in range(GROUPS):
                    a_.activation(at[u][:, g, :], bank(u, 0)[0:GT, g * GT:(g + 1) * GT], ACT.Exp, bias=sc[u][:, 9, g:g + 1],
                                  scale=D ** -0.5, accum_out=sc[u][:, 10, g:g + 1]).then_inc(s["at_exp"], GS)

            def weigh(t, u):
                t.unit("at_sum", u)
                for g in range(GROUPS):
                    t.group("v_mm", u, max(g, 1))
                    copy(vs[u][:, g, 0:D], v_bank(u, g), "v_ev", GS, sc[u][:, 11, g:g + 1])

            def flip2(t, u):
                t.wait("zT_mm", US * u + US // 2)
                copy(eT[u][0:DH2, 0, :], bank(u, 2)[0:DH2, 0:UT], "zT_a", US)

            def project(t, u):
                for g in range(GROUPS):
                    t.group("p_mm", u, g)
                    copy(proj[u][:, g, :], bank(u, g)[0:GT, 0:ZC], "p_ev", GS)
                t.unit("p_ev", u)
                a_.activation(sc[u][:, 12, :], proj[u][:, :, ZC - 1], ACT.Exp, scale=-1.0).then_inc(s["sg_exp"], US)
                for m in range(2):
                    t.wait("k_mm", US * u + US // 2 * (m + 1))
                    copy(uT[u][:, m, :], bank(u, m)[0:DH2, 0:UT], "k_ev", US // 2)

            def router(t, u):
                t.unit("score", u)
                for g in range(GROUPS):
                    copy(sy[u][:, g, :], proj[u][:, g, D:2 * D + 1], "sy_done", GS, sc[u][:, 13, g:g + 1])

            def pick_(t, u):
                t.unit("zs_mm", u)
                copy(zselT[u][0:DH2], bank(u, 2)[0:DH2, 0:128].rearrange("p (c n) -> p c n", c=2)[:, :, 0:USEL], "zs_ev", US)
                copy(pickT[u][:], bank(u, 2)[0:USEL, 128:128 + UT], "pT_ev", US)

            def logits(t, u):
                t.unit("l_nb", u)
                for k in range(2 * GROUPS):
                    c, g = k // GROUPS, k % GROUPS
                    a_.activation(pr[u][:, k, :], bank(u, c)[0:HS, g * GT:(g + 1) * GT], ACT.Exp,
                                  bias=lsc[u][:, 1, k:k + 1], scale=DH ** -0.5,
                                  accum_out=lsc[u][:, 2, k:k + 1]).then_inc(s["l_exp"], US // 6)

            def flip3(t, u):
                t.wait("prT_mm", US * u + US // 2)
                copy(prT[u][:, 0, :], bank(u, 0)[0:GT, 0:GROUPS * HS], "prT_a", US)

            def out_(t, u):
                t.unit("ao_mm", u)
                copy(ao[u][:], bank(u, 2)[0:USEL, 0:D], "ao_ev", US)

            def flip4(t, u):
                t.wait("z2T_mm", US * u + US // 2)
                copy(z2T[u][0:DH2, 0, :], bank(u, 2)[0:DH2, 0:UT], "z2T_a", US)

            def up(t, k):
                u, m = divmod(k, FC)
                t.wait("up_mm", US * u + UP * (m + 1))
                if k == 0:
                    t.before("dn_mm")
                a_.activation(gelu_t[u][:, m, :], spare(m)[:, 0:UR[u]], ACT.Gelu).then_inc(s["gelu_done"], UP)

            turns(act, dict(copy=window, turn=turn, patch=patch, flip1=flip1, uv=uv, score=score, weigh=weigh, flip2=flip2,
                            project=project, router=router, pick=pick_, logits=logits, flip3=flip3, out=out_, flip4=flip4, up=up))

        @block.vector
        def _(dve):
            v = nc.vector
            done = [0]

            def step(ins):
                done[0] += 1
                ins.then_inc(s["c_dve"], 1)
                dve.wait_ge(s["c_dve"], done[0])

            step(v.memset(wz_b[:], 0.0))
            step(v.memset(wz_b[:, 2 * D:2 * D + 1], 1.0))
            step(v.memset(wz[0:DH2, :, 2 * D:2 * D + 1], 0.0))
            dve.wait_ge(s["consts_done"], 1)
            step(v.tensor_reduce(px_ok[:, 0:1], px_sel[:, 0, :], AX_X, ALU.min))
            step(v.tensor_reduce(px_ok[:, 1:2], px_sel[:, 1, :], AX_X, ALU.min))
            dve.wait_ge(s["d_gb"], 16 * 4 * SH)
            for k in (1, 2):
                view = gb_raw[:, k].rearrange("p j a f -> p (j a f)")
                step(v.tensor_scalar(view, view, px_ok[:, k - 1:k], None, ALU.mult))
            for a in range(2):
                cnt = w_eff[:, a, D:D + 1]
                step(v.tensor_scalar(cnt, px_ok[:, 0:1], px_ok[:, 1:2], 2.0, ALU.add, ALU.add))
                step(v.tensor_scalar(cnt, cnt, px_ok[:, 3 - a:4 - a], None, ALU.add))
                for c in range(1, C):
                    step(v.tensor_copy(w_eff[:, 2 * c + a, D:D + 1], cnt))
            step(v.memset(w_eff[:, 0:KW, D + 1:], 0.0))
            step(v.memset(w_eff[0:EDGE, KW:, D:D + 1], 1.0))
            step(v.memset(w_eff[0:EDGE, KW:, D + 1:], 0.0))
            step(v.memset(w_eff[EDGE:EDGE + 1, CH - 1, D + 1:], 1.0))
            dve.wait_ge(s["d_tok"], 16 * N_TOK)
            dve.wait_ge(s["d_edge"], 16 * 3 * N_EDGE)
            for k in range(SH):
                for c in range(C):
                    for a in range(2):
                        dst, gam = w_eff[:, 2 * c + a, 0:D], gb_raw[:, k, 0, a, C * k + c:C * k + c + 1]
                        if k == 0:
                            ins = v.tensor_scalar(dst, w_raw[:, k, a, c], gam, None, ALU.mult)
                        else:
                            ins = v.scalar_tensor_tensor(out=dst, in0=w_raw[:, k, a, c], scalar=gam, in1=dst,
                                                         op0=ALU.mult, op1=ALU.add)
                        done[0] += 1
                        ins.then_inc(s["c_dve"], 1)
                dve.wait_ge(s["c_dve"], done[0])
            for q in range(2):
                step(v.tensor_scalar(w_eff[0:EDGE, KW + q, 0:D], w_edge[:, q, :], gb_edge[:, q, 0:1], None, ALU.mult))
            v.memset(lsc[0][:, 0, :], 0.0).then_inc(s["w_eff_ready"], 1)
            for k, dst in ((0, w_qT), (1, w_kT)):
                dve.wait_ge(s["c_pe"], 1 + k)
                step(v.tensor_copy(dst[:], ps[0:DH2, 6 + k, 0:2 * D].rearrange("p (c n) -> p c n", c=2)))
            dve.wait_ge(s["c_pe"], 3)
            step(v.tensor_copy(w_qk[:], ps[0:DH2, 5, 0:2 * D].rearrange("p (c n) -> p c n", c=2)))
            dve.wait_ge(s["c_pe"], 4)
            step(v.tensor_tensor(wz[DH2:, 0, 0:ZC], ps[0:1, 0, 0:ZC], wz_b[:, 0:ZC], ALU.add))
            step(v.tensor_tensor(wz[DH2:, 0, ZC:], ps[0:1, 1, 0:2 * D], wz_b[:, ZC:], ALU.add))
            for j in range(2):
                step(v.tensor_tensor(w1[DH2:, 0, j * 384:(j + 1) * 384], ps[0:1, 2 + j, 0:384], w1_b[:, j * 384:(j + 1) * 384], ALU.add))
            for c in range(2):
                step(v.tensor_scalar(wz[0:DH2, c, :], wz[0:DH2, c, :], gcol[:, 0, c:c + 1], None, ALU.mult))
                step(v.tensor_scalar(w1[0:DH2, c, :], w1[0:DH2, c, :], gcol[:, 2, c:c + 1], None, ALU.mult))
            dve.wait_ge(s["c_pe"], 5)
            step(v.tensor_copy(colsum[:], ps[0:GT, 4, 0:D]))
            step(v.tensor_tensor(rows1[:, 1, :], ps[0:1, 4, 256:256 + D], rows1[:, 1, :], ALU.add))
            dve.wait_ge(s["c_pe"], 6)
            v.tensor_copy(tok_bias[:], ps[0:GT, 5, 0:D]).then_inc(s["weights_ready"], 1)
            dve.wait_ge(s["weights_ready"], 1)

            def squares(t, w):
                t.wait("cnt_ready", GS * (w + 1))
                t.wait("main_copied", PER)
                v.tensor_tensor_reduce(wcnt[:], wcnt[:], wins[:, w, 0:WIN], 1.0, 0.0, ALU.mult, ALU.add,
                                       wins[:, w, WIN:WIN + 1]).then_inc(s["cnt_used"], GS)

            def sums(t, u):
                m = mom[u]
                t.unit("raw_ev", u)
                v.tensor_scalar(m[:, 0, :], raw[u][:, :, D], 1.0 / FEAT, None, ALU.mult).then_inc(s["m_mu"], US)
                t.unit("m_mu", u)
                v.tensor_tensor(m[:, 1, :], m[:, 0, :], m[:, 0, :], ALU.mult).then_inc(s["m_sq"], US)
                t.unit("m_sq", u)
                v.scalar_tensor_tensor(out=m[:, 2, :], in0=raw[u][:, :, D + 1], scalar=1.0 / FEAT, in1=m[:, 1, :],
                                       op0=ALU.mult, op1=ALU.subtract).then_inc(s["m_var"], US)
                t.unit("m_var", u)
                v.tensor_scalar(m[:, 3, :], m[:, 2, :], 0.0, EPS, ALU.max, ALU.add).then_inc(s["m_veps"], US)

            def stats(t, u, src, written, name, agg, outs):
                for g in range(GROUPS):
                    t.group(written, u, g)
                    v.bn_stats(bn[u][:, g, :], src[u][:, g, :]).then_inc(s[name], GS)
                t.unit(name, u)
                v.tensor_copy(mom[u][:, 1, :], bn[u][:, :, 0]).then_inc(s[agg], US // 4)
                for g in range(GROUPS):
                    v.bn_aggr(mv[u][:, g, :], bn[u][:, g, :]).then_inc(s[agg], US // 4)
                for ready, dst, fac, add in outs:
                    t.unit(agg, u)
                    v.tensor_scalar(sc[u][:, dst, :], mv[u][:, :, 1], fac, add, ALU.mult, ALU.add).then_inc(s[ready], US)

            def normalise(u, src, r, name):
                for g in range(GROUPS):
                    v.tensor_scalar(e[u][:, g, :], src[u][:, g, :], mv[u][:, g, 0:1], sc[u][:, r, g:g + 1],
                                    ALU.subtract, ALU.mult).then_inc(s[name], GS)

            def token(t, u):
                m = mom[u]
                t.unit("rp_ready", u)
                v.scalar_tensor_tensor(out=m[:, 5, :], in0=m[:, 0, :], scalar=-1.0, in1=m[:, 4, :],
                                       op0=ALU.mult, op1=ALU.mult).then_inc(s["m_nmr"], US)
                t.unit("m_nmr", u)
                t.before("base1")
                for g in range(GROUPS):
                    v.scalar_tensor_tensor(out=tmp[u][:, g, 0:D], in0=colsum[:], scalar=m[:, 5, g:g + 1], in1=tok_bias[:],
                                           op0=ALU.mult, op1=ALU.add).then_inc(s["t1_done"], GS)
                for g in range(GROUPS):
                    t.group("t1_done", u, g)
                    v.scalar_tensor_tensor(out=h[u][:, g, :], in0=raw[u][:, g, 0:D], scalar=m[:, 4, g:g + 1],
                                           in1=tmp[u][:, g, 0:D], op0=ALU.mult, op1=ALU.add).then_inc(s["h_done"], GS)
                stats(t, u, h, "h_done", "bn1", "bn1_agg", [("v1_ready", 0, 1.0, EPS)])

            def norm1(t, u):
                t.unit("r1_ready", u)
                normalise(u, h, 1, "e_done")

            def flip1(t, u):
                t.unit("eT_mm", u)
                v.tensor_copy(eT[u][0:DH2, 1, :], bank(u, 1)[0:DH2, 0:UT]).then_inc(s["eT_d"], US)

            def score(t, u):
                t.unit("s_mm", u)
                v.tensor_reduce(sc[u][:, 8, :], bank(u, 0)[0:GT, 0:UT].rearrange("p (g q) -> p g q", g=GROUPS), AX_X,
                                ALU.max).then_inc(s["s_max"], US)
                t.unit("s_max", u)
                v.tensor_scalar(sc[u][:, 9, :], sc[u][:, 8, :], -(D ** -0.5), None, ALU.mult).then_inc(s["s_nb"], US)

            def weigh(t, u):
                t.unit("at_exp", u)
                v.reciprocal(sc[u][:, 11, :], sc[u][:, 10, :]).then_inc(s["at_sum"], US)

            def attend(t, u):
                for g in range(GROUPS):
                    t.group("o_mm", u, max(g, 1))
                    v.tensor_tensor(h[u][:, g, :], h[u][:, g, :], o_bank(u, g), ALU.add).then_inc(s["h2_done"], GS)
                stats(t, u, h, "h2_done", "bn2", "bn2_agg",
                      [("v2_ready", 2, 1.0, EPS), ("v2b_ready", 3, 1.0 + EPS, EPS * EPS)])

            def norm2(t, u):
                t.unit("r2_ready", u)
                normalise(u, h, 5, "z_done")

            def flip2(t, u):
                t.unit("zT_mm", u)
                v.tensor_copy(eT[u][0:DH2, 1, :], bank(u, 1)[0:DH2, 0:UT]).then_inc(s["zT_d"], US)
                for g in range(GROUPS):
                    v.tensor_scalar(hid[u][:, g, :], h[u][:, g, :], mv[u][:, g, 0:1], sc[u][:, 4, g:g + 1],
                                    ALU.subtract, ALU.mult).then_inc(s["hid_done"], GS)

            def router(t, u):
                q = sc[u]
                t.unit("sg_exp", u)
                v.tensor_scalar(q[:, 14, :], q[:, 12, :], 1.0, None, ALU.add).then_inc(s["sg_add"], US)
                t.unit("sg_add", u)
                v.reciprocal(q[:, 13, :], q[:, 14, :]).then_inc(s["score"], US)

            def rank(t, u):
                m = mom[u]
                for g in range(GROUPS):
                    others = bank(u, 2)[0:GT, g * GT:(g + 1) * GT]
                    t.unit("rank_mm", u)
                    v.scalar_tensor_tensor(out=at[u][:, g, :], in0=others, scalar=sc[u][:, 13, g:g + 1],
                                           in1=same[:].rearrange("p i q -> p (i q)"), op0=ALU.is_lt, op1=ALU.mult,
                                           accum_out=m[:, 0, g:g + 1]).then_inc(s["rk1"], GS)
                    v.scalar_tensor_tensor(out=at[u][:, GROUPS + g, :], in0=others, scalar=sc[u][:, 13, g:g + 1],
                                           in1=before[:].rearrange("p i q -> p (i q)"), op0=ALU.is_equal, op1=ALU.mult,
                                           accum_out=m[:, 1, g:g + 1]).then_inc(s["rk2"], GS)
                t.unit("rk1", u)
                t.unit("rk2", u)
                v.tensor_tensor(m[:, 2, :], m[:, 0, :], m[:, 1, :], ALU.add).then_inc(s["rk3"], US)
                t.unit("rk3", u)
                for g in range(GROUPS):
                    v.scalar_tensor_tensor(out=pick[u][:, g, g * SEL:(g + 1) * SEL], in0=slot_no[:].rearrange("p i j -> p (i j)"),
                                           scalar=m[:, 2, g:g + 1], in1=same_sel[:].rearrange("p i j -> p (i j)"),
                                           op0=ALU.is_equal, op1=ALU.mult).then_inc(s["pick_done"], GS)
                v.tensor_scalar(m[:, 5, :], m[:, 2, :], float(TOPK), None, ALU.is_ge).then_inc(s["not_sel"], US)

            def pool_(t, u):
                q = sc[u]
                t.unit("pool_mm", u)
                v.tensor_scalar(q[:, 14, 0:2], bank(u, 0)[0:GT, D:D + 257:256], 1e-6, None, ALU.add).then_inc(s["al1"], US // 2)
                v.tensor_scalar(q[:, 14, 2:3], pool_bank(u, 2, D + 1, D), 1e-6, None, ALU.add).then_inc(s["al1"], US // 2)
                t.unit("al1", u)
                v.reciprocal(q[:, 15, :], q[:, 14, :]).then_inc(s["al2"], US)
                t.unit("al2", u)
                v.tensor_tensor(q[:, 8, :], q[:, 15, :], q[:, 13, :], ALU.mult).then_inc(s["al3"], US)
                t.unit("al3", u)
                for g in range(GROUPS):
                    v.scalar_tensor_tensor(out=tmp[u][:, g, 0:D], in0=pool_bank(u, g, D), scalar=q[:, 8, g:g + 1], in1=bm_all[:],
                                           op0=ALU.mult, op1=ALU.add).then_inc(s["mix1"], GS)

            def query(t, u):
                t.unit("q_mm", u)
                for c in range(2):
                    src = bank(u, 2)[0:DH2, 64 * c:64 * c + USEL].rearrange("p (g a j) -> p g a j", g=GROUPS, a=1)
                    v.tensor_tensor(qblk[u][:, c].rearrange("p g (h j) -> p g h j", h=HH),
                                    src.broadcast_to((DH2, GROUPS, HH, SEL)),
                                    head_mask[:].rearrange("p (a h) j -> p a h j", a=1).broadcast_to((DH2, GROUPS, HH, SEL)),
                                    ALU.mult).then_inc(s["qb_done"], US // 2)

            def logits(t, u):
                q = lsc[u]
                t.unit("l_mm", u)
                v.tensor_reduce(q[:, 0, :].rearrange("p (c g) -> p c g", c=2),
                                ps[0:HS, 3 * u:3 * u + 2, 0:UT].rearrange("p c (g k) -> p c g k", g=GROUPS),
                                AX_X, ALU.max).then_inc(s["l_max"], US)
                t.unit("l_max", u)
                v.tensor_scalar(q[:, 1, :], q[:, 0, :], -(DH ** -0.5), None, ALU.mult).then_inc(s["l_nb"], US)

            def shares(t, u):
                t.unit("l_exp", u)
                v.reciprocal(lsc[u][:, 3, :], lsc[u][:, 2, :]).then_inc(s["l_rcp"], US)
                t.unit("mix2", u)
                t.unit("not_sel", u)
                t.unit("hid_done", u)
                for g in range(GROUPS):
                    v.scalar_tensor_tensor(out=hid[u][:, g, :], in0=tmp[u][:, g, 0:D], scalar=mom[u][:, 5, g:g + 1],
                                           in1=hid[u][:, g, :], op0=ALU.mult, op1=ALU.add).then_inc(s["mix3"], GS)

            def flip3(t, u):
                t.unit("prT_mm", u)
                v.tensor_copy(prT[u][:, 1, :], bank(u, 1)[0:GT, 0:GROUPS * HS]).then_inc(s["prT_d"], US)

            def context(t, u):
                t.unit("c_mm", u)
                v.tensor_tensor(ctm[u].rearrange("p (c g n) -> p c g n", c=2, g=GROUPS),
                                ps[0:DH2, 3 * u:3 * u + 2, 0:GROUPS * HS].rearrange("p c (g n) -> p c g n", g=GROUPS),
                                head_mask[:].rearrange("p (a b h) j -> p a b (h j)", a=1, b=1)
                                .broadcast_to((DH2, 2, GROUPS, HS)), ALU.mult).then_inc(s["ctm_done"], US)
                t.unit("ctm_done", u)
                v.tensor_reduce(ctxT[u][0:DH2].rearrange("p c (g j) -> p (c g) j", g=GROUPS),
                                ctm[u].rearrange("p (x h j) -> p x j h", h=HH, j=SEL), AX_X, ALU.add).then_inc(s["ctx_done"], US)

            def scatter(t, u):
                for g in range(GROUPS):
                    t.group("x_mm", u, max(g, 1))
                    t.group("mix3", u, g)
                    v.tensor_tensor(hid[u][:, g, :], hid[u][:, g, :], x_bank(u, g), ALU.add).then_inc(s["hh_done"], GS)
                stats(t, u, hid, "hh_done", "bn3", "bn3_agg", [("v3_ready", 6, 1.0, EPS)])

            def norm3(t, u):
                t.unit("r3_ready", u)
                normalise(u, hid, 7, "z2_done")

            def flip4(t, u):
                t.unit("z2T_mm", u)
                v.tensor_copy(z2T[u][0:DH2, 1, :], bank(u, 1)[0:DH2, 0:UT]).then_inc(s["z2T_d"], US)

            def down(t, k):
                u, g = divmod(k, GROUPS)
                n = real(u, g)
                t.group("dn_mm", u, g)
                t.unit("base2", u)
                v.tensor_tensor(base[u][0:n, g, :], spare(k)[0:n, 0:D], base[u][0:n, g, :], ALU.add).then_inc(s["fin_done"], GS)

            turns(dve, dict(squares=squares, sums=sums, token=token, norm1=norm1, flip1=flip1, score=score, weigh=weigh,
                            attend=attend, norm2=norm2, flip2=flip2, router=router, rank=rank, pool=pool_, query=query,
                            logits=logits, shares=shares, flip3=flip3, context=context, scatter=scatter, norm3=norm3,
                            flip4=flip4, down=down))

        @block.tensor
        def _(pe):
            t = nc.tensor
            pe.wait_ge(s["consts_done"], 1)
            pe.wait_ge(s["d_small"], 16 * (N_SMALL + 2))
            for k in range(2):
                for c in range(2):
                    for m in range(2):
                        last = t.transpose(ps[0:DH2, 6 + k, m * D + c * DH2:m * D + (c + 1) * DH2],
                                           w_attn[:, c, k * D + m * DH2:k * D + (m + 1) * DH2], ident[0:DH2, 0:DH2])
                last.then_inc(s["c_pe"], 1)
            pe.wait_ge(s["c_dve"], SETUP_QK)
            for m in range(2):
                for c in range(2):
                    last = t.matmul(ps[0:DH2, 5, m * D:(m + 1) * D], w_qT[:, c, m * DH2:(m + 1) * DH2], w_kT[:, c, :],
                                    start=(c == 0), stop=(c == 1))
            last.then_inc(s["c_pe"], 1)
            for j, (src, k, lo, hi) in enumerate(((wz, 1, 0, ZC), (wz, 1, ZC, ZC + 2 * D), (w1, 3, 0, 384), (w1, 3, 384, 768))):
                for c in range(2):
                    last = t.matmul(ps[0:1, j, 0:hi - lo], gcol[:, k, c:c + 1], src[0:DH2, c, lo:hi], start=(c == 0), stop=(c == 1))
            last.then_inc(s["c_pe"], 1)
            pe.wait_ge(s["w_eff_ready"], 1)
            for j in range(CH):
                n = min(CHUNK[j], 128) if j < KW else EDGE
                t.matmul(ps[0:GT, 4, 0:D], ones[0:n, 0:GT], w_eff[0:n, j, 0:D], start=(j == 0), stop=(j == CH - 1))
            pieces = [(gb_raw[:, k, 1, a, C * k + c:C * k + c + 1], w_raw[:, k, a, c]) for k in range(SH) for c in range(C)
                      for a in range(2)] + [(gb_edge[:, q, 1:2], w_edge[:, q, :]) for q in range(2)]
            for j, (bet, w) in enumerate(pieces):
                last = t.matmul(ps[0:1, 4, 256:256 + D], bet, w, start=(j == 0), stop=(j == len(pieces) - 1))
            last.then_inc(s["c_pe"], 1)
            pe.wait_ge(s["c_dve"], SETUP_ROWS)
            for j in range(2):
                last = t.matmul(ps[0:GT, 5, 0:D], cls_rows[:, j, :], rows1[:, j, :], start=(j == 0), stop=(j == 1))
            last.then_inc(s["c_pe"], 1)
            pe.wait_ge(s["weights_ready"], 1)
            pe.wait_ge(s["d_big"], 16)

            def to_columns(tile, u, src, done, name, banks):
                for c in range(2):
                    for g in range(GROUPS):
                        if c == 0:
                            tile.group(done, u, g)
                        last = t.transpose(bank(u, banks[c])[0:DH2, g * GT:(g + 1) * GT],
                                           src[u][:, g, c * DH2:(c + 1) * DH2], ident[0:GT, 0:GT])
                    last.then_inc(s[name], US // 2)

            def turn(tile, n):
                j, half = n // 2, n % 2
                if n == 0:
                    tile.wait("main_copied", PER)
                    tile.wait("edge_copied", PER)
                if j == CH - 1:
                    tile.wait("cnt_used", PER)
                if j > 0:
                    tile.wait("ev_d" if half else "ev_a", TS_ * j)
                elif tile.i is not FIRST:
                    if type(tile.i) is int and tile.i == 1:
                        tile.wait("raw_ev", half * GS - GS)
                    else:
                        pe.wait_ge(s["fin_done"], tile.b - 2 * PER + PER + half * GS - GS)
                for w in range(3):
                    last = t.transpose(spare(half)[0:CHUNK[j], w * XP:(w + 1) * XP],
                                       wins[:, 3 * half + w, sum(CHUNK[:j]):sum(CHUNK[:j + 1])], ident[0:XP, 0:XP])
                last.then_inc(s["tr_d" if half else "tr_a"], TS_)

            def patch(tile, n):
                u, g = divmod(n, GROUPS)
                if n == 0:
                    tile.wait("ev_a", PER)
                    tile.wait("ev_d", PER)
                if n >= 2:
                    tile.wait("raw_ev", GS * (n - 1))
                for j in range(CH):
                    last = t.matmul(spare(n)[0:GT, 0:WCOL], winT[0:CHUNK[j], j, u, g * GT:(g + 1) * GT],
                                    w_eff[0:CHUNK[j], j, :], start=(j == 0), stop=(j == CH - 1))
                last.then_inc(s["tok_mm"], GS)

            def flip1(tile, u):
                to_columns(tile, u, e, "e_done", "eT_mm", (0, 1))

            def uv(tile, u):
                tile.unit("eT_a", u)
                tile.unit("eT_d", u)
                for m in range(2):
                    for c in range(2):
                        last = t.matmul(bank(u, 2 - 2 * m)[0:DH2, 0:UT], w_qk[:, c, m * DH2:(m + 1) * DH2], eT[u][0:DH2, c, :],
                                        start=(c == 0), stop=(c == 1))
                    last.then_inc(s["u_mm"], US // 2)
                for g in range(GROUPS - 1):
                    value(tile, u, g)

            def value(tile, u, g):
                for c in range(2):
                    last = t.matmul(v_bank(u, g), eT[u][0:DH2, c, g * GT:(g + 1) * GT], w_attn[:, c, 2 * D:3 * D],
                                    start=(c == 0), stop=(c == 1))
                last.then_inc(s["v_mm"], GS)

            def score(tile, u):
                tile.unit("u_ev", u)
                for g in range(GROUPS):
                    o = bank(u, 0)[0:GT, g * GT:(g + 1) * GT]
                    cols = slice(g * GT, (g + 1) * GT)
                    t.matmul(o, img_of_tok[:].rearrange("p i q -> p (i q)"), other_img[:].rearrange("p i q -> p (i q)"),
                             start=True, stop=False)
                    for c in range(2):
                        last = t.matmul(o, eT[u][0:DH2, c, cols], uT[u][:, c, cols], start=False, stop=(c == 1))
                last.then_inc(s["s_mm"], US)
                value(tile, u, GROUPS - 1)

            def attend(tile, u):
                for g in range(GROUPS):
                    tile.group("v_ev", u, g)
                    t.matmul(o_bank(u, g), at[u][:, g, :], vs[u][:, g, 0:D], start=True, stop=True).then_inc(s["o_mm"], GS)

            def flip2(tile, u):
                to_columns(tile, u, e, "z_done", "zT_mm", (2, 1))

            def project(tile, u):
                tile.unit("zT_a", u)
                tile.unit("zT_d", u)
                for g in range(GROUPS):
                    o = bank(u, g)[0:GT, 0:ZC]
                    t.matmul(o, eT[u][0:DH2 + 1, 0, g * GT:(g + 1) * GT], wz[:, 0, 0:ZC], start=True, stop=False)
                    t.matmul(o, eT[u][0:DH2, 1, g * GT:(g + 1) * GT], wz[0:DH2, 1, 0:ZC], start=False, stop=True)\
                        .then_inc(s["p_mm"], GS)
                for m in range(2):
                    o = bank(u, m)[0:DH2, 0:UT]
                    tile.group("p_ev", u, m)
                    cols = slice(ZC + m * DH2, ZC + (m + 1) * DH2)
                    t.matmul(o, wz[:, 0, cols], eT[u][:, 0, :], start=True, stop=False)
                    t.matmul(o, wz[0:DH2, 1, cols], eT[u][0:DH2, 1, :], start=False, stop=True).then_inc(s["k_mm"], US // 2)

            def rank(tile, u):
                tile.unit("score", u)
                tile.unit("p_ev", u)
                for g in range(GROUPS):
                    last = t.transpose(bank(u, 2)[0:GT, g * GT:(g + 1) * GT], sc[u][:, 13, g:g + 1].broadcast_to((GT, GT)),
                                       ident[0:GT, 0:GT])
                last.then_inc(s["rank_mm"], US)

            def pool_(tile, u):
                tile.unit("k_ev", u)
                for g in range(GROUPS):
                    tile.group("sy_done", u, g)
                    last = t.matmul(pool_bank(u, g), same[:].rearrange("p i q -> p (i q)"), sy[u][:, g, :], start=True, stop=True)
                last.then_inc(s["pool_mm"], US)

            def pick_(tile, u):
                for c in range(2):
                    for g in range(GROUPS):
                        if c == 0:
                            tile.group("pick_done", u, g)
                        last = t.matmul(bank(u, 2)[0:DH2, 64 * c + g * SEL:64 * c + (g + 1) * SEL],
                                        e[u][:, g, c * DH2:(c + 1) * DH2], pick[u][:, g, g * SEL:(g + 1) * SEL],
                                        start=True, stop=True)
                for g in range(GROUPS):
                    last = t.transpose(bank(u, 2)[0:USEL, 128 + g * GT:128 + (g + 1) * GT], pick[u][:, g, :], ident[0:GT, 0:GT])
                last.then_inc(s["zs_mm"], US)

            def query(tile, u):
                tile.unit("zs_ev", u)
                tile.unit("pT_ev", u)
                for m in range(2):
                    o = bank(u, 2)[0:DH2, 64 * m:64 * m + USEL]
                    cols = slice(ZC + D + m * DH2, ZC + D + (m + 1) * DH2)
                    t.matmul(o, wz[:, 0, cols], zselT[u][:, 0, :], start=True, stop=False)
                    last = t.matmul(o, wz[0:DH2, 1, cols], zselT[u][0:DH2, 1, :], start=False, stop=True)
                last.then_inc(s["q_mm"], US)

            def logits(tile, u):
                tile.unit("qb_done", u)
                for c in range(2):
                    for g in range(GROUPS):
                        o = bank(u, c)[0:HS, g * GT:(g + 1) * GT]
                        t.matmul(o, img_of_sel[:].rearrange("p h i j -> p (h i j)"), other_img[:].rearrange("p i q -> p (i q)"),
                                 start=True, stop=False)
                        last = t.matmul(o, qblk[u][:, c, g, :], uT[u][:, c, g * GT:(g + 1) * GT], start=False, stop=True)
                last.then_inc(s["l_mm"], US)

            def flip3(tile, u):
                tile.unit("pr_done", u)
                for c in range(2):
                    for g in range(GROUPS):
                        last = t.transpose(bank(u, c)[0:GT, g * HS:(g + 1) * HS], pr[u][:, c * GROUPS + g, :],
                                           ident[0:HS, 0:HS])
                    last.then_inc(s["prT_mm"], US // 2)

            def context(tile, u):
                tile.unit("prT_a", u)
                tile.unit("prT_d", u)
                for c in range(2):
                    for g in range(GROUPS):
                        last = t.matmul(bank(u, c)[0:DH2, g * HS:(g + 1) * HS], proj[u][:, g, c * DH2:(c + 1) * DH2],
                                        prT[u][:, c, g * HS:(g + 1) * HS], start=True, stop=True)
                last.then_inc(s["c_mm"], US)

            def out_(tile, u):
                tile.unit("ctx_done", u)
                t.matmul(bank(u, 2)[0:USEL, 0:D], ctxT[u][:, 0, :], wo[:, 0, :], start=True, stop=False)
                t.matmul(bank(u, 2)[0:USEL, 0:D], ctxT[u][0:DH2, 1, :], wo[0:DH2, 1, :], start=False, stop=True)\
                    .then_inc(s["ao_mm"], US)

            def scatter(tile, u):
                tile.unit("ao_ev", u)
                for g in range(GROUPS):
                    t.matmul(x_bank(u, g), pickT[u][:, g * GT:(g + 1) * GT], ao[u][:], start=True, stop=True)\
                        .then_inc(s["x_mm"], GS)

            def flip4(tile, u):
                to_columns(tile, u, e, "z2_done", "z2T_mm", (2, 1))

            def up(tile, k):
                u, m = divmod(k, FC)
                if m == 0:
                    tile.unit("z2T_a", u)
                    tile.unit("z2T_d", u)
                if k >= 2:
                    tile.wait("gelu_done", UP * (k - 1))
                elif type(tile.i) is int and tile.i == ITERS - 1:
                    pe.wait_ge(s["fin_done"], tile.b + k * GS - GS)
                else:
                    pe.wait_ge(s["raw_ev"], tile.b + 2 * PER + k * GS - GS)
                o = spare(m)[:, 0:UR[u]]
                t.matmul(o, w1[:, 0, m * 128:(m + 1) * 128], z2T[u][:, 0, 0:UR[u]], start=True, stop=False)
                t.matmul(o, w1[0:DH2, 1, m * 128:(m + 1) * 128], z2T[u][0:DH2, 1, 0:UR[u]], start=False, stop=True)\
                    .then_inc(s["up_mm"], UP)

            def down(tile, k):
                u, g = divmod(k, GROUPS)
                n = real(u, g)
                if k == 0:
                    tile.wait("gelu_done", PER)
                if k >= 2:
                    tile.wait("fin_done", GS * (k - 1))
                for m in range(FC):
                    last = t.matmul(spare(k)[0:n, 0:D], gelu_t[u][:, m, g * GT:g * GT + n], w2[:, m, :],
                                    start=(m == 0), stop=(m == FC - 1))
                last.then_inc(s["dn_mm"], GS)

            turns(pe, dict(turn=turn, patch=patch, flip1=flip1, uv=uv, score=score, attend=attend, flip2=flip2, project=project,
                           rank=rank, pool=pool_, pick=pick_, query=query, logits=logits, flip3=flip3, context=context,
                           out=out_, scatter=scatter, flip4=flip4, up=up, down=down))


SETUP_COUNTS = 3 + 2 + 2 + 2 * (2 + (C - 1)) + 4
SETUP_QK = SETUP_COUNTS + SH * C * 2 + 2 + 2
SETUP_ROWS = SETUP_QK + 1 + 4 + 4 + 2

_INS = ['x', 'cls_tok', 'L0_tok_ln_gamma', 'L0_tok_ln_beta', 'L0_tok_W', 'L0_tok_b', 'L0_attn_W', 'L0_ffn_g1', 'L0_ffn_b1',
        'L0_ffn_g2', 'L0_ffn_b2', 'L0_ffn_Wr', 'L0_ffn_br', 'L0_ffn_Wq', 'L0_ffn_bq', 'L0_ffn_Wk', 'L0_ffn_bk', 'L0_ffn_Wv',
        'L0_ffn_bv', 'L0_ffn_Wo', 'L0_ffn_bo', 'L0_ffn_Wm', 'L0_ffn_bm', 'L0_ffn_W1', 'L0_ffn_bf1', 'L0_ffn_W2', 'L0_ffn_bf2']


def kernel(**inputs):
    import numpy as _np
    import concourse.bacc as _bacc
    from concourse import mybir as _mybir
    from concourse.bass_utils import run_bass_kernel_spmd as _run

    nc = _bacc.Bacc("TRN2", target_bir_lowering=False, num_devices=1)
    arrays, args = {}, {}
    for name in _INS:
        a = _np.ascontiguousarray(inputs[name])
        if a.ndim == 0:
            a = a.reshape(1)
        arrays[f"in_{name}_dram"] = a
        args[name] = nc.dram_tensor(f"in_{name}_dram", a.shape, _mybir.dt.from_np(a.dtype), kind="ExternalInput").ap()
    out = nc.dram_tensor("out_0_dram", (B, POS, D), _mybir.dt.float32, kind="ExternalOutput").ap()
    vit_tower(nc, args, out)
    r = _run(nc, [arrays], core_ids=[0])
    return r.results[0]["out_0_dram"]
```

```python
from contextlib import ExitStack

import concourse.bass as bass
from concourse import mybir

F32 = mybir.dt.float32
BF16 = mybir.dt.bfloat16
ALU = mybir.AluOpType
ACT = mybir.ActivationFunctionType
AX_X = mybir.AxisListType.X

B, C, HW = 64, 3, 96
PS = 16
NP = HW // PS
POS = NP * NP + 1
D = 192
DH2 = D // 2
SH = 5
FEAT = PS * PS * SH * C
HEADS, DH = 12, 16
HH = HEADS // 2
F = 768
FC = F // 128
TOPK = max(1, int(round(0.15 * POS)))
EPS = 1e-5

IB = 16
ITERS = B // IB
UNITS = 2
GI = 3
GROUPS = 3
SLOTS = GI * GROUPS
GT = GI * POS
UT = SLOTS * POS
UR = [min(UT, IB * POS - u * UT) for u in range(UNITS)]
SEL = GI * TOPK
USEL = SEL * GROUPS
HS = HH * SEL
XP = NP * IB

ROWS = PS + 2
MAIN = C * PS * PS
EDGE = 2 * C * PS
WIN = MAIN + 2 * EDGE
KW = MAIN // 128
CH = KW + 2
WCOL = D + 2
CHUNK = [128] * KW + [EDGE, EDGE + 1]

PER = 24
GS = PER // (UNITS * GROUPS)
US = PER // UNITS
TJOBS = 16
TS_ = PER // (TJOBS // 2)
UP = US // FC


PROLOGUE = """
    attn.0 qk.0 bands.0 shift.0 shift.1 shift.2 shift.3 shift.4 halo.0 copy.0 copy.1 copy.2 copy.3 copy.4 copy.5
    norm_row.0 window.0 turn.0 turn.1 window.1 squares.0 turn.2 turn.3 window.2 squares.1 turn.4 turn.5
    window.3 squares.2 turn.6 turn.7 window.4 squares.3 turn.8 turn.9 window.5 squares.4 turn.10 turn.11
    window.6 squares.5 turn.12 turn.13 window.7 turn.14 turn.15
    patch.0 patch.1 bias.0 patch.2 ready.0
"""

FIRST_TURN = """
    copy.0 patch.3 patch.4 halo.0 copy.1 sums.0 token.0 squares.0 copy.2 patch.5 norm1.0 sums.1
    copy.3 squares.1 flip1.0 token.1 rows.0 squares.2 uv.0 score.0 norm1.1 rows.1 weigh.0 flip1.1
    rows.2 copy.4 attend.0 squares.3 uv.1 score.1 copy.5 norm2.0 weigh.1 rows.3 flip2.0 turn.0
    turn.1 attend.1 turn.2 squares.4 norm2.1 factors.0 turn.3 project.0 router.0 flip2.1 turn.4
    rank.0 pool.0 squares.5 project.1 pick.0 router.1 rank.1 turn.5 turn.6 query.0 pool.1 pick.1
    turn.7 turn.8 query.1 logits.0 logits.1 shares.0 turn.9 turn.10 shares.1 flip3.0 turn.11
    turn.12 flip3.1 context.0 turn.13 context.1 turn.14 turn.15 out.0 scatter.0 norm3.0 out.1
    patch.0 scatter.1 patch.1 flip4.0 patch.2 norm3.1 flip4.1
"""

TURN = """
    sums.0 copy.0 patch.3 patch.4 token.0 patch.5 norm1.0 sums.1 copy.1 up.0 flip1.0 up.1 copy.2
    up.2 copy.3 up.3 halo.0 token.1 up.4 copy.4 uv.0 norm1.1 squares.0 up.5 flip1.1 score.0 uv.1
    weigh.0 score.1 up.6 attend.0 up.7 squares.1 up.8 copy.5 up.9 up.10 norm2.0 up.11 turn.0
    weigh.1 flip2.0 turn.1 squares.2 turn.2 attend.1 squares.3 project.0 turn.3 turn.4 router.0
    norm2.1 rank.0 flip2.1 turn.5 turn.6 squares.4 pool.0 turn.7 turn.8 pick.0 squares.5 project.1
    turn.9 turn.10 router.1 rank.1 query.0 turn.11 turn.12 pool.1 turn.13 turn.14 pick.1 turn.15
    down.0 query.1 logits.0 logits.1 shares.0 down.1 down.2 shares.1 flip3.0 down.3 flip3.1
    context.0 context.1 down.4 out.0 down.5 scatter.0 out.1 patch.0 norm3.0 scatter.1 patch.1
    patch.2 norm3.1 flip4.0 flip4.1
"""

LAST_TURN = """
    patch.3 sums.0 token.0 patch.4 patch.5 up.0 norm1.0 sums.1 flip1.0 up.1 token.1 up.2 norm1.1
    up.3 uv.0 up.4 up.5 flip1.1 score.0 weigh.0 uv.1 attend.0 up.6 up.7 score.1 norm2.0 weigh.1
    flip2.0 up.8 up.9 attend.1 project.0 norm2.1 router.0 flip2.1 rank.0 pool.0 project.1 router.1
    rank.1 pick.0 up.10 up.11 query.0 pool.1 pick.1 logits.0 query.1 down.0 logits.1 down.1
    shares.0 shares.1 down.2 flip3.0 flip3.1 context.0 context.1 down.3 out.0 scatter.0 out.1
    norm3.0 down.4 down.5 flip4.0 scatter.1 last_up.0 last_up.1 last_up.2 norm3.1 last_up.3 flip4.1
    last_up.4 last_up.5 last_up.6 last_up.7 last_up.8 last_up.9 last_up.10 last_up.11 last_down.0
    last_down.1 last_down.2 last_down.3 last_down.4 last_down.5
"""


def items(order):
    return [(name, int(k)) for name, k in (item.split(".") for item in order.split())]


DIAG = 128 + PS
BAND = DIAG + PS * PS
EROW = (2 * C - 1) * PS
ECOL = (2 * C - 1) * PS + PS // 2

ZC = 2 * D + 2
NEG = -1e30


def vit_tower(nc, A, out):
    x_d, cls_d = A["x"], A["cls_tok"]

    with ExitStack() as ctx:
        def sb(name, shape, dt=F32):
            return ctx.enter_context(nc.sbuf_tensor(name, shape, dt))

        def sem(name):
            return ctx.enter_context(nc.semaphore(name))

        ps = ctx.enter_context(nc.psum_tensor("ps", [128, 8, 512], F32))

        ident = sb("ident", [128, 128])
        ones = sb("ones", [128, 128])
        same = sb("same", [GT, GI, POS])
        before = sb("before", [GT, GI, POS])
        same_sel = sb("same_sel", [GT, GI, TOPK])
        slot_no = sb("slot_no", [GT, GI, TOPK])
        head_mask = sb("head_mask", [DH2, HH, SEL])
        img_of_tok = sb("img_of_tok", [GI, GI, POS], BF16)
        img_of_sel = sb("img_of_sel", [GI, HH, GI, TOPK], BF16)
        other_img = sb("other_img", [GI, GI, POS], BF16)
        cls_rows = sb("cls_rows", [1, 2, GT])
        row_of = sb("row_of", [2, 2, GT])
        minus_half = sb("minus_half", [128, 4])
        counts = sb("counts", [XP, WIN], BF16)
        one_bf = sb("one_bf", [1, 1], BF16)
        px_ok = sb("px_ok", [128, 2])
        px_sel = sb("px_sel", [128, 2, 8])

        late = sb("late", [128, 5868])
        w_raw = late[:, 0:2 * SH * C * D].rearrange("p (a f d) -> p a f d", a=2, d=D)
        o_p = FC * sum(UR)
        gelu_t = [late[:, FC * sum(UR[:u]):FC * sum(UR[:u + 1])].rearrange("p (m t) -> p m t", m=FC) for u in range(UNITS)]
        proj = [late[0:GT, o_p + u * GROUPS * ZC:o_p + (u + 1) * GROUPS * ZC].rearrange("p (g n) -> p g n", g=GROUPS)
                for u in range(UNITS)]
        gb_raw = sb("gb_raw", [128, 2, 2, SH * C])
        w_eff = sb("w_eff", [128, CH, WCOL])
        rows1 = sb("rows1", [1, 2, D])
        norm_rows = sb("norm_rows", [2, D])
        colsum = sb("colsum", [GT, D])
        tok_bias = sb("tok_bias", [GT, D])
        w_attn = sb("w_attn", [DH2, 2, 3 * D])
        w_qT = sb("w_qT", [DH2, 2, D])
        w_kT = sb("w_kT", [DH2, 2, D])
        w_qk = sb("w_qk", [DH2, 2, D])
        gcol = sb("gcol", [DH2, 4, 2])
        wz = sb("wz", [DH2 + 1, 2, ZC + 2 * D])
        wz_b = sb("wz_b", [1, ZC + 2 * D])
        wo = sb("wo", [DH2 + 1, 2, D])
        w1 = sb("w1", [DH2 + 1, 2, F])
        w1_b = sb("w1_b", [1, F])
        w2 = sb("w2", [128, FC, D])
        w2_flat = w2[:].rearrange("p m d -> p (m d)")
        band = w2_flat[:, 0:BAND]
        band_left, band_right = [w2_flat[:, BAND + k * 256:BAND + (k + 1) * 256] for k in range(2)]
        row_sel = sb("row_sel", [128, 2, EROW + EDGE])
        col_sel = sb("col_sel", [128, 2, ECOL + EDGE])
        bm_all = sb("bm_all", [GT, D])
        bf2_all = sb("bf2_all", [GT, D])

        strips = sb("strips", [XP, C, ROWS, HW])
        wins = sb("wins", [XP, NP, WIN + 1])
        wcnt = sb("wcnt", [XP, WIN])
        winT = sb("winT", [128, CH, UNITS, UT])

        def per_unit(name, shape):
            return [sb(f"{name}{u}", shape) for u in range(UNITS)]

        mom = per_unit("mom", [GT, 6, GROUPS])
        bn = per_unit("bn", [GT, GROUPS, 6])
        mv = per_unit("mv", [GT, GROUPS, 2])
        sc = per_unit("sc", [GT, 16, GROUPS])
        h = per_unit("h", [GT, GROUPS, D])
        e = per_unit("e", [GT, GROUPS, D])
        hid = per_unit("hid", [GT, GROUPS, D])
        raw = per_unit("raw", [GT, GROUPS, WCOL])
        tmp = per_unit("tmp", [GT, GROUPS, D + 1])
        vs = tmp
        eT = per_unit("eT", [DH2 + 1, 2, UT])
        z2T = per_unit("z2T", [DH2 + 1, 2, UT])
        shareT = per_unit("shareT", [GT, 2, UT])
        uT = [shareT[u][0:DH2] for u in range(UNITS)]
        pick = per_unit("pick", [GT, GROUPS, USEL])
        pickT = per_unit("pickT", [USEL, UT])
        zselT = per_unit("zselT", [DH2 + 1, 2, USEL])
        qblk = per_unit("qblk", [DH2, 2, GROUPS, HS])
        probs = per_unit("probs", [GT, 2 * GROUPS, GT])
        pr = [probs[u][0:HS] for u in range(UNITS)]
        at = probs
        lsc = per_unit("lsc", [HS, 4, 2 * GROUPS])
        prT = [shareT[u][:, :, 0:GROUPS * HS] for u in range(UNITS)]
        ctm = [pr[u][0:DH2].rearrange("p x k -> p (x k)")[:, 0:2 * GROUPS * HS] for u in range(UNITS)]
        ctxT = per_unit("ctxT", [DH2 + 1, 2, USEL])
        ao = per_unit("ao", [USEL, D])
        base = per_unit("base", [GT, GROUPS, D])

        s = {n: sem(n) for n in (
            "d_tok0 d_tok1 d_tok2 d_tok3 d_tok4 d_gb d_attn d_small d_big x_in out_done "
            "c_pool c_dve strips_zero shifts_ready pads_zero consts_done counts_done bands_done biases_zero "
            "attn_mm attn_ev qk_mm qk_ev norms_mm gamma_done window_mm count_mm window_a window_d count_ev "
            "norm_rows_ready rows_mm rows_ev factors_done bias_mm weights_ready "
            "main_copied edge_copied cnt_ready cnt_used tr_a tr_d ev_a ev_d tok_mm m_mu m_sq m_var m_veps "
            "rp_ready m_nmr t1_done h_done bn1 bn1_agg v1_ready r1_ready raw_ev e_done eT_mm eT_a eT_d u_mm u_ev v_mm v_ev s_mm s_max "
            "s_nb at_exp at_sum o_mm h2_done bn2 bn2_agg v2_ready v2b_ready r2_ready z_done hid_done zT_mm zT_a zT_d p_mm p_ev "
            "k_mm k_ev sg_exp sg_add score rank_mm rk1 rk2 rk3 pick_done not_sel sy_done pool_mm al1 al2 al3 mix1 mix2 mix3 "
            "pT_ev zs_mm zs_ev q_mm qb_done l_mm l_max l_nb l_exp l_rcp pr_done prT_mm prT_a prT_d c_mm ctm_done "
            "ctx_done ao_mm ao_ev x_mm hh_done bn3 bn3_agg v3_ready r3_ready z2_done z2T_mm z2T_a z2T_d base1 base2 up_mm gelu_done dn_mm fin_done"
        ).split()}

        STORED = 16 * UNITS * GROUPS

        class Tile:

            def __init__(self, eng, i):
                self.eng, self.i, self.b = eng, i, i * PER

            def wait(self, name, n):
                self.eng.wait_ge(s[name], self.b + n)

            def group(self, name, u, g):
                self.wait(name, US * u + GS * (g + 1))

            def unit(self, name, u):
                self.wait(name, US * (u + 1))

            def number(self):
                return self.i if type(self.i) is int else None

            def before(self, name):
                if self.number() != 0:
                    self.wait(name, 0)

        def turns(eng, do):
            def run(i, order):
                for name, k in order:
                    if name in ("up", "down"):
                        tile = i - 1
                    elif name in ("last_up", "last_down"):
                        name, tile = name[5:], i
                    elif name in ("halo", "copy", "squares", "turn") or (name == "patch" and k < GROUPS):
                        tile = i + 1
                    else:
                        tile = i
                    if name in do:
                        do[name](Tile(eng, tile), k)

            run(-1, items(PROLOGUE))
            run(0, items(FIRST_TURN))
            with eng.Fori(1, ITERS - 1) as i:
                run(i, items(TURN))
            run(ITERS - 1, items(LAST_TURN))

        def bank(u, k):
            return ps[:, 3 * u + k, :]

        def spare(n):
            return ps[:, 6 + n % 2, :]

        def win_src(j, half):
            return spare(half)[0:CHUNK[j], 0:3 * XP].rearrange("p (w h b) -> p b h w", w=3, h=NP)

        def win_dst(j, half):
            v = winT[0:CHUNK[j], j].rearrange("p u t -> p (u t)")[:, 0:IB * POS].rearrange("p (b q) -> p b q", q=POS)[:, :, 1:]
            return v.rearrange("p b (h w) -> p b h w", w=NP)[:, :, :, 3 * half:3 * half + 3]

        def v_bank(u, g):
            return bank(u, 1)[0:GT, g * D:(g + 1) * D] if g < 2 else bank(u, 2)[0:GT, 0:D]

        def o_bank(u, g):
            return bank(u, 0)[0:GT, g * D:(g + 1) * D] if g < 2 else bank(u, 1)[0:GT, 0:D]

        def pool_bank(u, g, n=D + 1, o=0):
            return bank(u, 0)[0:GT, g * 256 + o:g * 256 + n] if g < 2 else bank(u, 1)[0:GT, o:n]

        def x_bank(u, g):
            return bank(u, 0)[0:GT, g * 256:g * 256 + D] if g < 2 else bank(u, 1)[0:GT, 0:D]

        ROW_PARTS = [(wz, 1, 0, ZC), (wz, 1, ZC, ZC + 2 * D), (w1, 3, 0, F // 2), (w1, 3, F // 2, F)]

        def real(u, g):
            return min(GT, UR[u] - GT * g)

        tok_rows = A["L0_tok_W"].rearrange("(a p f) d -> p a f d", a=2, f=SH * C)
        OFF = [0, 1, -1, PS, -PS]
        edges = [(0, 0, 3), (0, 1, 4), (1, 0, 1), (1, 1, 2)]
        attn_w = A["L0_attn_W"].rearrange("u (c p) n -> p (u c) n", c=2)
        out_rows = out.rearrange("b n d -> (b n) d")

        def chunked(name):
            return A[name].rearrange("(c p) n -> p c n", c=2)

        def row(name):
            return A[name].rearrange("(a n) -> a n", a=1)

        small = [
            (rows1[:, 0, :], cls_d.rearrange("a b d -> (a b) d")), (rows1[:, 1, :], row("L0_tok_b")),
            (wz[0:DH2, :, 0:D], chunked("L0_ffn_Wv")), (wz[0:DH2, :, D:2 * D], chunked("L0_ffn_Wm")),
            (wz[0:DH2, :, 2 * D + 1:ZC], A["L0_ffn_Wr"].rearrange("(c p n) -> p c n", c=2, n=1)),
            (wz[0:DH2, :, ZC:ZC + D], chunked("L0_ffn_Wk")), (wz[0:DH2, :, ZC + D:], chunked("L0_ffn_Wq")),
            (w1[0:DH2], chunked("L0_ffn_W1")), (w1_b[:], row("L0_ffn_bf1")),
            (wz_b[:, 0:D], row("L0_ffn_bv")), (wz_b[:, 2 * D + 1:ZC], A["L0_ffn_br"].rearrange("(a n) -> a n", a=1)),
            (wz_b[:, ZC:ZC + D], row("L0_ffn_bk")), (wz_b[:, ZC + D:], row("L0_ffn_bq")),
            (wo[0:DH2], chunked("L0_ffn_Wo")), (wo[DH2:, 0, :], row("L0_ffn_bo")),
            (bm_all[:], row("L0_ffn_bm").broadcast_to((GT, D))), (bf2_all[:], row("L0_ffn_bf2").broadcast_to((GT, D))),
        ] + [(gcol[:, k, :], A[n].rearrange("(c p) -> p c", c=2)) for k, n in
             enumerate(("L0_ffn_g1", "L0_ffn_b1", "L0_ffn_g2", "L0_ffn_b2"))]

        ctx.enter_context(nc.allow_non_contiguous_dma(reason="columns of per-feature factors, a few hundred words"))
        block = ctx.enter_context(nc.Block())

        @block.sync
        def _(sp):
            def load_images(i):
                for y in range(NP):
                    r0, r1 = max(0, PS * y - 1), min(HW, PS * y + PS + 1)
                    o = r0 - (PS * y - 1)
                    sp.dma_start(strips[IB * y:IB * (y + 1), :, o:o + r1 - r0, :],
                                 x_d[bass.ds(i * IB, IB), :, r0:r1, :]).then_inc(s["x_in"], 16)

            sp.dma_start(w_attn[:], attn_w).then_inc(s["d_attn"], 16)
            for j, n in enumerate(("L0_tok_ln_gamma", "L0_tok_ln_beta")):
                sp.dma_start(gb_raw[:, j], A[n].rearrange("(a p f) -> p a f", a=2, f=SH * C)).then_inc(s["d_gb"], 16)
            for k in range(SH):
                sp.dma_start(w_raw[:, :, C * k:C * (k + 1)], tok_rows[:, :, C * k:C * (k + 1)]).then_inc(s[f"d_tok{k}"], 16)
            sp.wait_ge(s["strips_zero"], 2)
            load_images(0)
            sp.wait_ge(s["biases_zero"], 1)
            for dst, src in small:
                sp.dma_start(dst, src).then_inc(s["d_small"], 16)
            sp.wait_ge(s["window_mm"], CH)
            sp.wait_ge(s["count_mm"], 1)
            sp.dma_start(w2[:], A["L0_ffn_W2"].rearrange("(c p) n -> p c n", p=128)).then_inc(s["d_big"], 16)

            with sp.Fori(0, ITERS - 1) as i:
                t = Tile(sp, i)
                t.wait("main_copied", PER)
                t.wait("edge_copied", PER)
                load_images(i + 1)
            with sp.Fori(0, ITERS) as i:
                t = Tile(sp, i)
                for u in range(UNITS):
                    for g in range(GROUPS):
                        t.group("fin_done", u, g)
                        sp.dma_start(out_rows[bass.ds(i * (IB * POS) + (u * UT + g * GT), real(u, g)), :],
                                     base[u][0:real(u, g), g, :]).then_inc(s["out_done"], 16)
            sp.wait_ge(s["out_done"], ITERS * STORED)

        @block.gpsimd
        def _(pool):
            g = nc.gpsimd
            done = [0]

            def step(ins):
                done[0] += 1
                ins.then_inc(s["c_pool"], 1)
                pool.wait_ge(s["c_pool"], done[0])

            def select(view, src, pattern, base, cm, op, fill=0.0):
                step(g.affine_select(out=view, in_=src, compare_op=op, fill=fill, base=base,
                                     pattern=pattern, channel_multiplier=cm))

            def blocks(view, step_, width, n, inner):
                step(g.memset(view, 1.0))
                select(view, view, [[-step_, n], *[[0, k] for k in inner]], 0, 1, ALU.is_ge)
                select(view, view, [[step_, n], *[[0, k] for k in inner]], width - 1, -1, ALU.is_ge)

            step(g.memset(ident[:], 0.0))
            select(ident[:], ident[:], [[-1, 128]], 0, 1, ALU.not_equal, 1.0)
            g.memset(strips[:, :, 0, :], 0.0).then_inc(s["strips_zero"], 1)
            g.memset(strips[:, :, ROWS - 1, :], 0.0).then_inc(s["strips_zero"], 1)
            step(g.memset(px_sel[:], 1.0))
            select(px_sel[:, 0, :], px_sel[:, 0, :], [[-PS, 8]], -(PS - 1), 1, ALU.not_equal)
            select(px_sel[:, 1, :], px_sel[:, 1, :], [[-PS, 8]], 0, 1, ALU.not_equal)
            step(g.memset(band, 0.0))
            select(band, band, [[-1, BAND]], DIAG, 1, ALU.not_equal, 1.0)
            step(g.memset(row_sel[:], 0.0))
            step(g.memset(col_sel[:], 0.0))
            for side in range(2):
                view = row_sel[:, side, EROW:EROW + PS]
                select(view, view, [[-1, PS]], -side * (128 - PS), 1, ALU.not_equal, 1.0)
                view = col_sel[:, side, ECOL:ECOL + PS // 2]
                select(view, view, [[-PS, PS // 2]], -side * (PS - 1), 1, ALU.not_equal, 1.0)
            g.memset(minus_half[:], -0.5).then_inc(s["shifts_ready"], 1)

            w5 = wins[:, :, MAIN:WIN].rearrange("p w (k a c x) -> p w k a c x", k=2, a=2, c=C)
            st5 = strips[:].rearrange("p c y (w x) -> p c y w x", x=PS)

            def halo(t, _):
                pool.wait_ge(s["x_in"], (t.i + 1) * (16 * NP))
                if t.number() == 0:
                    pool.wait_ge(s["pads_zero"], 4)
                t.before("tr_a")
                t.before("tr_d")
                for a in range(2):
                    src = st5[:, :, a * (ROWS - 1), :, :].rearrange("p c w x -> p w c x")
                    g.tensor_copy(w5[:, :, 0, a, :, :], src).then_inc(s["edge_copied"], PER // 4)
                for a in range(2):
                    x0 = PS - 1 if a == 0 else PS
                    src = strips[:, :, 1:PS + 1, x0:x0 + PS * (NP - 2) + 1:PS].rearrange("p c y w -> p w c y")
                    g.tensor_copy(w5[:, 1 - a:NP - a, 1, a, :, :], src).then_inc(s["edge_copied"], PER // 4)

            def rsqrt(t, u, src, dst, name, ready):
                t.unit(name, u)
                g.tensor_tensor(dst, src, minus_half[0:GT, 0:GROUPS], ALU.pow).then_inc(s[ready], US)

            def sums(t, u):
                rsqrt(t, u, mom[u][:, 3, :], mom[u][:, 4, :], "m_veps", "rp_ready")

            def token(t, u):
                rsqrt(t, u, sc[u][:, 0, :], sc[u][:, 1, :], "v1_ready", "r1_ready")

            def attend(t, u):
                t.unit("v2_ready", u)
                t.unit("v2b_ready", u)
                g.tensor_tensor(sc[u][:, 4:6, :], sc[u][:, 2:4, :],
                                minus_half[0:GT, 0:1].broadcast_to((GT, 2 * GROUPS)).rearrange("p (a g) -> p a g", a=2),
                                ALU.pow).then_inc(s["r2_ready"], US)

            def pool_(t, u):
                t.unit("mix1", u)
                g.tensor_tensor(tmp[u][:, :, 0:D], tmp[u][:, :, 0:D], proj[u][:, :, D:2 * D], ALU.add).then_inc(s["mix2"], US)

            def shares(t, u):
                t.unit("l_rcp", u)
                g.tensor_tensor(pr[u][:], pr[u][:], lsc[u][:, 3, :].rearrange("p (x a) -> p x a", a=1)
                                .broadcast_to((HS, 2 * GROUPS, GT)), ALU.mult).then_inc(s["pr_done"], US)

            def scatter(t, u):
                rsqrt(t, u, sc[u][:, 6, :], sc[u][:, 7, :], "v3_ready", "r3_ready")
                if t.number() != 0:
                    pool.wait_ge(s["out_done"], t.i * STORED)
                g.tensor_tensor(base[u][:], h[u][:], hid[u][:], ALU.add).then_inc(s["base1"], US)
                t.unit("base1", u)
                g.tensor_tensor(base[u][:], base[u][:], bf2_all[:].rearrange("p (a d) -> p a d", a=1)
                                .broadcast_to((GT, GROUPS, D)), ALU.add).then_inc(s["base2"], US)

            def constants(t, _):
                for u in range(UNITS):
                    step(g.memset(pick[u][:], 0.0))
                    if UR[u] < UT:
                        step(g.memset(shareT[u][:, :, UR[u]:], 0.0))
                    step(g.memset(eT[u][DH2:, 0, :], 1.0))
                    step(g.memset(z2T[u][DH2:, 0, :], 1.0))
                    step(g.memset(zselT[u][DH2:, 0, :], 1.0))
                    step(g.memset(ctxT[u][DH2:, 0, :], 1.0))
                blocks(same[:], POS, POS, GI, [POS])
                step(g.tensor_copy(before[:], same[:]))
                select(before[:], before[:], [[-POS, GI], [-1, POS]], 0, 1, ALU.is_gt)
                blocks(same_sel[:], POS, POS, GI, [TOPK])
                for j in range(TOPK):
                    step(g.memset(slot_no[:, :, j:j + 1], float(j)))
                blocks(head_mask[:], DH, DH, HH, [SEL])
                step(g.memset(img_of_tok[:], 0.0))
                select(img_of_tok[:], img_of_tok[:], [[-1, GI], [0, POS]], 0, 1, ALU.not_equal, 1.0)
                step(g.memset(other_img[:], NEG))
                select(other_img[:], other_img[:], [[-1, GI], [0, POS]], 0, 1, ALU.not_equal, 0.0)
                step(g.memset(img_of_sel[:], 0.0))
                select(img_of_sel[:], img_of_sel[:], [[0, HH], [-1, GI], [0, TOPK]], 0, 1, ALU.not_equal, 1.0)
                cr = cls_rows[:].rearrange("a k (i q) -> a k i q", i=GI)
                step(g.memset(cls_rows[:, 0, :], 0.0))
                step(g.memset(cr[:, 0, :, 0:1], 1.0))
                step(g.memset(cls_rows[:, 1, :], 1.0))
                step(g.memset(cr[:, 1, :, 0:1], 0.0))
                step(g.memset(row_of[:], 0.0))
                for k in range(2):
                    select(row_of[:, k, :], row_of[:, k, :], [[0, GT]], -k, 1, ALU.not_equal, 1.0)
                g.memset(row_of[:, 1, 0:GT:POS], 0.0).then_inc(s["consts_done"], 1)

            turns(pool, dict(attn=constants, halo=halo, sums=sums, token=token, attend=attend, pool=pool_,
                             shares=shares, scatter=scatter))

        @block.scalar
        def _(act):
            a_ = nc.scalar

            def copy(dst, src, name, n, scale=1.0):
                a_.activation(dst, src, ACT.Copy, scale=scale).then_inc(s[name], n)

            def copy_window(t, w):
                if w == 0:
                    act.wait_ge(s["x_in"], (t.i + 1) * (16 * NP))
                    t.before("tr_a")
                    t.before("tr_d")
                copy(wins[:, w, 0:MAIN].rearrange("p (c y x) -> p c y x", c=C, y=PS),
                     strips[:, :, 1:PS + 1, PS * w:PS * (w + 1)], "main_copied", GS)

            def squares(t, w):
                if w == 0:
                    t.wait("edge_copied", PER)
                t.wait("main_copied", GS * (w + 1))
                if w > 0:
                    t.wait("cnt_used", GS * w)
                else:
                    t.before("cnt_used")
                a_.activation(wcnt[:], wins[:, w, 0:WIN], ACT.Square).then_inc(s["cnt_ready"], GS)

            def window(t, j):
                if j == CH - 1:
                    act.wait_ge(s["window_mm"], CH)
                    copy(w_eff[0:EDGE, j - 1:j + 1, 0:D], ps[0:EDGE, j // 2, 0:2 * D].rearrange("p (c n) -> p c n", c=2), "window_a", 1)

            def turn(t, n):
                j, half = n // 2, n % 2
                t.wait("tr_d" if half else "tr_a", TS_ * (j + 1))
                if n == 0:
                    t.before("tok_mm")
                copy(win_dst(j, half), win_src(j, half), "ev_d" if half else "ev_a", TS_)

            def patch(t, n):
                u, g = divmod(n, GROUPS)
                t.group("tok_mm", u, g)
                if n == 0:
                    t.before("h_done")
                copy(raw[u][:, g, :], spare(n)[0:GT, 0:WCOL], "raw_ev", GS)

            def flip1(t, u):
                t.wait("eT_mm", US * u + US // 2)
                copy(eT[u][0:DH2, 0, :], bank(u, 0)[0:DH2, 0:UT], "eT_a", US)

            def uv(t, u):
                for m in range(2):
                    t.wait("u_mm", US * u + US // 2 * (m + 1))
                    copy(uT[u][:, m, 0:UR[u]], bank(u, 2 - 2 * m)[0:DH2, 0:UR[u]], "u_ev", US // 2)

            def score(t, u):
                t.unit("s_nb", u)
                for g in range(GROUPS):
                    a_.activation(at[u][:, g, :], bank(u, 0)[0:GT, g * GT:(g + 1) * GT], ACT.Exp, bias=sc[u][:, 9, g:g + 1],
                                  scale=D ** -0.5, accum_out=sc[u][:, 10, g:g + 1]).then_inc(s["at_exp"], GS)

            def weigh(t, u):
                t.unit("at_sum", u)
                for g in range(GROUPS):
                    t.group("v_mm", u, max(g, 1))
                    copy(vs[u][:, g, 0:D], v_bank(u, g), "v_ev", GS, sc[u][:, 11, g:g + 1])

            def flip2(t, u):
                t.wait("zT_mm", US * u + US // 2)
                copy(eT[u][0:DH2, 0, :], bank(u, 2)[0:DH2, 0:UT], "zT_a", US)

            def project(t, u):
                for g in range(GROUPS):
                    t.group("p_mm", u, g)
                    copy(proj[u][:, g, :], bank(u, g)[0:GT, 0:ZC], "p_ev", GS)
                t.unit("p_ev", u)
                a_.activation(sc[u][:, 12, :], proj[u][:, :, ZC - 1], ACT.Exp, scale=-1.0).then_inc(s["sg_exp"], US)
                for m in range(2):
                    t.wait("k_mm", US * u + US // 2 * (m + 1))
                    copy(uT[u][:, m, 0:UR[u]], bank(u, m)[0:DH2, 0:UR[u]], "k_ev", US // 2)

            def router(t, u):
                t.unit("score", u)
                for g in range(GROUPS):
                    copy(tmp[u][:, g, :], proj[u][:, g, D:2 * D + 1], "sy_done", GS, sc[u][:, 13, g:g + 1])

            def pick_(t, u):
                t.unit("zs_mm", u)
                copy(zselT[u][0:DH2], bank(u, 2)[0:DH2, 0:128].rearrange("p (c n) -> p c n", c=2)[:, :, 0:USEL], "zs_ev", US)
                copy(pickT[u][:], bank(u, 2)[0:USEL, 128:128 + UT], "pT_ev", US)

            def logits(t, u):
                t.unit("l_nb", u)
                for k in range(2 * GROUPS):
                    c, g = k // GROUPS, k % GROUPS
                    a_.activation(pr[u][:, k, :], bank(u, c)[0:HS, g * GT:(g + 1) * GT], ACT.Exp,
                                  bias=lsc[u][:, 1, k:k + 1], scale=DH ** -0.5,
                                  accum_out=lsc[u][:, 2, k:k + 1]).then_inc(s["l_exp"], US // 6)

            def flip3(t, u):
                t.wait("prT_mm", US * u + US // 2)
                copy(prT[u][:, 0, :], bank(u, 0)[0:GT, 0:GROUPS * HS], "prT_a", US)

            def out_(t, u):
                t.unit("ao_mm", u)
                copy(ao[u][:], bank(u, 2)[0:USEL, 0:D], "ao_ev", US)

            def flip4(t, u):
                t.wait("z2T_mm", US * u + US // 2)
                copy(z2T[u][0:DH2, 0, :], bank(u, 2)[0:DH2, 0:UT], "z2T_a", US)

            def up(t, k):
                u, m = divmod(k, FC)
                t.wait("up_mm", US * u + UP * (m + 1))
                if k == 0:
                    t.before("dn_mm")
                a_.activation(gelu_t[u][:, m, :], spare(m)[:, 0:UR[u]], ACT.Gelu).then_inc(s["gelu_done"], UP)

            def ready(t, _):
                act.wait_ge(s["weights_ready"], 2)

            turns(act, dict(
                window=window, ready=ready,
                copy=copy_window, squares=squares, turn=turn, patch=patch, up=up,
                flip1=flip1, uv=uv, score=score, weigh=weigh, flip2=flip2, project=project, router=router, pick=pick_,
                logits=logits, flip3=flip3, out=out_, flip4=flip4))


        @block.vector
        def _(dve):
            v = nc.vector
            done = [0]

            def step(ins):
                done[0] += 1
                ins.then_inc(s["c_dve"], 1)
                dve.wait_ge(s["c_dve"], done[0])

            v.memset(wins[:, 0, MAIN + EDGE:MAIN + EDGE + EDGE // 2], 0.0).then_inc(s["pads_zero"], 1)
            v.memset(wins[:, NP - 1, MAIN + EDGE + EDGE // 2:WIN], 0.0).then_inc(s["pads_zero"], 1)
            wt = winT[:].rearrange("p j u t -> p j (u t)")
            v.memset(wt[:, :, 0:IB * POS:POS], 0.0).then_inc(s["pads_zero"], 1)
            v.memset(wt[:, :, IB * POS:], 0.0).then_inc(s["pads_zero"], 1)
            step(v.memset(wz_b[:], 0.0))
            step(v.memset(wz_b[:, 2 * D:2 * D + 1], 1.0))
            v.memset(wz[0:DH2, :, 2 * D:2 * D + 1], 0.0).then_inc(s["biases_zero"], 1)
            cm = counts[:, 0:MAIN].rearrange("p (c y x) -> p c y x", c=C, y=PS)
            inner, sides = slice(1, PS - 1), slice(0, PS, PS - 1)
            for ys, xs, n in ((inner, inner, SH), (inner, sides, SH - 1), (sides, inner, SH - 1), (sides, sides, SH - 2)):
                v.memset(cm[:, :, ys, xs], float(n)).then_inc(s["counts_done"], 1)
            v.memset(counts[:, MAIN:], 1.0).then_inc(s["counts_done"], 1)
            v.memset(one_bf[:], 1.0).then_inc(s["counts_done"], 1)
            step(v.memset(ones[:], 1.0))
            step(v.memset(w_eff[:, 0:KW, D + 1:], 0.0))
            step(v.memset(w_eff[96:, CH - 1, :], 0.0))
            step(v.memset(w_eff[0:EDGE, KW:, D:D + 1], 1.0))
            step(v.memset(w_eff[0:EDGE, KW:, D + 1:], 0.0))
            step(v.memset(w_eff[EDGE:EDGE + 1, CH - 1, D + 1:], 1.0))
            def attn(t, _):
                for k, dst in ((0, w_qT), (1, w_kT)):
                    dve.wait_ge(s["attn_mm"], 1 + k)
                    v.tensor_copy(dst[:], ps[0:DH2, k, 0:2 * D].rearrange("p (c n) -> p c n", c=2)).then_inc(s["attn_ev"], 1)

            def qk(t, _):
                dve.wait_ge(s["qk_mm"], 1)
                v.tensor_copy(w_qk[:], ps[0:DH2, 2, 0:2 * D].rearrange("p (c n) -> p c n", c=2)).then_inc(s["qk_ev"], 1)

            def bands(t, _):
                dve.wait_ge(s["shifts_ready"], 1)
                step(v.tensor_reduce(px_ok[:, 0:1], px_sel[:, 0, :], AX_X, ALU.min))
                step(v.tensor_reduce(px_ok[:, 1:2], px_sel[:, 1, :], AX_X, ALU.min))
                v.tensor_scalar(band_left, band[:, DIAG + 1 - 128:DIAG + 1 + 128], px_ok[:, 1:2], None, ALU.mult)\
                    .then_inc(s["bands_done"], 1)
                v.tensor_scalar(band_right, band[:, DIAG - 1:DIAG - 1 + 256], px_ok[:, 0:1], None, ALU.mult)\
                    .then_inc(s["bands_done"], 1)

            def shift(t, k):
                dve.wait_ge(s["norms_mm"], k + 1)
                view = w_raw[:, :, C * k:C * (k + 1)]
                gam = gb_raw[:, 0, :, C * k:C * (k + 1)].rearrange("p a (f n) -> p a f n", n=1).broadcast_to((128, 2, C, D))
                v.tensor_tensor(view, view, gam, ALU.mult).then_inc(s["gamma_done"], 1)

            def window(t, j):
                if j < KW and j % 2 == 1:
                    dve.wait_ge(s["window_mm"], j + 1)
                    v.tensor_tensor(w_eff[:, j - 1:j + 1, 0:D], ps[:, j // 2, 0:2 * D].rearrange("p (c n) -> p c n", c=2),
                                    w_raw[:, :, j // 2, :], ALU.add)\
                        .then_inc(s["window_d"], 1)
                if j == 0:
                    dve.wait_ge(s["count_mm"], 1)
                    v.tensor_copy(w_eff[:, 0:KW, D].rearrange("p (c a) -> p c a", c=C),
                                  ps[:, 4, 0:2].rearrange("p (b a) -> p b a", b=1).broadcast_to((128, C, 2))).then_inc(s["count_ev"], 1)

            def norm_row(t, _):
                dve.wait_ge(s["norms_mm"], SH)
                v.tensor_copy(norm_rows[:], ps[0:2, 5, 0:D]).then_inc(s["norm_rows_ready"], 1)

            def rows(t, n):
                dve.wait_ge(s["rows_mm"], n + 1)
                dst, _, lo, hi = ROW_PARTS[n]
                bias_row = (wz_b, w1_b)[n // 2]
                v.tensor_tensor(dst[DH2:, 0, lo:hi], spare(n)[0:1, 0:hi - lo], bias_row[:, lo:hi], ALU.add).then_inc(s["rows_ev"], 1)
                if n == len(ROW_PARTS) - 1:
                    for c in range(2):
                        v.tensor_scalar(wz[0:DH2, c, :], wz[0:DH2, c, :], gcol[:, 0, c:c + 1], None, ALU.mult)\
                            .then_inc(s["factors_done"], 1)
                        v.tensor_scalar(w1[0:DH2, c, :], w1[0:DH2, c, :], gcol[:, 2, c:c + 1], None, ALU.mult)\
                            .then_inc(s["factors_done"], 1)

            def bias(t, _):
                dve.wait_ge(s["bias_mm"], 1)
                v.tensor_copy(colsum[:], ps[0:GT, 4, 0:D]).then_inc(s["weights_ready"], 1)
                dve.wait_ge(s["bias_mm"], 2)
                v.tensor_copy(tok_bias[:], ps[0:GT, 5, 0:D]).then_inc(s["weights_ready"], 1)

            def ready(t, _):
                dve.wait_ge(s["weights_ready"], 2)
                dve.wait_ge(s["consts_done"], 1)

            def squares(t, w):
                t.wait("cnt_ready", GS * (w + 1))
                if t.number() == 0 and w == 0:
                    dve.wait_ge(s["counts_done"], 5)
                v.tensor_tensor_reduce(wcnt[:], wcnt[:], counts[:], 1.0, 0.0, ALU.mult, ALU.add,
                                       wins[:, w, WIN:WIN + 1]).then_inc(s["cnt_used"], GS)

            def sums(t, u):
                m = mom[u]
                t.unit("raw_ev", u)
                v.tensor_scalar(m[:, 0, :], raw[u][:, :, D], 1.0 / FEAT, None, ALU.mult).then_inc(s["m_mu"], US)
                t.unit("m_mu", u)
                v.tensor_tensor(m[:, 1, :], m[:, 0, :], m[:, 0, :], ALU.mult).then_inc(s["m_sq"], US)
                t.unit("m_sq", u)
                v.scalar_tensor_tensor(out=m[:, 2, :], in0=raw[u][:, :, D + 1], scalar=1.0 / FEAT, in1=m[:, 1, :],
                                       op0=ALU.mult, op1=ALU.subtract).then_inc(s["m_var"], US)
                t.unit("m_var", u)
                v.tensor_scalar(m[:, 3, :], m[:, 2, :], 0.0, EPS, ALU.max, ALU.add).then_inc(s["m_veps"], US)

            def stats(t, u, src, written, name, agg, outs):
                for g in range(GROUPS):
                    t.group(written, u, g)
                    v.bn_stats(bn[u][:, g, :], src[u][:, g, :]).then_inc(s[name], GS)
                t.unit(name, u)
                v.tensor_copy(mom[u][:, 1, :], bn[u][:, :, 0]).then_inc(s[agg], US // 4)
                for g in range(GROUPS):
                    v.bn_aggr(mv[u][:, g, :], bn[u][:, g, :]).then_inc(s[agg], US // 4)
                for ready, dst, fac, add in outs:
                    t.unit(agg, u)
                    v.tensor_scalar(sc[u][:, dst, :], mv[u][:, :, 1], fac, add, ALU.mult, ALU.add).then_inc(s[ready], US)

            def normalise(u, src, r, name):
                for g in range(GROUPS):
                    v.tensor_scalar(e[u][:, g, :], src[u][:, g, :], mv[u][:, g, 0:1], sc[u][:, r, g:g + 1],
                                    ALU.subtract, ALU.mult).then_inc(s[name], GS)

            def token(t, u):
                m = mom[u]
                t.unit("rp_ready", u)
                v.scalar_tensor_tensor(out=m[:, 5, :], in0=m[:, 0, :], scalar=-1.0, in1=m[:, 4, :],
                                       op0=ALU.mult, op1=ALU.mult).then_inc(s["m_nmr"], US)
                t.unit("m_nmr", u)
                t.before("base1")
                for g in range(GROUPS):
                    v.scalar_tensor_tensor(out=tmp[u][:, g, 0:D], in0=colsum[:], scalar=m[:, 5, g:g + 1], in1=tok_bias[:],
                                           op0=ALU.mult, op1=ALU.add).then_inc(s["t1_done"], GS)
                for g in range(GROUPS):
                    t.group("t1_done", u, g)
                    v.scalar_tensor_tensor(out=h[u][:, g, :], in0=raw[u][:, g, 0:D], scalar=m[:, 4, g:g + 1],
                                           in1=tmp[u][:, g, 0:D], op0=ALU.mult, op1=ALU.add).then_inc(s["h_done"], GS)
                stats(t, u, h, "h_done", "bn1", "bn1_agg", [("v1_ready", 0, 1.0, EPS)])

            def norm1(t, u):
                t.unit("r1_ready", u)
                normalise(u, h, 1, "e_done")

            def flip1(t, u):
                t.unit("eT_mm", u)
                v.tensor_copy(eT[u][0:DH2, 1, :], bank(u, 1)[0:DH2, 0:UT]).then_inc(s["eT_d"], US)

            def score(t, u):
                t.unit("s_mm", u)
                v.tensor_reduce(sc[u][:, 8, :], bank(u, 0)[0:GT, 0:UT].rearrange("p (g q) -> p g q", g=GROUPS), AX_X,
                                ALU.max).then_inc(s["s_max"], US)
                t.unit("s_max", u)
                v.tensor_scalar(sc[u][:, 9, :], sc[u][:, 8, :], -(D ** -0.5), None, ALU.mult).then_inc(s["s_nb"], US)

            def weigh(t, u):
                t.unit("at_exp", u)
                v.reciprocal(sc[u][:, 11, :], sc[u][:, 10, :]).then_inc(s["at_sum"], US)

            def attend(t, u):
                for g in range(GROUPS):
                    t.group("o_mm", u, max(g, 1))
                    v.tensor_tensor(h[u][:, g, :], h[u][:, g, :], o_bank(u, g), ALU.add).then_inc(s["h2_done"], GS)
                stats(t, u, h, "h2_done", "bn2", "bn2_agg",
                      [("v2_ready", 2, 1.0, EPS), ("v2b_ready", 3, 1.0 + EPS, EPS * EPS)])

            def norm2(t, u):
                t.unit("r2_ready", u)
                normalise(u, h, 5, "z_done")

            def flip2(t, u):
                t.unit("zT_mm", u)
                v.tensor_copy(eT[u][0:DH2, 1, :], bank(u, 1)[0:DH2, 0:UT]).then_inc(s["zT_d"], US)
                for g in range(GROUPS):
                    v.tensor_scalar(hid[u][:, g, :], h[u][:, g, :], mv[u][:, g, 0:1], sc[u][:, 4, g:g + 1],
                                    ALU.subtract, ALU.mult).then_inc(s["hid_done"], GS)

            def router(t, u):
                q = sc[u]
                t.unit("sg_exp", u)
                v.tensor_scalar(q[:, 14, :], q[:, 12, :], 1.0, None, ALU.add).then_inc(s["sg_add"], US)
                t.unit("sg_add", u)
                v.reciprocal(q[:, 13, :], q[:, 14, :]).then_inc(s["score"], US)

            def rank(t, u):
                m = mom[u]
                for g in range(GROUPS):
                    others = bank(u, 2)[0:GT, g * GT:(g + 1) * GT]
                    t.unit("rank_mm", u)
                    v.scalar_tensor_tensor(out=at[u][:, g, :], in0=others, scalar=sc[u][:, 13, g:g + 1],
                                           in1=same[:].rearrange("p i q -> p (i q)"), op0=ALU.is_lt, op1=ALU.mult,
                                           accum_out=m[:, 0, g:g + 1]).then_inc(s["rk1"], GS)
                    v.scalar_tensor_tensor(out=at[u][:, GROUPS + g, :], in0=others, scalar=sc[u][:, 13, g:g + 1],
                                           in1=before[:].rearrange("p i q -> p (i q)"), op0=ALU.is_equal, op1=ALU.mult,
                                           accum_out=m[:, 1, g:g + 1]).then_inc(s["rk2"], GS)
                t.unit("rk1", u)
                t.unit("rk2", u)
                v.tensor_tensor(m[:, 2, :], m[:, 0, :], m[:, 1, :], ALU.add).then_inc(s["rk3"], US)
                t.unit("rk3", u)
                for g in range(GROUPS):
                    v.scalar_tensor_tensor(out=pick[u][:, g, g * SEL:(g + 1) * SEL], in0=slot_no[:].rearrange("p i j -> p (i j)"),
                                           scalar=m[:, 2, g:g + 1], in1=same_sel[:].rearrange("p i j -> p (i j)"),
                                           op0=ALU.is_equal, op1=ALU.mult).then_inc(s["pick_done"], GS)
                v.tensor_scalar(m[:, 5, :], m[:, 2, :], float(TOPK), None, ALU.is_ge).then_inc(s["not_sel"], US)

            def pool_(t, u):
                q = sc[u]
                t.unit("pool_mm", u)
                v.tensor_scalar(q[:, 14, 0:2], bank(u, 0)[0:GT, D:D + 257:256], 1e-6, None, ALU.add).then_inc(s["al1"], US // 2)
                v.tensor_scalar(q[:, 14, 2:3], pool_bank(u, 2, D + 1, D), 1e-6, None, ALU.add).then_inc(s["al1"], US // 2)
                t.unit("al1", u)
                v.reciprocal(q[:, 15, :], q[:, 14, :]).then_inc(s["al2"], US)
                t.unit("al2", u)
                v.tensor_tensor(q[:, 8, :], q[:, 15, :], q[:, 13, :], ALU.mult).then_inc(s["al3"], US)
                t.unit("al3", u)
                for g in range(GROUPS):
                    v.scalar_tensor_tensor(out=tmp[u][:, g, 0:D], in0=pool_bank(u, g, D), scalar=q[:, 8, g:g + 1], in1=bm_all[:],
                                           op0=ALU.mult, op1=ALU.add).then_inc(s["mix1"], GS)

            def query(t, u):
                t.unit("q_mm", u)
                for c in range(2):
                    src = bank(u, 2)[0:DH2, 64 * c:64 * c + USEL].rearrange("p (g a j) -> p g a j", g=GROUPS, a=1)
                    v.tensor_tensor(qblk[u][:, c].rearrange("p g (h j) -> p g h j", h=HH),
                                    src.broadcast_to((DH2, GROUPS, HH, SEL)),
                                    head_mask[:].rearrange("p (a h) j -> p a h j", a=1).broadcast_to((DH2, GROUPS, HH, SEL)),
                                    ALU.mult).then_inc(s["qb_done"], US // 2)

            def logits(t, u):
                q = lsc[u]
                t.unit("l_mm", u)
                v.tensor_reduce(q[:, 0, :].rearrange("p (c g) -> p c g", c=2),
                                ps[0:HS, 3 * u:3 * u + 2, 0:UT].rearrange("p c (g k) -> p c g k", g=GROUPS),
                                AX_X, ALU.max).then_inc(s["l_max"], US)
                t.unit("l_max", u)
                v.tensor_scalar(q[:, 1, :], q[:, 0, :], -(DH ** -0.5), None, ALU.mult).then_inc(s["l_nb"], US)

            def shares(t, u):
                t.unit("l_exp", u)
                v.reciprocal(lsc[u][:, 3, :], lsc[u][:, 2, :]).then_inc(s["l_rcp"], US)
                t.unit("mix2", u)
                t.unit("not_sel", u)
                t.unit("hid_done", u)
                for g in range(GROUPS):
                    v.scalar_tensor_tensor(out=hid[u][:, g, :], in0=tmp[u][:, g, 0:D], scalar=mom[u][:, 5, g:g + 1],
                                           in1=hid[u][:, g, :], op0=ALU.mult, op1=ALU.add).then_inc(s["mix3"], GS)

            def flip3(t, u):
                t.unit("prT_mm", u)
                v.tensor_copy(prT[u][:, 1, :], bank(u, 1)[0:GT, 0:GROUPS * HS]).then_inc(s["prT_d"], US)

            def context(t, u):
                t.unit("c_mm", u)
                v.tensor_tensor(ctm[u].rearrange("p (c g n) -> p c g n", c=2, g=GROUPS),
                                ps[0:DH2, 3 * u:3 * u + 2, 0:GROUPS * HS].rearrange("p c (g n) -> p c g n", g=GROUPS),
                                head_mask[:].rearrange("p (a b h) j -> p a b (h j)", a=1, b=1)
                                .broadcast_to((DH2, 2, GROUPS, HS)), ALU.mult).then_inc(s["ctm_done"], US)
                t.unit("ctm_done", u)
                v.tensor_reduce(ctxT[u][0:DH2].rearrange("p c (g j) -> p (c g) j", g=GROUPS),
                                ctm[u].rearrange("p (x h j) -> p x j h", h=HH, j=SEL), AX_X, ALU.add).then_inc(s["ctx_done"], US)

            def scatter(t, u):
                for g in range(GROUPS):
                    t.group("x_mm", u, max(g, 1))
                    t.group("mix3", u, g)
                    v.tensor_tensor(hid[u][:, g, :], hid[u][:, g, :], x_bank(u, g), ALU.add).then_inc(s["hh_done"], GS)
                stats(t, u, hid, "hh_done", "bn3", "bn3_agg", [("v3_ready", 6, 1.0, EPS)])

            def norm3(t, u):
                t.unit("r3_ready", u)
                normalise(u, hid, 7, "z2_done")

            def flip4(t, u):
                t.unit("z2T_mm", u)
                v.tensor_copy(z2T[u][0:DH2, 1, :], bank(u, 1)[0:DH2, 0:UT]).then_inc(s["z2T_d"], US)

            def down(t, k):
                u, g = divmod(k, GROUPS)
                n = real(u, g)
                t.group("dn_mm", u, g)
                t.unit("base2", u)
                v.tensor_tensor(base[u][0:n, g, :], spare(k)[0:n, 0:D], base[u][0:n, g, :], ALU.add).then_inc(s["fin_done"], GS)

            turns(dve, dict(
                attn=attn, qk=qk, bands=bands, shift=shift, norm_row=norm_row, window=window, rows=rows, bias=bias, ready=ready,
                squares=squares, down=down,
                sums=sums, token=token, norm1=norm1, flip1=flip1, score=score, weigh=weigh, attend=attend, norm2=norm2,
                flip2=flip2, router=router, rank=rank, pool=pool_, query=query, logits=logits, shares=shares,
                flip3=flip3, context=context, scatter=scatter, norm3=norm3, flip4=flip4))


        @block.tensor
        def _(pe):
            t = nc.tensor

            def attn(tile, _):
                pe.wait_ge(s["c_pool"], 2)
                pe.wait_ge(s["d_attn"], 16)
                for k in range(2):
                    for c in range(2):
                        for m in range(2):
                            last = t.transpose(ps[0:DH2, k, m * D + c * DH2:m * D + (c + 1) * DH2],
                                               w_attn[:, c, k * D + m * DH2:k * D + (m + 1) * DH2], ident[0:DH2, 0:DH2])
                    last.then_inc(s["attn_mm"], 1)

            def qk(tile, _):
                pe.wait_ge(s["attn_ev"], 2)
                for m in range(2):
                    for c in range(2):
                        last = t.matmul(ps[0:DH2, 2, m * D:(m + 1) * D], w_qT[:, c, m * DH2:(m + 1) * DH2], w_kT[:, c, :],
                                        start=(c == 0), stop=(c == 1))
                last.then_inc(s["qk_mm"], 1)

            def shift(tile, k):
                if k == 0:
                    pe.wait_ge(s["d_gb"], 32)
                pe.wait_ge(s[f"d_tok{k}"], 16)
                for f in range(C * k, C * (k + 1)):
                    for a in range(2):
                        last = t.matmul(ps[0:2, 5, 0:D], gb_raw[:, :, a, f], w_raw[:, a, f, :],
                                        start=(f == 0 and a == 0), stop=(f == SH * C - 1 and a == 1))
                last.then_inc(s["norms_mm"], 1)

            def moves(k, a):
                for half in range(2):
                    by = OFF[k] + 128 * (a - half)
                    if abs(by) >= 128:
                        continue
                    if k == 1:
                        yield half, band_left[:, by - 1 + 128:by - 1 + 256]
                    elif k == 2:
                        yield half, band_right[:, by + 1:by + 1 + 128]
                    else:
                        yield half, band[:, DIAG + by:DIAG + by + 128]

            def window(tile, j):
                if j == 0:
                    pe.wait_ge(s["gamma_done"], SH)
                    pe.wait_ge(s["bands_done"], 2)
                    pe.wait_ge(s["shifts_ready"], 1)
                    pe.wait_ge(s["qk_ev"], 1)
                    pe.wait_ge(s["counts_done"], 6)
                    for a in range(2):
                        last = t.matmul(ps[:, 4, a:a + 1], counts[0:1, 128 * a:128 * (a + 1)], one_bf[:], start=True, stop=True)
                    last.then_inc(s["count_mm"], 1)
                o = ps[:, j // 2, (j % 2) * D:(j % 2 + 1) * D]
                if j < KW:
                    c, a = divmod(j, 2)
                    terms = [(m, w_raw[:, half, C * k + c, :]) for k in range(1, SH) for half, m in moves(k, a)]
                else:
                    o = o[0:EDGE]
                    terms = []
                    for q, side, k in edges:
                        if q != j - KW:
                            continue
                        for c in range(C):
                            at_ = side * (EDGE // 2) + c * PS
                            if q == 1:
                                for half in range(2):
                                    lo = ECOL - at_ - half * (PS // 2)
                                    terms.append((col_sel[:, side, lo:lo + EDGE], w_raw[:, half, C * k + c, :]))
                            else:
                                lo = EROW - at_
                                terms.append((row_sel[:, side, lo:lo + EDGE], w_raw[:, side, C * k + c, :]))
                for n, (m, w) in enumerate(terms):
                    last = t.matmul(o, m, w, start=(n == 0), stop=(n == len(terms) - 1))
                last.then_inc(s["window_mm"], 1)

            def rows(tile, n):
                if n == 0:
                    pe.wait_ge(s["d_small"], 16 * len(small))
                if n < 2:
                    pe.wait_ge(s["raw_ev"], PER - GS * (1 - n))
                else:
                    pe.wait_ge(s["rows_ev"], n - 1)
                src, k, lo, hi = ROW_PARTS[n]
                for c in range(2):
                    last = t.matmul(spare(n)[0:1, 0:hi - lo], gcol[:, k, c:c + 1], src[0:DH2, c, lo:hi], start=(c == 0), stop=(c == 1))
                last.then_inc(s["rows_mm"], 1)

            def factors(tile, _):
                pe.wait_ge(s["rows_ev"], len(ROW_PARTS))
                pe.wait_ge(s["factors_done"], 4)

            def bias(tile, _):
                pe.wait_ge(s["norm_rows_ready"], 1)
                pe.wait_ge(s["consts_done"], 1)
                pe.wait_ge(s["count_ev"], 1)
                pe.wait_ge(s["d_small"], 16 * len(small))
                t.matmul(ps[0:GT, 4, 0:D], row_of[:, 0, :], norm_rows[:], start=True, stop=True).then_inc(s["bias_mm"], 1)
                t.matmul(ps[0:GT, 5, 0:D], row_of[:, 1, :], norm_rows[:], start=True, stop=False)
                for j in range(2):
                    last = t.matmul(ps[0:GT, 5, 0:D], cls_rows[:, j, :], rows1[:, j, :], start=False, stop=(j == 1))
                last.then_inc(s["bias_mm"], 1)

            def ready(tile, _):
                pe.wait_ge(s["weights_ready"], 2)
                pe.wait_ge(s["d_big"], 16)

            def to_columns(tile, u, src, done, name, banks):
                for c in range(2):
                    for g in range(GROUPS):
                        if c == 0:
                            tile.group(done, u, g)
                        last = t.transpose(bank(u, banks[c])[0:DH2, g * GT:(g + 1) * GT],
                                           src[u][:, g, c * DH2:(c + 1) * DH2], ident[0:GT, 0:GT])
                    last.then_inc(s[name], US // 2)

            def turn(tile, n):
                j, half = n // 2, n % 2
                if n == 0:
                    tile.wait("main_copied", PER)
                    tile.wait("edge_copied", PER)
                if j == CH - 1:
                    tile.wait("cnt_used", PER)
                if j > 0:
                    tile.wait("ev_d" if half else "ev_a", TS_ * j)
                elif tile.number() == 1:
                    pe.wait_ge(s["rows_ev"], len(ROW_PARTS) - 1 + half)
                elif tile.number() != 0:
                    pe.wait_ge(s["gelu_done"], tile.b - PER + half * UP - UP)
                for w in range(3):
                    last = t.transpose(spare(half)[0:CHUNK[j], w * XP:(w + 1) * XP],
                                       wins[:, 3 * half + w, sum(CHUNK[:j]):sum(CHUNK[:j + 1])], ident[0:XP, 0:XP])
                last.then_inc(s["tr_d" if half else "tr_a"], TS_)

            def patch(tile, n):
                u, g = divmod(n, GROUPS)
                if n == 0:
                    tile.wait("ev_a", PER)
                    tile.wait("ev_d", PER)
                if tile.number() == 0 and n == 0:
                    pe.wait_ge(s["pads_zero"], 4)
                    pe.wait_ge(s["window_a"], 1)
                    pe.wait_ge(s["window_d"], C)
                    pe.wait_ge(s["count_ev"], 1)
                if n >= 2:
                    tile.wait("raw_ev", GS * (n - 1))
                elif tile.number() not in (0, 1):
                    pe.wait_ge(s["fin_done"], tile.b - PER + n * GS - GS)
                for j in range(CH):
                    last = t.matmul(spare(n)[0:GT, 0:WCOL], winT[0:CHUNK[j], j, u, g * GT:(g + 1) * GT],
                                    w_eff[0:CHUNK[j], j, :], start=(j == 0), stop=(j == CH - 1))
                last.then_inc(s["tok_mm"], GS)

            def flip1(tile, u):
                to_columns(tile, u, e, "e_done", "eT_mm", (0, 1))

            def uv(tile, u):
                tile.unit("eT_a", u)
                tile.unit("eT_d", u)
                for m in range(2):
                    for c in range(2):
                        last = t.matmul(bank(u, 2 - 2 * m)[0:DH2, 0:UR[u]], w_qk[:, c, m * DH2:(m + 1) * DH2], eT[u][0:DH2, c, 0:UR[u]],
                                        start=(c == 0), stop=(c == 1))
                    last.then_inc(s["u_mm"], US // 2)
                for g in range(GROUPS - 1):
                    value(tile, u, g)

            def value(tile, u, g):
                for c in range(2):
                    last = t.matmul(v_bank(u, g), eT[u][0:DH2, c, g * GT:(g + 1) * GT], w_attn[:, c, 2 * D:3 * D],
                                    start=(c == 0), stop=(c == 1))
                last.then_inc(s["v_mm"], GS)

            def score(tile, u):
                tile.unit("u_ev", u)
                for g in range(GROUPS):
                    o = bank(u, 0)[0:GT, g * GT:(g + 1) * GT]
                    cols = slice(g * GT, (g + 1) * GT)
                    t.matmul(o, img_of_tok[:].rearrange("p i q -> p (i q)"), other_img[:].rearrange("p i q -> p (i q)"),
                             start=True, stop=False)
                    for c in range(2):
                        last = t.matmul(o, eT[u][0:DH2, c, cols], uT[u][:, c, cols], start=False, stop=(c == 1))
                last.then_inc(s["s_mm"], US)
                value(tile, u, GROUPS - 1)

            def attend(tile, u):
                for g in range(GROUPS):
                    tile.group("v_ev", u, g)
                    t.matmul(o_bank(u, g), at[u][:, g, :], vs[u][:, g, 0:D], start=True, stop=True).then_inc(s["o_mm"], GS)

            def flip2(tile, u):
                to_columns(tile, u, e, "z_done", "zT_mm", (2, 1))

            def project(tile, u):
                tile.unit("zT_a", u)
                tile.unit("zT_d", u)
                for g in range(GROUPS):
                    o = bank(u, g)[0:GT, 0:ZC]
                    t.matmul(o, eT[u][0:DH2 + 1, 0, g * GT:(g + 1) * GT], wz[:, 0, 0:ZC], start=True, stop=False)
                    t.matmul(o, eT[u][0:DH2, 1, g * GT:(g + 1) * GT], wz[0:DH2, 1, 0:ZC], start=False, stop=True)\
                        .then_inc(s["p_mm"], GS)
                for m in range(2):
                    o = bank(u, m)[0:DH2, 0:UR[u]]
                    tile.group("p_ev", u, m)
                    cols = slice(ZC + m * DH2, ZC + (m + 1) * DH2)
                    t.matmul(o, wz[:, 0, cols], eT[u][:, 0, 0:UR[u]], start=True, stop=False)
                    t.matmul(o, wz[0:DH2, 1, cols], eT[u][0:DH2, 1, 0:UR[u]], start=False, stop=True).then_inc(s["k_mm"], US // 2)

            def rank(tile, u):
                tile.unit("score", u)
                tile.unit("p_ev", u)
                for g in range(GROUPS):
                    last = t.transpose(bank(u, 2)[0:GT, g * GT:(g + 1) * GT], sc[u][:, 13, g:g + 1].broadcast_to((GT, GT)),
                                       ident[0:GT, 0:GT])
                last.then_inc(s["rank_mm"], US)

            def pool_(tile, u):
                tile.unit("k_ev", u)
                for g in range(GROUPS):
                    tile.group("sy_done", u, g)
                    last = t.matmul(pool_bank(u, g), same[:].rearrange("p i q -> p (i q)"), tmp[u][:, g, :], start=True, stop=True)
                last.then_inc(s["pool_mm"], US)

            def pick_(tile, u):
                for c in range(2):
                    for g in range(GROUPS):
                        if c == 0:
                            tile.group("pick_done", u, g)
                        last = t.matmul(bank(u, 2)[0:DH2, 64 * c + g * SEL:64 * c + (g + 1) * SEL],
                                        e[u][:, g, c * DH2:(c + 1) * DH2], pick[u][:, g, g * SEL:(g + 1) * SEL],
                                        start=True, stop=True)
                for g in range(GROUPS):
                    last = t.transpose(bank(u, 2)[0:USEL, 128 + g * GT:128 + (g + 1) * GT], pick[u][:, g, :], ident[0:GT, 0:GT])
                last.then_inc(s["zs_mm"], US)

            def query(tile, u):
                tile.unit("zs_ev", u)
                tile.unit("pT_ev", u)
                for m in range(2):
                    o = bank(u, 2)[0:DH2, 64 * m:64 * m + USEL]
                    cols = slice(ZC + D + m * DH2, ZC + D + (m + 1) * DH2)
                    t.matmul(o, wz[:, 0, cols], zselT[u][:, 0, :], start=True, stop=False)
                    last = t.matmul(o, wz[0:DH2, 1, cols], zselT[u][0:DH2, 1, :], start=False, stop=True)
                last.then_inc(s["q_mm"], US)

            def logits(tile, u):
                tile.unit("qb_done", u)
                for c in range(2):
                    for g in range(GROUPS):
                        o = bank(u, c)[0:HS, g * GT:(g + 1) * GT]
                        t.matmul(o, img_of_sel[:].rearrange("p h i j -> p (h i j)"), other_img[:].rearrange("p i q -> p (i q)"),
                                 start=True, stop=False)
                        last = t.matmul(o, qblk[u][:, c, g, :], uT[u][:, c, g * GT:(g + 1) * GT], start=False, stop=True)
                last.then_inc(s["l_mm"], US)

            def flip3(tile, u):
                tile.unit("pr_done", u)
                for c in range(2):
                    for g in range(GROUPS):
                        last = t.transpose(bank(u, c)[0:GT, g * HS:(g + 1) * HS], pr[u][:, c * GROUPS + g, :],
                                           ident[0:HS, 0:HS])
                    last.then_inc(s["prT_mm"], US // 2)

            def context(tile, u):
                tile.unit("prT_a", u)
                tile.unit("prT_d", u)
                for c in range(2):
                    for g in range(GROUPS):
                        last = t.matmul(bank(u, c)[0:DH2, g * HS:(g + 1) * HS], proj[u][:, g, c * DH2:(c + 1) * DH2],
                                        prT[u][:, c, g * HS:(g + 1) * HS], start=True, stop=True)
                last.then_inc(s["c_mm"], US)

            def out_(tile, u):
                tile.unit("ctx_done", u)
                t.matmul(bank(u, 2)[0:USEL, 0:D], ctxT[u][:, 0, :], wo[:, 0, :], start=True, stop=False)
                t.matmul(bank(u, 2)[0:USEL, 0:D], ctxT[u][0:DH2, 1, :], wo[0:DH2, 1, :], start=False, stop=True)\
                    .then_inc(s["ao_mm"], US)

            def scatter(tile, u):
                tile.unit("ao_ev", u)
                for g in range(GROUPS):
                    t.matmul(x_bank(u, g), pickT[u][:, g * GT:(g + 1) * GT], ao[u][:], start=True, stop=True)\
                        .then_inc(s["x_mm"], GS)

            def flip4(tile, u):
                to_columns(tile, u, e, "z2_done", "z2T_mm", (2, 1))

            def up(tile, k):
                u, m = divmod(k, FC)
                if m == 0:
                    tile.unit("z2T_a", u)
                    tile.unit("z2T_d", u)
                if k >= 2:
                    tile.wait("gelu_done", UP * (k - 1))
                elif tile.number() == ITERS - 1:
                    pe.wait_ge(s["fin_done"], tile.b + k * GS - GS)
                else:
                    pe.wait_ge(s["raw_ev"], tile.b + 2 * PER + k * GS - GS)
                o = spare(m)[:, 0:UR[u]]
                t.matmul(o, w1[:, 0, m * 128:(m + 1) * 128], z2T[u][:, 0, 0:UR[u]], start=True, stop=False)
                t.matmul(o, w1[0:DH2, 1, m * 128:(m + 1) * 128], z2T[u][0:DH2, 1, 0:UR[u]], start=False, stop=True)\
                    .then_inc(s["up_mm"], UP)

            def down(tile, k):
                u, g = divmod(k, GROUPS)
                n = real(u, g)
                if k == 0:
                    tile.wait("gelu_done", PER)
                if k < 2 and tile.number() not in (ITERS - 2, ITERS - 1):
                    pe.wait_ge(s["ev_d" if k else "ev_a"], tile.b + 3 * PER)
                if k >= 2:
                    tile.wait("fin_done", GS * (k - 1))
                for m in range(FC):
                    last = t.matmul(spare(k)[0:n, 0:D], gelu_t[u][:, m, g * GT:g * GT + n], w2[:, m, :],
                                    start=(m == 0), stop=(m == FC - 1))
                last.then_inc(s["dn_mm"], GS)

            turns(pe, dict(
                attn=attn, qk=qk, shift=shift, window=window, rows=rows, factors=factors, bias=bias, ready=ready,
                turn=turn, patch=patch, up=up, down=down,
                flip1=flip1, uv=uv, score=score, attend=attend, flip2=flip2, project=project, rank=rank, pool=pool_,
                pick=pick_, query=query, logits=logits, flip3=flip3, context=context, out=out_, scatter=scatter,
                flip4=flip4))



_INS = ['x', 'cls_tok', 'L0_tok_ln_gamma', 'L0_tok_ln_beta', 'L0_tok_W', 'L0_tok_b', 'L0_attn_W', 'L0_ffn_g1', 'L0_ffn_b1',
        'L0_ffn_g2', 'L0_ffn_b2', 'L0_ffn_Wr', 'L0_ffn_br', 'L0_ffn_Wq', 'L0_ffn_bq', 'L0_ffn_Wk', 'L0_ffn_bk', 'L0_ffn_Wv',
        'L0_ffn_bv', 'L0_ffn_Wo', 'L0_ffn_bo', 'L0_ffn_Wm', 'L0_ffn_bm', 'L0_ffn_W1', 'L0_ffn_bf1', 'L0_ffn_W2', 'L0_ffn_bf2']


def kernel(**inputs):
    import numpy as _np
    import concourse.bacc as _bacc
    from concourse import mybir as _mybir
    from concourse.bass_utils import run_bass_kernel_spmd as _run

    nc = _bacc.Bacc("TRN2", target_bir_lowering=False, num_devices=1)
    arrays, args = {}, {}
    for name in _INS:
        a = _np.ascontiguousarray(inputs[name])
        if a.ndim == 0:
            a = a.reshape(1)
        arrays[f"in_{name}_dram"] = a
        args[name] = nc.dram_tensor(f"in_{name}_dram", a.shape, _mybir.dt.from_np(a.dtype), kind="ExternalInput").ap()
    out = nc.dram_tensor("out_0_dram", (B, POS, D), _mybir.dt.float32, kind="ExternalOutput").ap()
    vit_tower(nc, args, out)
    r = _run(nc, [arrays], core_ids=[0])
    return r.results[0]["out_0_dram"]
```
